# Optimizing a Trainium2 kernel written in Bass

```python
import numpy as np
import jax
import jax.numpy as jnp

def _softmax(x, axis=-1):
    return jax.nn.softmax(x, axis=axis)

def _gelu(x):
    return jax.nn.gelu(x, approximate=True)

def _silu(x):
    return jax.nn.silu(x)

def _sigmoid(x):
    return jax.nn.sigmoid(x)

def _layernorm(x, axis=-1, eps=1e-05):
    m = jnp.mean(x, axis=axis, keepdims=True)
    v = jnp.var(x, axis=axis, keepdims=True)
    return (x - m) / jnp.sqrt(v + eps)

def _scatter_add(tgt, idx, src, axis=0):
    return tgt.at[idx].add(src)

def _segment_sum(src, seg, n):
    return jax.ops.segment_sum(src, seg, n)
kernel_name = 'mk_flamingo_gated_d2_seqx_r4_99f862'

def setup_inputs(seed: int=0):
    np.random.seed(seed)
    _w = jnp.asarray

    def _rec_inputs():
        import jax
        import jax.numpy as jnp
        _rk = jax.random.key(seed)
        x = -0.0002928 + 1 * jax.random.normal(jax.random.fold_in(_rk, 1), (4, 512, 512), jnp.float32)
        _lenS = 512 - jax.random.randint(jax.random.fold_in(_rk, 7), (4,), 0, max(1, 512 // 4) + 1, jnp.int32)
        _lenS2 = 512 - jax.random.randint(jax.random.fold_in(_rk, 8), (4,), 0, max(1, 512 // 4) + 1, jnp.int32)
        _ctx_2048P = jax.random.normal(jax.random.fold_in(_rk, 11), (4, 16, 512), jnp.float32)
        _ctx_2048c = jax.random.dirichlet(jax.random.fold_in(_rk, 511), 0.3 * jnp.ones((16,), jnp.float32), (4, 512))
        _ctx_2048t = jnp.einsum('bsk,bkd->bsd', _ctx_2048c, _ctx_2048P)
        _ctx_2048t = _ctx_2048t * jax.lax.rsqrt(jnp.mean(jnp.square(_ctx_2048t)) + 1e-12) * 0.953939
        ctx_2048 = -1.39393e-06 + 0.999914 * (_ctx_2048t + 0.3 * jax.random.normal(jax.random.fold_in(_rk, 611), (4, 512, 512), jnp.float32))
        _g = jax.random.normal(jax.random.fold_in(_rk, 9001), (2, 2), jnp.float32)
        _g = jnp.sign(_g) * jnp.maximum(jnp.abs(_g), 1.0) + (_g == 0) * 1.0
        g_xattn = _g[0]
        g_ffn = _g[1]
        return (x, ctx_2048, g_xattn, g_ffn)
    x, ctx_2048, g_xattn, g_ffn = _rec_inputs()

    def _L0_xattn_setup():
        import jax, jax.numpy as jnp
        import numpy as np
        import math
        N_HEADS = 8
        key = jax.random.key(seed)
        k1, k2, k3 = jax.random.split(key, 3)
        N, W, T, S = (4, 128, 512, 512)
        q = jax.random.normal(k1, (N, W, T), dtype=jnp.float32)
        k = jax.random.normal(k2, (N, W, S), dtype=jnp.float32)
        v = jax.random.normal(k3, (N, W, S), dtype=jnp.float32)
        return {'q': q, 'k': k, 'v': v}
    _L0_xattn_all = _L0_xattn_setup()
    _L0_xattn_in = {k: v for k, v in _L0_xattn_all.items() if k in ()}
    del _L0_xattn_all

    def _L0_ffn_setup():
        import jax, jax.numpy as jnp
        import numpy as np
        B, S, D = (4, 512, 512)
        E, K, M = (8, 2, 256)
        key = jax.random.key(seed)
        k0, k1, k2, k3, k4 = jax.random.split(key, 5)
        d_scale = D ** (-0.5)
        m_scale = M ** (-0.5)
        return {'x': jax.random.normal(k0, (B, S, D), jnp.float32), 'w_gate': jax.random.normal(k1, (D, E), jnp.float32) * d_scale, 'wi_0': jax.random.normal(k2, (E, D, M), jnp.float32) * d_scale, 'wi_1': jax.random.normal(k3, (E, D, M), jnp.float32) * d_scale, 'wo': jax.random.normal(k4, (E, M, D), jnp.float32) * m_scale}
    _L0_ffn_all = _L0_ffn_setup()
    _L0_ffn_in = {k: v for k, v in _L0_ffn_all.items() if k in ('w_gate', 'wi_0', 'wi_1', 'wo')}
    del _L0_ffn_all

    def _L1_xattn_setup():
        import jax, jax.numpy as jnp
        import numpy as np
        from jax import lax
        LN_EPS = 1e-05
        key = jax.random.key(seed)
        ks = jax.random.split(key, 8)
        B, S, T, D = (4, 128, 512, 512)
        scale = 0.02
        return {'Z': jax.random.normal(ks[0], (B, S, D), dtype=jnp.float32), 'kv': jax.random.normal(ks[1], (B, T, D), dtype=jnp.float32), 'decay': jnp.float32(0.9), 'W_in': jax.random.normal(ks[2], (D, D), dtype=jnp.float32) * scale, 'b_in': jnp.zeros((D,), dtype=jnp.float32), 'W_out': jax.random.normal(ks[3], (D, D), dtype=jnp.float32) * scale, 'b_out': jnp.zeros((D,), dtype=jnp.float32), 'gamma': jnp.ones((D,), dtype=jnp.float32), 'beta': jnp.zeros((D,), dtype=jnp.float32)}
    _L1_xattn_all = _L1_xattn_setup()
    _L1_xattn_in = {k: v for k, v in _L1_xattn_all.items() if k in ('decay', 'W_in', 'b_in', 'W_out', 'b_out', 'gamma', 'beta')}
    del _L1_xattn_all

    def _L1_ffn_setup():
        import jax, jax.numpy as jnp
        import numpy as np
        B, T, D = (2, 256, 512)
        E, K, H = (64, 4, 128)
        S, HS = (2, H * K)
        CAP = 128
        key = jax.random.key(seed)
        ks = jax.random.split(key, 9)
        scale = 0.02
        return {'x': jax.random.normal(ks[0], (B, T, D), jnp.float32), 'Wr': jax.random.normal(ks[1], (D, E), jnp.float32) * scale, 'router_bias': jnp.zeros((E,), jnp.float32), 'Wg': jax.random.normal(ks[2], (E, D, H), jnp.float32) * scale, 'Wu': jax.random.normal(ks[3], (E, D, H), jnp.float32) * scale, 'Wd': jax.random.normal(ks[4], (E, H, D), jnp.float32) * scale, 'Sg': jax.random.normal(ks[5], (S, D, HS), jnp.float32) * scale, 'Su': jax.random.normal(ks[6], (S, D, HS), jnp.float32) * scale, 'Sd': jax.random.normal(ks[7], (S, HS, D), jnp.float32) * scale}
    _L1_ffn_all = _L1_ffn_setup()
    _L1_ffn_in = {k: v for k, v in _L1_ffn_all.items() if k in ('Wr', 'router_bias', 'Wg', 'Wu', 'Wd', 'Sg', 'Su', 'Sd')}
    del _L1_ffn_all
    return {'x': x, 'ctx_2048': ctx_2048, 'g_xattn': g_xattn, 'g_ffn': g_ffn, 'L0_ffn_w_gate': _L0_ffn_in['w_gate'], 'L0_ffn_wi_0': _L0_ffn_in['wi_0'], 'L0_ffn_wi_1': _L0_ffn_in['wi_1'], 'L0_ffn_wo': _L0_ffn_in['wo'], 'L1_xattn_decay': _L1_xattn_in['decay'], 'L1_xattn_W_in': _L1_xattn_in['W_in'], 'L1_xattn_b_in': _L1_xattn_in['b_in'], 'L1_xattn_W_out': _L1_xattn_in['W_out'], 'L1_xattn_b_out': _L1_xattn_in['b_out'], 'L1_xattn_gamma': _L1_xattn_in['gamma'], 'L1_xattn_beta': _L1_xattn_in['beta'], 'L1_ffn_Wr': _L1_ffn_in['Wr'], 'L1_ffn_router_bias': _L1_ffn_in['router_bias'], 'L1_ffn_Wg': _L1_ffn_in['Wg'], 'L1_ffn_Wu': _L1_ffn_in['Wu'], 'L1_ffn_Wd': _L1_ffn_in['Wd'], 'L1_ffn_Sg': _L1_ffn_in['Sg'], 'L1_ffn_Su': _L1_ffn_in['Su'], 'L1_ffn_Sd': _L1_ffn_in['Sd']}

def reference(x, ctx_2048, g_xattn, g_ffn, L0_ffn_w_gate, L0_ffn_wi_0, L0_ffn_wi_1, L0_ffn_wo, L1_xattn_decay, L1_xattn_W_in, L1_xattn_b_in, L1_xattn_W_out, L1_xattn_b_out, L1_xattn_gamma, L1_xattn_beta, L1_ffn_Wr, L1_ffn_router_bias, L1_ffn_Wg, L1_ffn_Wu, L1_ffn_Wd, L1_ffn_Sg, L1_ffn_Su, L1_ffn_Sd):
    import jax
    import jax.numpy as jnp

    def _L0_xattn_ref(q, k, v):
        import jax, jax.numpy as jnp
        import numpy as np
        import math
        N_HEADS = 8
        bs, width, T = q.shape
        S = k.shape[-1]
        ch = width // N_HEADS
        qh = q.reshape(bs * N_HEADS, ch, T)
        kh = k.reshape(bs * N_HEADS, ch, S)
        vh = v.reshape(bs * N_HEADS, ch, S)
        scale = 1.0 / math.sqrt(ch)
        attn = jnp.einsum('bct,bcs->bts', qh * scale, kh * scale)
        attn = jax.nn.softmax(attn, axis=-1)
        out = jnp.einsum('bts,bcs->bct', attn, vh)
        return out.reshape(bs, width, T)

    def _L0_ffn_ref(x, w_gate, wi_0, wi_1, wo):
        import jax, jax.numpy as jnp
        import numpy as np
        B, S, D = (4, 512, 512)
        E, K, M = (8, 2, 256)
        b, s, d = x.shape
        e = w_gate.shape[1]
        xf = x.reshape(-1, d)
        logits = jnp.dot(xf, w_gate)
        top_logits, top_idx = jax.lax.top_k(logits, K)
        weights = jax.nn.softmax(top_logits, axis=-1)
        flat_idx = top_idx.reshape(-1)
        sort_order = jnp.argsort(flat_idx)
        token_ids = sort_order // K
        sorted_x = jnp.take(xf, token_ids, axis=0)
        group_sizes = jnp.bincount(flat_idx, length=E).astype(jnp.int32)
        h0 = jax.lax.ragged_dot(sorted_x, wi_0, group_sizes)
        h1 = jax.lax.ragged_dot(sorted_x, wi_1, group_sizes)
        inter = jax.nn.silu(h0) * h1
        out_sorted = jax.lax.ragged_dot(inter, wo, group_sizes)
        unsort = jnp.argsort(sort_order)
        out = jnp.take(out_sorted, unsort, axis=0).reshape(-1, K, d)
        out = jnp.einsum('tkd,tk->td', out, weights)
        return out.reshape(b, s, d)

    def _L1_xattn_ref(Z, kv, decay, W_in, b_in, W_out, b_out, gamma, beta):
        import jax, jax.numpy as jnp
        import numpy as np
        from jax import lax
        LN_EPS = 1e-05
        B, T, D = kv.shape
        K = jax.nn.sigmoid(decay)
        x = jnp.einsum('btd,ed->bte', kv, W_in) + b_in

        def scan_fn(s, xt):
            s = K * s + xt
            return (s, s)
        s0 = jnp.zeros((B, D), dtype=kv.dtype)
        _, states = lax.scan(scan_fn, s0, jnp.swapaxes(x, 0, 1))
        states = jnp.swapaxes(states, 0, 1)
        proj = jnp.einsum('btd,ed->bte', states, W_out) + b_out
        summary = jnp.mean(proj, axis=1, keepdims=True)
        y = Z + summary
        mu = jnp.mean(y, axis=-1, keepdims=True)
        var = jnp.mean((y - mu) ** 2, axis=-1, keepdims=True)
        return (y - mu) / jnp.sqrt(var + LN_EPS) * gamma + beta

    def _L1_ffn_ref(x, Wr, router_bias, Wg, Wu, Wd, Sg, Su, Sd):
        import jax, jax.numpy as jnp
        import numpy as np
        B, T, D = (2, 256, 512)
        E, K, H = (64, 4, 128)
        S, HS = (2, H * K)
        CAP = 128
        Bx, Tx, Dx = x.shape
        N = Bx * Tx
        flat = x.reshape(N, Dx)
        logits = flat @ Wr + router_bias
        scores = jax.nn.softmax(logits, axis=-1)
        topk_scores, topk_idx = jax.lax.top_k(scores, K)
        topk_scores = topk_scores / topk_scores.sum(-1, keepdims=True)
        eid = topk_idx.reshape(-1)
        w = topk_scores.reshape(-1)
        tok = jnp.repeat(jnp.arange(N), K)
        oh = jax.nn.one_hot(eid, E, dtype=jnp.int32)
        pos = (jnp.cumsum(oh, axis=0) * oh).sum(-1) - 1
        valid = pos < CAP
        xb = jnp.zeros((E, CAP, Dx), x.dtype).at[eid, pos].set(flat[tok], mode='drop')
        h = jax.nn.silu(jnp.einsum('ecd,edh->ech', xb, Wg)) * jnp.einsum('ecd,edh->ech', xb, Wu)
        yb = jnp.einsum('ech,ehd->ecd', h, Wd)
        y = yb[eid, jnp.minimum(pos, CAP - 1)] * (w * valid)[:, None]
        out = jnp.zeros((N, Dx), x.dtype).at[tok].add(y)
        hs = jax.nn.silu(jnp.einsum('nd,sdh->nsh', flat, Sg)) * jnp.einsum('nd,sdh->nsh', flat, Su)
        out = out + jnp.einsum('nsh,shd->nd', hs, Sd)
        return out.reshape(Bx, Tx, Dx)
    x = x + jnp.tanh(g_xattn[0]) * _L0_xattn_ref(_layernorm(x, axis=-1), ctx_2048, ctx_2048)
    x = x + jnp.tanh(g_ffn[0]) * _L0_ffn_ref(_layernorm(x, axis=-1), L0_ffn_w_gate, L0_ffn_wi_0, L0_ffn_wi_1, L0_ffn_wo)
    x = x + jnp.tanh(g_xattn[1]) * _L1_xattn_ref(_layernorm(x, axis=-1), ctx_2048, L1_xattn_decay, L1_xattn_W_in, L1_xattn_b_in, L1_xattn_W_out, L1_xattn_b_out, L1_xattn_gamma, L1_xattn_beta)
    x = x + jnp.tanh(g_ffn[1]) * _L1_ffn_ref(_layernorm(x, axis=-1), L1_ffn_Wr, L1_ffn_router_bias, L1_ffn_Wg, L1_ffn_Wu, L1_ffn_Wd, L1_ffn_Sg, L1_ffn_Su, L1_ffn_Sd)
    return x

_drawn_inputs = setup_inputs


def setup_inputs(seed=0):
    import zlib

    import numpy as np

    out = dict(_drawn_inputs(seed))
    spreads = {'g_ffn': (-1.0, 0.6),
     'L1_xattn_b_in': (0.0, 0.1),
     'L1_xattn_b_out': (0.0, 0.1),
     'L1_xattn_gamma': (1.0, 0.2),
     'L1_xattn_beta': (0.0, 0.1),
     'L1_ffn_router_bias': (0.0, 0.714)}
    factors = {'L1_ffn_Wr': 3.794, 'L1_ffn_Wg': 3.732, 'L1_ffn_Wu': 3.674, 'L1_ffn_Wd': 3.62}
    for name, (base, spread) in spreads.items():
        noise = np.random.default_rng([zlib.crc32(name.encode()), seed]).standard_normal(out[name].shape)
        drawn = base * np.exp(spread * noise) if base else spread * noise
        out[name] = jnp.asarray(drawn.astype(out[name].dtype))
    for name, factor in factors.items():
        out[name] = (out[name] * factor).astype(out[name].dtype)
    return out
```

```python
from contextlib import ExitStack

import concourse.bass as bass
from concourse import mybir

F32 = mybir.dt.float32
BF16 = mybir.dt.bfloat16
I32 = mybir.dt.int32
U32 = mybir.dt.uint32
ALU = mybir.AluOpType
ACT = mybir.ActivationFunctionType
AX = mybir.AxisListType

P = 128
B, SEQ, D = 4, 512, 512
TILES = B * SEQ // P
TPB = SEQ // P
DB = D // P
HEAD = 64
E0, M0 = 8, 256
E1, H1, TOP1, CAP1 = 64, 128, 4, 128
NSH, HSH = 2, 512
LN_EPS = 1e-5
E0_STRIDE = B * SEQ + P
L0_TILES = 40
DUMMY_ROW = E0 * E0_STRIDE
TAB0_ROWS = DUMMY_ROW + E0 * P
RSQRT_MAGIC = float(0x5F3759DF)


def seen(k):
    return min(k + 1, TILES) if isinstance(k, int) else k + 1


def need(eng, sem, value, alone=0):
    if not isinstance(value, int):
        if alone:
            eng.wait_ge(sem, alone)
        eng.wait_ge(sem, value)
    elif value > 0:
        eng.wait_ge(sem, value)


def row(t, k):
    if isinstance(k, int):
        return t[:, k, :]
    return t[:, bass.ds(k, 1), :].rearrange("p o d -> p (o d)")


def valid(*tiles, n=TILES):
    return all(not isinstance(k, int) or 0 <= k < n for k in tiles)


def steps(eng, step, n, ring, lead, tail):
    first, last = max(-(-lead // ring), -(-4 // ring)), (n - lead) // ring
    for i in range(-lead, first * ring):
        step(i, i // ring, i % ring)
    with eng.Fori(first, last) as u:
        for c in range(ring):
            step(u * ring + c, u, c)
    for i in range(last * ring, n + tail):
        step(i, i // ring, i % ring)


def rsqrt(nc, dve, y, v, half, scratch):
    ve, t = scratch
    nc.vector.tensor_scalar(ve, v, LN_EPS, None, ALU.add)
    dve.drain()
    nc.vector.tensor_scalar(half.bitcast(I32), ve.bitcast(I32), 1, None, ALU.logical_shift_right)
    dve.drain()
    nc.vector.tensor_scalar(y.bitcast(I32), half.bitcast(I32), -1.0, RSQRT_MAGIC, ALU.mult, ALU.add)
    dve.drain()
    for _ in range(3):
        nc.vector.tensor_tensor(t, y, y, ALU.mult)
        dve.drain()
        nc.vector.scalar_tensor_tensor(t, t, -0.5, ve, ALU.mult, ALU.mult)
        dve.drain()
        nc.vector.scalar_tensor_tensor(y, t, 1.5, y, ALU.add, ALU.mult)
        dve.drain()


def build(nc, A, out):
    ctx = ExitStack()
    with ctx:
        def sb(name, shape, dt=F32, c=ctx, side=None):
            return c.enter_context(nc.sbuf_tensor(name, shape, dt, side=side))

        bank = [ctx.enter_context(nc.psum_tensor(f"bank{n}", [P, 512], F32)) for n in range(8)]

        x_sb = sb("x_sb", [P, TILES, D])
        ident = sb("ident", [P, P])
        identb = sb("identb", [P, P], BF16)
        onesb = sb("onesb", [P, P], BF16)
        before = sb("before", [P, P], BF16)
        iota_e = sb("iota_e", [P, E1])
        base0 = sb("base0", [P, E0])
        base1 = sb("base1", [P, E1])
        rowid = sb("rowid", [P, 1])
        gates = sb("gates", [P, 4])
        top0 = sb("top0", [P, TILES, 2])
        slot0 = sb("slot0", [P, TILES, 2], I32)
        take0 = sb("take0", [P, TILES, 2], I32)
        summary = sb("summary", [P, B, D])
        tinfo = sb("tinfo", [1, L0_TILES, 2], I32)

        tab0 = nc.dram_tensor("tab0", (TAB0_ROWS, D), F32, kind="Internal").ap()
        ytab0 = nc.dram_tensor("ytab0", (L0_TILES * P, D), F32, kind="Internal").ap()
        tab1 = nc.dram_tensor("tab1", (E1 * CAP1, D), F32, kind="Internal").ap()
        ytab1 = nc.dram_tensor("ytab1", (E1 * CAP1, D), F32, kind="Internal").ap()

        arena0 = ExitStack()
        later = ExitStack()
        with arena0:
            w01 = sb("w01", [P, E0 * DB, 2 * M0], F32, arena0, "right")
            wo0 = sb("wo0", [P, E0 * (M0 // P), D], F32, arena0, "right")
            s_w0 = arena0.enter_context(nc.semaphore("weights0_loaded"))
            s_zero1 = ctx.enter_context(nc.semaphore("table1_zeroed"))
            T = dict(locals())
            held = ExitStack()
            with held:
                T["ctx_sb"] = sb("ctx_sb", [P, TILES, D], F32, held)
                T["zeros"] = sb("zeros", [P, D], F32, held)
                T["chosen"] = sb("chosen", [P, 2, E0], BF16, held)
                attention(nc, A, T)
                summary_and_tiles(nc, A, T)
            later.__enter__()
            T["ws"] = [sb(n, [P, NSH, DB, HSH], F32, later) for n in ("w_sg", "w_su", "w_sd")]
            T["s_ws"] = later.enter_context(nc.semaphore("shared_weights_loaded"))
            mixture0(nc, A, T)
        with later:
            T["flatT"] = sb("flatT", [P, B, DB, SEQ], F32, later)
            T["top1"] = sb("top1", [P, TILES, TOP1], F32, later)
            T["take1"] = sb("take1", [P, TILES, TOP1], I32, later)
            T["wt1"] = sb("wt1", [P, TILES, TOP1], F32, later)
            T["kept1"] = sb("kept1", [P, TILES, TOP1], F32, later)
            middle(nc, A, T)
            experts(nc, A, T)
            finish(nc, A, T, out)


def attention(nc, A, T):
    c = ExitStack()
    with c:
        def sb(name, shape, dt=F32):
            return c.enter_context(nc.sbuf_tensor(name, shape, dt))

        def sem(name):
            return c.enter_context(nc.semaphore(name))

        x_sb, bank = T["x_sb"], T["bank"]
        ident, identb, onesb, before = T["ident"], T["identb"], T["onesb"], T["before"]
        gates, iota_e, base0, rowid = T["gates"], T["iota_e"], T["base0"], T["rowid"]
        w01, wo0, s_w0, s_zero1 = T["w01"], T["wo0"], T["s_w0"], T["s_zero1"]

        ctx_sb, zeros, chosen = T["ctx_sb"], T["zeros"], T["chosen"]
        k_sb = sb("k_sb", [P, 2, D])
        q_sb = sb("q_sb", [P, 2, D])
        kb = sb("kb", [P, 2, D], BF16)
        qb = sb("qb", [P, 2, D], BF16)
        vT = sb("vT", [P, 2, 4, 3, HEAD])
        negmax = sb("negmax", [P, 2, 8], BF16)
        probs = sb("probs", [P, 2, 2, D])
        attn = sb("attn", [P, D])
        xn = sb("xn", [P, 2, D])
        xnT = sb("xnT", [P, DB, P])
        bn = sb("bn", [P, 2, 6])
        mv = sb("mv", [P, 2, 2])
        rstd = sb("rstd", [P, 2])
        half, ve, nt = sb("half", [P, 2]), sb("ve", [P, 2]), sb("nt", [P, 2])
        ln1 = sb("ln1", [P, 2, 2])
        ln2 = sb("ln2", [P, 2, 2])
        logits = sb("logits", [P, E0])
        m8 = sb("m8", [P, 8])
        i8 = sb("i8", [P, 8], U32)
        idxf = sb("idxf", [P, 2])
        onehot = sb("onehot", [P, 2, E0])
        mask = sb("mask", [P, 2, E0], BF16)
        rows = sb("rows", [P, E0])
        junk = sb("junk", [P, 2, E0])
        slotf = sb("slotf", [P, 2])
        wg = sb("wg", [P, DB, E0])
        graw = sb("graw", [P, 4])

        s_xA, s_xB, s_cA, s_cB, s_small = (sem(n) for n in (
            "xA_loaded", "xB_loaded", "ctxA_loaded", "ctxB_loaded", "small_loaded"))
        consts_ready, zeros_ready, gates_ready = sem("consts_ready"), sem("zeros_ready"), sem("gates_ready")
        pm_full, pm_read = sem("pm_full"), sem("pm_read")
        k_ready, qkb_ready, q_ready = sem("k_ready"), sem("qkb_ready"), sem("q_ready")
        ln1_ready, ln2_ready, xn_ready = sem("ln1_ready"), sem("ln2_ready"), sem("xn_ready")
        vT_full, vT_ready = sem("vT_full"), sem("vT_ready")
        s_full, p_ready, p_used, qk_done = sem("s_full"), sem("p_ready"), sem("p_used"), sem("qk_done")
        sums_ready, po_read, x1_ready = sem("sums_ready"), sem("po_read"), sem("x1_ready")
        xnT_full, xnT_ready = sem("xnT_full"), sem("xnT_ready")
        lg_full, mask_ready, pos_full, pos_read = sem("lg_full"), sem("mask_ready"), sem("pos_full"), sem("pos_read")
        slot_ready = sem("slot_ready")
        scattered = [sem("scattered_even"), sem("scattered_odd")]
        dummy_zeroed = sem("dummy_zeroed")

        pS, pO, pM, pT = bank[0:2], bank[2:6], bank[6], bank[7]
        x_v = A["x"].rearrange("b (t p) d -> p (b t) d", p=P)
        c_v = A["ctx_2048"].rearrange("b (t p) d -> p (b t) d", p=P)
        NA = 3
        SMALL = 16 * 3

        block = c.enter_context(nc.Block())

        @block.sync
        def _(sp):
            sp.dma_start(x_sb[:, 0:NA, :], x_v[:, 0:NA, :]).then_inc(s_xA, 16)
            sp.dma_start(ctx_sb[:, 0:NA, :], c_v[:, 0:NA, :]).then_inc(s_cA, 16)
            sp.dma_start(graw[:, 0:2], A["g_xattn"].partition_broadcast(P)).then_inc(s_small, 16)
            sp.dma_start(graw[:, 2:4], A["g_ffn"].partition_broadcast(P)).then_inc(s_small, 16)
            sp.dma_start(wg[:], A["L0_ffn_w_gate"].rearrange("(b p) e -> p b e", p=P)).then_inc(s_small, 16)
            sp.dma_start(x_sb[:, NA:, :], x_v[:, NA:, :]).then_inc(s_xB, 16)
            sp.dma_start(ctx_sb[:, NA:, :], c_v[:, NA:, :]).then_inc(s_cB, 16)
            w01_v = w01[:].rearrange("p (e b) m -> p e b m", e=E0)
            for name, at in (("L0_ffn_wi_0", 0), ("L0_ffn_wi_1", M0)):
                for e in range(E0):
                    sp.dma_start(w01_v[:, e, :, at:at + M0],
                                 A[name][e].rearrange("(b p) m -> p b m", p=P)).then_inc(s_w0, 16)
            sp.dma_start(wo0[:].rearrange("p (e b) d -> p e b d", e=E0),
                         A["L0_ffn_wo"].rearrange("e (b p) d -> p e b d", p=P)).then_inc(s_w0, 16)
            sp.wait_ge(zeros_ready, 1)
            reps = 8
            t1 = T["tab1"].rearrange("(n r p) d -> n p r d", p=P, r=reps)
            for n in range(E1 * CAP1 // (reps * P)):
                sp.dma_start(t1[n], zeros[:].unsqueeze(1).broadcast_to([P, reps, D])).then_inc(s_zero1, 16)
            sp.dma_start(T["tab0"][DUMMY_ROW:, :].rearrange("(r p) d -> p r d", p=P),
                         zeros[:].unsqueeze(1).broadcast_to([P, E0, D])).then_inc(dummy_zeroed, 16)
            sp.wait_ge(dummy_zeroed, 16)

        @block.gpsimd
        def _(pool):
            nc.gpsimd.memset(ident[:], 0.0)
            nc.gpsimd.memset(onesb[:], 1.0)
            nc.gpsimd.memset(zeros[:], 0.0)
            nc.gpsimd.memset(vT[:, :, :, 1, :], 1.0)
            nc.gpsimd.memset(chosen[:], 0.0)
            nc.gpsimd.iota(iota_e[:], [[1, E1]], base=0, channel_multiplier=0, allow_small_or_imprecise_dtypes=True)
            nc.gpsimd.iota(base0[:], [[E0_STRIDE, E0]], base=0, channel_multiplier=0,
                           allow_small_or_imprecise_dtypes=True)
            nc.gpsimd.iota(T["base1"][:], [[CAP1, E1]], base=0, channel_multiplier=0,
                           allow_small_or_imprecise_dtypes=True)
            nc.gpsimd.iota(rowid[:], [[0, 1]], base=0, channel_multiplier=1, allow_small_or_imprecise_dtypes=True)
            pool.drain()
            nc.gpsimd.affine_select(ident[:], ident[:], [[-1, P]], ALU.not_equal, 1.0, base=0, channel_multiplier=1)
            nc.gpsimd.affine_select(before[:], onesb[:], [[1, P]], ALU.is_ge, 0.0, base=-1, channel_multiplier=-1)
            pool.drain()
            nc.gpsimd.tensor_copy(identb[:], ident[:])
            pool.drain()
            nc.gpsimd.engine_nop().then_inc(consts_ready, 1)
            nc.gpsimd.engine_nop().then_inc(zeros_ready, 1)
            for i in range(-2, TILES + 2):
                if valid(i + 1):
                    pool.wait_ge(s_cA if i + 1 < NA else s_cB, 16)
                    need(pool, qk_done, i)
                    nc.gpsimd.tensor_copy(k_sb[:, (i + 1) % 2, :], ctx_sb[:, i + 1, :]).then_inc(k_ready, 1)
                if valid(i - 1):
                    pool.wait_ge(po_read, i)
                    nc.gpsimd.tensor_tensor(x_sb[:, i - 1, :], x_sb[:, i - 1, :], attn[:],
                                            ALU.add).then_inc(x1_ready, 1)
                if valid(i + 2):
                    s = i % 2
                    need(pool, pm_full, 8 * (i + 1))
                    pool.wait_ge(s_cA if i + 2 < NA else s_cB, 16)
                    nc.gpsimd.tensor_copy(kb[:, s, :], ctx_sb[:, i + 2, :])
                    pool.wait_ge(ln1_ready, i + 3)
                    nc.gpsimd.tensor_scalar(qb[:, s, :], x_sb[:, i + 2, :], ln1[:, s, 0:1], ln1[:, s, 1:2],
                                            ALU.mult, ALU.add).then_inc(qkb_ready, 1)
                if valid(i - 2):
                    pool.wait_ge(slot_ready, i - 1)
                    for k in range(2):
                        nc.gpsimd.indirect_dma_start(
                            T["tab0"], bass.IndirectOffsetOnAxis(T["slot0"][:, i - 2, k:k + 1], 0),
                            xn[:, i % 2, :], None).then_inc(scattered[i % 2], 16)
            for s in range(2):
                pool.wait_ge(scattered[s], 16 * TILES)

        @block.tensor
        def _(pe):
            pe.wait_ge(consts_ready, 1)
            pe.wait_ge(s_small, SMALL)

            def scores(i, s, sb_):
                for h in range(2):
                    need(pe, p_ready, i * 8 + (sb_ * 2 + h - 1))
                    kh = slice(HEAD * h, HEAD * h + HEAD)
                    last = nc.tensor.matmul(pS[h][:], k_sb[kh, s, sb_ * P:sb_ * P + P], q_sb[kh, s, :],
                                            start=True, stop=False)
                if sb_ == 3:
                    last.then_inc(qk_done, 1)
                for h in range(2):
                    for t in range(4):
                        m = h * 4 + t
                        last = nc.tensor.matmul(pS[h][:, t * P:t * P + P],
                                                negmax[:, s, m:m + 1].broadcast_to([P, P]), identb[:],
                                                start=False, stop=(t == 3))
                    last.then_inc(s_full, 1)

            def values(k, s, sb_):
                for h in range(2):
                    need(pe, p_ready, k * 8 + (sb_ * 2 + h + 1))
                    nc.tensor.matmul(pO[s * 2 + h][:], vT[:, s, sb_, h:h + 2, :].rearrange("p a c -> p (a c)"),
                                     probs[:, sb_ % 2, h, :], start=(sb_ == 0), stop=(sb_ == 3)).then_inc(p_used, 1)

            def rough(k, s, m):
                h, t = m // 4, m % 4
                need(pe, pm_read, k * 8 + m)
                hp = slice(HEAD * h, HEAD * h + HEAD)
                nc.tensor.matmul(pM[:], qb[hp, s, t * P:t * P + P], kb[hp, s, :],
                                 start=True, stop=True).then_inc(pm_full, 1)

            def step(i, u, odd):
                s, o = odd, 1 - odd
                if valid(i):
                    need(pe, q_ready, i + 1)
                    need(pe, k_ready, i + 1)
                    need(pe, pm_read, i * 8 + 8)
                if valid(i + 1):
                    need(pe, qkb_ready, i + 2)
                for b in range(4):
                    if valid(i):
                        scores(i, s, b)
                    if valid(i + 1):
                        rough(i + 1, o, 2 * b)
                    if b == 0 and valid(i - 1):
                        values(i - 1, o, 3)
                    if b > 0 and valid(i):
                        if b == 1:
                            need(pe, po_read, i - 1)
                            need(pe, vT_ready, i + 1)
                        values(i, s, b - 1)
                    if valid(i + 1):
                        rough(i + 1, o, 2 * b + 1)
                    if b == 0 and valid(i + 1):
                        need(pe, k_ready, i + 2)
                        need(pe, xnT_ready, i - 1)
                        for t in range(4):
                            last = nc.tensor.transpose(pT[:, t * P:t * P + P], k_sb[:, o, t * P:t * P + P], ident[:])
                        last.then_inc(vT_full, 1)
                    if b == 1 and valid(i - 2):
                        need(pe, vT_ready, seen(i + 1))
                        need(pe, xnT_ready, i - 1)
                        for d in range(DB):
                            last = nc.tensor.matmul(pT[:, 0:E0], xnT[:, d, :], wg[:, d, :],
                                                    start=(d == 0), stop=(d == DB - 1))
                        last.then_inc(lg_full, 1)
                    if b == 2 and valid(i - 2):
                        need(pe, mask_ready, i - 1)
                        nc.tensor.matmul(pT[:, 0:E0], before[:], mask[:, s, :], start=True, stop=False)
                        nc.tensor.matmul(pT[:, 0:E0], onesb[:], chosen[:, s, :], start=False,
                                         stop=True).then_inc(pos_full, 1)
                    if b == 3 and valid(i - 1):
                        need(pe, pos_read, i - 1)
                        if not valid(i - 2):
                            need(pe, vT_ready, seen(i + 1))
                        need(pe, xn_ready, i)
                        for t in range(DB):
                            last = nc.tensor.transpose(pT[:, t * P:t * P + P], xn[:, o, t * P:t * P + P], ident[:])
                        last.then_inc(xnT_full, 1)

            steps(pe, step, TILES, 2, 2, 2)

        @block.scalar
        def _(act):
            act.wait_ge(s_small, SMALL)
            nc.scalar.activation(gates[:], graw[:], ACT.Tanh).then_inc(gates_ready, 1)

            def step(i, u, odd):
                s, o = odd, 1 - odd
                for b in range(4):
                    if valid(i):
                        for h in range(2):
                            n = b * 2 + h
                            need(act, p_used, i * 8 + (n - 3))
                            need(act, s_full, i * 8 + (n + 1))
                            nc.scalar.activation(probs[:, b % 2, h, :], pS[h][:], ACT.Exp,
                                                 scale=1.0 / HEAD).then_inc(p_ready, 1)
                    if b == 0 and valid(i - 1):
                        need(act, x1_ready, i - 1)
                        need(act, p_used, i * 8)
                        nc.scalar.copy(attn[0:HEAD, :], pO[o * 2][HEAD:P, :])
                        nc.scalar.copy(attn[HEAD:P, :], pO[o * 2 + 1][0:HEAD, :]).then_inc(sums_ready, 1)
                    if b == 1 and valid(i + 1):
                        need(act, p_used, i * 8)
                        need(act, vT_full, i + 2)
                        pv = pT[:].rearrange("p (t a c) -> p t a c", t=4, a=2)
                        nc.scalar.copy(vT[:, o, :, 0, :], pv[:, :, 0, :])
                        nc.scalar.copy(vT[:, o, :, 2, :], pv[:, :, 1, :]).then_inc(vT_ready, 1)
                    if b == 2 and valid(i + 1):
                        need(act, ln1_ready, i + 2, alone=1)
                        need(act, qk_done, i)
                        nc.scalar.activation(q_sb[:, o, :], row(x_sb, i + 1), ACT.Identity,
                                             scale=ln1[:, o, 0:1], bias=ln1[:, o, 1:2]).then_inc(q_ready, 1)
                    if b == 3 and valid(i - 1):
                        half_ = u + (odd - 1) // 2
                        need(act, ln2_ready, i, alone=1)
                        need(act, scattered[o], half_ * 32)
                        nc.scalar.activation(xn[:, o, :], row(x_sb, i - 1), ACT.Identity,
                                             scale=ln2[:, o, 0:1], bias=ln2[:, o, 1:2]).then_inc(xn_ready, 1)
                        need(act, xnT_full, i)
                        nc.scalar.copy(xnT[:].rearrange("p d t -> p (d t)"), pT[:]).then_inc(xnT_ready, 1)

            steps(act, step, TILES, 2, 2, 2)

        @block.vector
        def _(dve):
            dve.wait_ge(consts_ready, 1)
            dve.wait_ge(gates_ready, 1)

            def rough_max(k, s, m):
                need(dve, pm_full, k * 8 + (m + 1))
                if m == 0:
                    need(dve, s_full, k * 8 - 8)
                nc.vector.tensor_reduce(negmax[:, s, m:m + 1], pM[:], AX.X, ALU.max,
                                        negate=True).then_inc(pm_read, 1)

            def choose(k, s):
                need(dve, lg_full, k + 1)
                nc.vector.tensor_copy(logits[:], pT[:, 0:E0])
                dve.drain()
                nc.vector.max(m8[:], logits[:])
                dve.drain()
                nc.vector.max_index(i8[:], m8[:], logits[:])
                nc.vector.tensor_copy(row(T["top0"], k), m8[:, 0:2])
                dve.drain()
                nc.vector.tensor_copy(idxf[:], i8[:, 0:2])
                dve.drain()
                for c_ in range(2):
                    nc.vector.tensor_scalar(onehot[:, c_, :], iota_e[:, 0:E0], idxf[:, c_:c_ + 1], None, ALU.is_equal)
                dve.drain()
                nc.vector.tensor_tensor(mask[:, s, :], onehot[:, 0, :], onehot[:, 1, :],
                                        ALU.add).then_inc(mask_ready, 1)

            def place(k, s):
                need(dve, pos_full, k + 1)
                nc.vector.tensor_tensor(rows[:], pT[:, 0:E0], base0[:], ALU.add).then_inc(pos_read, 1)
                nc.vector.tensor_tensor(chosen[:, 1 - s, :], chosen[:, s, :], mask[:, s, :], ALU.add)
                dve.drain()
                for c_ in range(2):
                    nc.vector.tensor_tensor_reduce(out=junk[:, c_, :], in0=onehot[:, c_, :], in1=rows[:], scale=1.0,
                                                   scalar=0.0, op0=ALU.mult, op1=ALU.add,
                                                   accum_out=slotf[:, c_:c_ + 1])
                dve.drain()
                nc.vector.tensor_copy(row(T["slot0"], k), slotf[:]).then_inc(slot_ready, 1)

            def step(i, u, odd):
                s, o = odd, 1 - odd
                if isinstance(i, int) and i == NA - 2:
                    dve.wait_ge(s_xB, 16)
                for b in range(4):
                    if valid(i + 1):
                        rough_max(i + 1, o, 2 * b)
                        rough_max(i + 1, o, 2 * b + 1)
                    if b == 0 and valid(i - 1):
                        dve.drain()
                        need(dve, sums_ready, i)
                        nc.vector.reciprocal(attn[:], attn[:])
                    if b == 1 and valid(i - 2):
                        choose(i - 2, s)
                    if b == 1 and valid(i - 1):
                        dve.drain()
                        for h in range(2):
                            hp = slice(HEAD * h, HEAD * h + HEAD)
                            last = nc.vector.scalar_tensor_tensor(attn[hp, :], pO[o * 2 + h][hp, :], gates[hp, 0:1],
                                                                  attn[hp, :], ALU.mult, ALU.mult)
                        last.then_inc(po_read, 1)
                    if b == 2 and valid(i - 2):
                        place(i - 2, s)
                    if b == 2 and (valid(i - 1) or valid(i + 2)):
                        cols = [n for n, k in enumerate((i - 1, i + 2)) if valid(k)]
                        a, z = cols[0], cols[-1] + 1
                        dve.drain()
                        if valid(i + 2):
                            if isinstance(i, int):
                                dve.wait_ge(s_xA, 16)
                            nc.vector.bn_stats(bn[:, 1, :], row(x_sb, i + 2))
                        if valid(i - 1):
                            need(dve, x1_ready, i, alone=1)
                            nc.vector.bn_stats(bn[:, 0, :], row(x_sb, i - 1))
                        dve.drain()
                        for n in cols:
                            nc.vector.bn_aggr(mv[:, n, :], bn[:, n, :])
                        dve.drain()
                        rsqrt(nc, dve, rstd[:, a:z], mv[:, a:z, 1], half[:, a:z], (ve[:, a:z], nt[:, a:z]))
                        if valid(i + 2):
                            need(dve, q_ready, i + 1)
                            need(dve, qkb_ready, i + 1)
                            nc.vector.tensor_copy(ln1[:, s, 0:1], rstd[:, 1:2])
                            nc.vector.scalar_tensor_tensor(ln1[:, s, 1:2], mv[:, 1, 0:1], -1.0, rstd[:, 1:2],
                                                           ALU.mult, ALU.mult).then_inc(ln1_ready, 1)
                        if valid(i - 1):
                            need(dve, xn_ready, i - 2)
                            nc.vector.tensor_copy(ln2[:, o, 0:1], rstd[:, 0:1])
                            nc.vector.scalar_tensor_tensor(ln2[:, o, 1:2], mv[:, 0, 0:1], -1.0, rstd[:, 0:1],
                                                           ALU.mult, ALU.mult).then_inc(ln2_ready, 1)

            steps(dve, step, TILES, 2, 2, 2)


def summary_and_tiles(nc, A, T):
    c = ExitStack()
    with c:
        def sb(name, shape, dt=F32):
            return c.enter_context(nc.sbuf_tensor(name, shape, dt))

        def sem(name):
            return c.enter_context(nc.semaphore(name))

        bank, ident, onesb = T["bank"], T["ident"], T["onesb"]
        pS, pO, pM, pT = bank[0:2], bank[2:6], bank[6], bank[7]
        base0, rowid, chosen, ctx_sb, zeros = T["base0"], T["rowid"], T["chosen"], T["ctx_sb"], T["zeros"]
        flip = sb("flip", [P, P])
        ones = sb("ones", [P, P])
        iota_i = sb("iota_i", [1, L0_TILES])
        cnt = sb("cnt", [P, E0])
        padf = sb("padf", [P, E0])
        padrow = sb("padrow", [P, E0], I32)
        ntf = sb("ntf", [P, E0])
        nti = sb("nti", [P, E0], I32)
        cum = sb("cum", [1, E0])
        texp = sb("texp", [1, L0_TILES])
        tskip = sb("tskip", [1, L0_TILES])
        trow = sb("trow", [1, L0_TILES])
        win = sb("win", [P, DB, D])
        wout = sb("wout", [P, DB, D])
        woutT = sb("woutT", [P, DB, D])
        bin_col = sb("bin_col", [P, DB])
        bout_row = sb("bout_row", [P, D])
        decay = sb("decay", [1, 4])
        kdec = sb("kdec", [1, 1])
        crow = sb("crow", [1, SEQ])
        invt = sb("invt", [1, 1])
        ccol = sb("ccol", [P, 2, TPB])
        csum = sb("csum", [P, 1])
        mstate = sb("mstate", [P, DB, B])
        usum = sb("usum", [P, D])
        big = sb("big", [P, D])
        past = big[0:1, 0:L0_TILES * E0].rearrange("p (t e) -> p t e", e=E0)
        slotf = usum[:, 2 * TILES:4 * TILES]

        s_sw = sem("summary_weights_loaded")
        consts_ready = sem("summary_consts_ready")
        cnt_full, pad_ready, padded = sem("cnt_full"), sem("pad_ready"), sem("padded")
        dve_step, pe_step, act_step, decay_ready = sem("dve_step"), sem("pe_step"), sem("act_step"), sem("decay_ready")

        block = c.enter_context(nc.Block())

        @block.sync
        def _(sp):
            sp.dma_start(decay[0:1, 0:1], A["L1_xattn_decay"]).then_inc(decay_ready, 16)
            sp.dma_start(win[:], A["L1_xattn_W_in"].rearrange("(b p) d -> p b d", p=P)).then_inc(s_sw, 16)
            sp.dma_start(wout[:], A["L1_xattn_W_out"].rearrange("(b p) d -> p b d", p=P)).then_inc(s_sw, 16)
            sp.dma_start(bin_col[:], A["L1_xattn_b_in"].rearrange("(b p) -> p b", p=P),
                         allow_slow_non_contiguous=True).then_inc(s_sw, 16)
            sp.dma_start(bout_row[:], A["L1_xattn_b_out"].partition_broadcast(P)).then_inc(s_sw, 16)

        @block.gpsimd
        def _(pool):
            nc.gpsimd.memset(flip[:], 0.0)
            nc.gpsimd.memset(ones[:], 1.0)
            nc.gpsimd.memset(invt[:], 1.0 / SEQ)
            nc.gpsimd.iota(iota_i[:], [[1, L0_TILES]], base=0, channel_multiplier=0,
                           allow_small_or_imprecise_dtypes=True)
            pool.drain()
            nc.gpsimd.affine_select(flip[:], flip[:], [[1, P]], ALU.not_equal, 1.0, base=1 - P, channel_multiplier=1)
            pool.drain()
            nc.gpsimd.engine_nop().then_inc(consts_ready, 1)
            pool.wait_ge(pad_ready, 1)
            for e in range(E0):
                nc.gpsimd.indirect_dma_start(T["tab0"], bass.IndirectOffsetOnAxis(padrow[:, e:e + 1], 0),
                                             zeros[:, 0:D], None).then_inc(padded, 16)
            pool.wait_ge(padded, 16 * E0)

        @block.tensor
        def _(pe):
            nc.tensor.matmul(pT[:, 0:E0], onesb[:], chosen[:, TILES % 2, :], start=True, stop=True).then_inc(cnt_full, 1)

            pe.wait_ge(consts_ready, 1)
            pe.wait_ge(dve_step, 1)
            for j in range(TPB):
                last = nc.tensor.matmul(pS[0][:, j:j + 1], crow[0:1, j * P:j * P + P], ones[0:1, 0:1], start=True, stop=True)
            last.then_inc(pe_step, 1)
            pe.wait_ge(dve_step, 2)
            nc.tensor.matmul(pS[1][:, 0:TPB], flip[:], ccol[:, 0, :], start=True, stop=True).then_inc(pe_step, 1)
            pe.wait_ge(dve_step, 3)
            nc.tensor.matmul(pS[0][:, 0:TPB], ones[:], ccol[:, 1, :], start=True, stop=True)
            for b in range(B):
                for j in range(TPB):
                    last = nc.tensor.matmul(pO[b][:], ccol[:, 1, j:j + 1].broadcast_to([P, P]),
                                            ctx_sb[:, b * TPB + j, :], start=(j == 0), stop=(j == TPB - 1))
            last.then_inc(pe_step, 1)
            pe.wait_ge(s_sw, 64)
            for n in range(DB):
                tb = (pM, pT)[n % 2]
                if n == 0:
                    pe.wait_ge(pad_ready, 1)
                if n >= 2:
                    pe.wait_ge(act_step, n)
                for r in range(DB):
                    last = nc.tensor.transpose(tb[:, r * P:r * P + P], wout[:, r, n * P:n * P + P], ident[:])
                last.then_inc(pe_step, 1)
            pe.wait_ge(act_step, 1 + DB)
            pe.wait_ge(dve_step, 4)
            for b in range(B):
                if b >= 2:
                    pe.wait_ge(dve_step, 4 + b - 1)
                for n in range(DB):
                    last = nc.tensor.matmul(pS[b % 2][:], mstate[:, n, b:b + 1].broadcast_to([P, P]), woutT[:, n, :],
                                            start=(n == 0), stop=(n == DB - 1))
                last.then_inc(pe_step, 1)

        @block.scalar
        def _(act):
            act.wait_ge(decay_ready, 16)
            nc.scalar.activation(decay[0:1, 1:2], decay[0:1, 0:1], ACT.Exp, scale=-1.0).then_inc(act_step, 1)

            for n in range(DB):
                act.wait_ge(pe_step, 4 + n)
                nc.scalar.copy(woutT[:, n, :], (pM, pT)[n % 2][:]).then_inc(act_step, 1)

        @block.vector
        def _(dve):
            dve.wait_ge(consts_ready, 1)
            dve.wait_ge(cnt_full, 1)
            nc.vector.tensor_copy(cnt[:], pT[:, 0:E0])
            dve.drain()
            nc.vector.scalar_tensor_tensor(padf[:], cnt[:], rowid[:, 0:1], base0[:], ALU.add, ALU.add)
            nc.vector.tensor_scalar(ntf[:], cnt[:], float(P - 1), None, ALU.add)
            dve.drain()
            nc.vector.tensor_copy(padrow[:], padf[:]).then_inc(pad_ready, 1)
            nc.vector.tensor_copy(nti[:], ntf[:])
            dve.drain()
            nc.vector.tensor_scalar(nti[:], nti[:], 7, None, ALU.logical_shift_right)
            dve.drain()
            nc.vector.tensor_copy(ntf[:], nti[:])
            dve.drain()
            nc.vector.tensor_tensor_scan(cum[:], ones[0:1, 0:E0], ntf[0:1, :], 0.0, ALU.mult, ALU.add)
            dve.drain()
            nc.vector.tensor_tensor(past, iota_i[:].unsqueeze(2).broadcast_to([1, L0_TILES, E0]),
                                    cum[:].unsqueeze(1).broadcast_to([1, L0_TILES, E0]), ALU.is_ge)
            dve.drain()
            nc.vector.tensor_reduce(texp[:], past, AX.X, ALU.add)
            dve.drain()
            nc.vector.tensor_tensor(past, past, ntf[0:1, :].unsqueeze(1).broadcast_to([1, L0_TILES, E0]), ALU.mult)
            dve.drain()
            nc.vector.tensor_reduce(tskip[:], past, AX.X, ALU.add)
            nc.vector.tensor_scalar(trow[:], texp[:], float(E0_STRIDE), None, ALU.mult)
            dve.drain()
            nc.vector.tensor_tensor(tskip[:], iota_i[:], tskip[:], ALU.subtract)
            dve.drain()
            nc.vector.scalar_tensor_tensor(trow[:], tskip[:], float(P), trow[:], ALU.mult, ALU.add)
            dve.drain()
            nc.vector.tensor_copy(T["tinfo"][0:1, :, 0], trow[:])
            nc.vector.tensor_scalar(T["tinfo"][0:1, :, 1], texp[:], float(E0 - 1), None, ALU.min)

            ge = big[:, 0:2 * TILES * (E0 - 1)].rearrange("p (t e) -> p t e", e=E0 - 1)
            shape = [P, 2 * TILES, E0 - 1]
            nc.vector.tensor_copy(slotf, T["slot0"][:].rearrange("p t k -> p (t k)"))
            nc.vector.tensor_scalar(ntf[:], ntf[:], float(P), float(-E0_STRIDE), ALU.mult, ALU.add)
            dve.drain()
            nc.vector.tensor_tensor(ge, slotf.unsqueeze(2).broadcast_to(shape),
                                    base0[:, 1:E0].unsqueeze(1).broadcast_to(shape), ALU.is_ge)
            dve.drain()
            nc.vector.tensor_tensor(ge, ge, ntf[:, 0:E0 - 1].unsqueeze(1).broadcast_to(shape), ALU.mult)
            dve.drain()
            nc.vector.tensor_reduce(usum[:, 0:2 * TILES], ge, AX.X, ALU.add)
            dve.drain()
            nc.vector.tensor_tensor(T["take0"][:].rearrange("p t k -> p (t k)"), slotf, usum[:, 0:2 * TILES], ALU.add)
            dve.drain()

            dve.wait_ge(act_step, 1)
            nc.vector.tensor_scalar(decay[0:1, 2:3], decay[0:1, 1:2], 1.0, None, ALU.add)
            dve.drain()
            nc.vector.reciprocal(kdec[:], decay[0:1, 2:3])
            dve.drain()
            nc.vector.tensor_tensor_scan(crow[:], kdec[:].broadcast_to([1, SEQ]), invt[:].broadcast_to([1, SEQ]), 0.0, ALU.mult, ALU.add).then_inc(dve_step, 1)
            dve.wait_ge(pe_step, 1)
            nc.vector.tensor_copy(ccol[:, 0, :], pS[0][:, 0:TPB]).then_inc(dve_step, 1)
            dve.wait_ge(pe_step, 2)
            for j in range(TPB):
                last = nc.vector.tensor_copy(ccol[:, 1, j:j + 1], pS[1][:, TPB - 1 - j:TPB - j])
            last.then_inc(dve_step, 1)
            dve.wait_ge(pe_step, 3)
            dve.wait_ge(s_sw, 64)
            nc.vector.tensor_reduce(csum[:], pS[0][:, 0:TPB], AX.X, ALU.add)
            for b in range(B):
                dve.drain()
                nc.vector.tensor_copy(usum[:], pO[b][:])
                for n in range(DB):
                    dve.drain()
                    nc.vector.tensor_tensor_reduce(out=big[:], in0=win[:, n, :], in1=usum[:], scale=1.0, scalar=0.0,
                                                   op0=ALU.mult, op1=ALU.add, accum_out=mstate[:, n, b:b + 1])
            dve.drain()
            for b in range(B):
                last = nc.vector.scalar_tensor_tensor(mstate[:, :, b], bin_col[:], csum[:, 0:1], mstate[:, :, b],
                                                      ALU.mult, ALU.add)
            last.then_inc(dve_step, 1)
            for b in range(B):
                dve.wait_ge(pe_step, 3 + DB + b + 1)
                nc.vector.tensor_tensor(T["summary"][:, b, :], pS[b % 2][:], bout_row[:], ALU.add).then_inc(dve_step, 1)


def mixture0(nc, A, T):
    c = ExitStack()
    with c:
        def sb(name, shape, dt=F32):
            return c.enter_context(nc.sbuf_tensor(name, shape, dt))

        def sem(name):
            return c.enter_context(nc.semaphore(name))

        bank, ident, tinfo, w01, wo0 = T["bank"], T["ident"], T["tinfo"], T["w01"], T["wo0"]
        N, MB = L0_TILES, M0 // P
        xb = sb("m0_x", [P, 2, D])
        xT = sb("m0_xT", [P, 2, DB, P])
        act_g = sb("m0_silu", [P, 2, M0])
        inter = sb("m0_inter", [P, 2, M0])
        interT = sb("m0_interT", [P, 2, MB, P])
        y = sb("m0_y", [P, 2, D])
        x_loaded = [sem("m0_x_even"), sem("m0_x_odd")]
        stored = [sem("m0_stored_even"), sem("m0_stored_odd")]
        xT_full, xT_ready, h_full, g_ready = sem("xT_full"), sem("xT_ready"), sem("h_full"), sem("g_ready")
        in_ready, inT_full, inT_ready = sem("in_ready"), sem("inT_full"), sem("inT_ready")
        y_full, y_ready = sem("y_full"), sem("y_ready")
        pX, pH, pI, pY = bank[0:2], bank[2:4], bank[4:6], bank[6:8]
        block = c.enter_context(nc.Block())

        @block.sync
        def _(sp):
            def first_row(i):
                at = tinfo[0:1, i, 0:1] if isinstance(i, int) else \
                    tinfo[0:1, bass.ds(i, 1), 0:1].rearrange("p o d -> p (o d)")
                return sp.value_load(at, min_val=0, max_val=TAB0_ROWS - P)

            def step(i, u, odd):
                if valid(i + 2, n=N):
                    need(sp, xT_full, i + 1)
                    sp.dma_start(xb[:, odd, :], T["tab0"][bass.ds(first_row(i + 2), P), :]).then_inc(x_loaded[odd], 16)
                if valid(i, n=N):
                    need(sp, y_ready, i + 1)
                    sp.dma_start(T["ytab0"][bass.ds(i * P, P), :], y[:, odd, :]).then_inc(stored[odd], 16)

            steps(sp, step, N, 2, 2, 0)
            for s in range(2):
                sp.wait_ge(stored[s], 16 * N // 2)

        @block.tensor
        def _(pe):
            pe.wait_ge(T["s_w0"], 16 * (2 * E0 + 1))

            def step(i, u, odd):
                s, o = odd, 1 - odd
                if valid(i - 1, n=N):
                    need(pe, in_ready, i)
                    need(pe, inT_ready, i - 2)
                    for m in range(MB):
                        last = nc.tensor.transpose(pI[o][:, m * P:m * P + P], inter[:, o, m * P:m * P + P], ident[:])
                    last.then_inc(inT_full, 1)
                if valid(i, n=N):
                    e = expert(pe, tinfo, i)
                    need(pe, xT_ready, i + 1)
                    need(pe, in_ready, i - 1)
                    for d in range(DB):
                        last = nc.tensor.matmul(pH[s][:], xT[:, s, d, :], row(w01, e * DB + d),
                                                start=(d == 0), stop=(d == DB - 1))
                    last.then_inc(h_full, 1)
                if valid(i + 1, n=N):
                    need(pe, x_loaded[o], (u + (odd + 1) // 2) * 16 + 16)
                    need(pe, xT_ready, i)
                    for d in range(DB):
                        last = nc.tensor.transpose(pX[o][:, d * P:d * P + P], xb[:, o, d * P:d * P + P], ident[:])
                    last.then_inc(xT_full, 1)
                if valid(i - 1, n=N):
                    e = expert(pe, tinfo, i - 1)
                    need(pe, inT_ready, i)
                    need(pe, y_ready, i - 2)
                    for m in range(MB):
                        last = nc.tensor.matmul(pY[o][:], interT[:, o, m, :], row(wo0, e * MB + m),
                                                start=(m == 0), stop=(m == MB - 1))
                    last.then_inc(y_full, 1)

            steps(pe, step, N, 2, 1, 1)

        @block.scalar
        def _(act):
            for w, name in zip(T["ws"], ("L1_ffn_Sg", "L1_ffn_Su", "L1_ffn_Sd")):
                for s in range(NSH):
                    act.dma_start(w[:, s], A[name][s].rearrange("(b p) h -> p b h", p=P)).then_inc(T["s_ws"], 16)

            def step(i, u, odd):
                s, o = odd, 1 - odd
                if valid(i, n=N):
                    need(act, h_full, i + 1)
                    need(act, in_ready, i - 1)
                    nc.scalar.activation(act_g[:, s, :], pH[s][:, 0:M0], ACT.Silu).then_inc(g_ready, 1)
                if valid(i + 1, n=N):
                    need(act, xT_full, i + 2)
                    need(act, h_full, i)
                    nc.scalar.copy(xT[:, o].rearrange("p d t -> p (d t)"), pX[o][:]).then_inc(xT_ready, 1)
                if valid(i - 1, n=N):
                    need(act, y_full, i)
                    need(act, stored[o], (u + (odd - 1) // 2) * 16)
                    nc.scalar.copy(y[:, o, :], pY[o][:]).then_inc(y_ready, 1)

            steps(act, step, N, 2, 1, 1)

        @block.vector
        def _(dve):
            def step(i, u, odd):
                s, o = odd, 1 - odd
                if valid(i - 1, n=N):
                    need(dve, inT_full, i)
                    need(dve, y_full, i - 2)
                    nc.vector.tensor_copy(interT[:, o].rearrange("p m t -> p (m t)"),
                                          pI[o][:, 0:M0]).then_inc(inT_ready, 1)
                if valid(i, n=N):
                    need(dve, g_ready, i + 1)
                    need(dve, inT_full, i - 1)
                    nc.vector.tensor_tensor(inter[:, s, :], act_g[:, s, :], pH[s][:, M0:2 * M0],
                                            ALU.mult).then_inc(in_ready, 1)

            steps(dve, step, N, 2, 1, 1)


def expert(eng, tinfo, i):
    at = tinfo[0:1, i, 1:2] if isinstance(i, int) else tinfo[0:1, bass.ds(i, 1), 1:2].rearrange("p o d -> p (o d)")
    return eng.value_load(at, min_val=0, max_val=E0 - 1)


def middle(nc, A, T):
    c = ExitStack()
    with c:
        def sb(name, shape, dt=F32):
            return c.enter_context(nc.sbuf_tensor(name, shape, dt))

        def sem(name):
            return c.enter_context(nc.semaphore(name))

        x_sb, bank, ident, onesb, before = T["x_sb"], T["bank"], T["ident"], T["onesb"], T["before"]
        gates, iota_e, summary, flatT = T["gates"], T["iota_e"], T["summary"], T["flatT"]
        top0, take0, top1, take1, kept1 = T["top0"], T["take0"], T["top1"], T["take1"], T["kept1"]
        pX, pL, pC, pG, pU = bank[0:2], bank[2], bank[3], bank[4:6], bank[6:8]

        y0 = sb("y0", [P, TPB, 2, D])
        z = sb("z", [P, TPB, D])
        flat = sb("flat", [P, TPB, D])
        flatTt = sb("flatTt", [P, 2, DB, P])
        wr = sb("wr", [P, DB, E1])
        bias_r = sb("bias_r", [P, E1])
        gamma = sb("gamma", [P, D])
        beta = sb("beta", [P, D])
        wmix = sb("wmix", [P, TILES, 2])
        wtmp = sb("wtmp", [P, 3, TILES])
        bn = sb("bn1", [P, TPB, 6])
        mv = sb("mv1", [P, TPB, 2])
        rstd = sb("rstd1", [P, TPB])
        half, ve, nt = sb("half1", [P, TPB]), sb("ve1", [P, TPB]), sb("nt1", [P, TPB])
        lnz = sb("lnz", [P, TPB, 2])
        lnf = sb("lnf", [P, TPB, 2])
        logits = sb("logits1", [P, TPB, E1])
        m8 = sb("m81", [P, 8])
        i8 = sb("i81", [P, 8], U32)
        idxf = sb("idxf1", [P, TPB, TOP1])
        onehot = sb("onehot1", [P, TPB, TOP1, E1])
        pair = sb("pair1", [P, 2, E1])
        mask = sb("mask1", [P, TPB, E1], BF16)
        chosen = sb("chosen1", [P, 2, E1], BF16)
        junk = sb("junk1", [P, TOP1, E1])
        posf = sb("posf", [P, TOP1])
        drop = sb("drop", [P, TOP1])
        slotf = sb("slotf1", [P, TOP1])
        slot1 = sb("slot1", [P, TPB, TOP1], I32)
        shared = SharedExperts(nc, T, c, "a")

        small_loaded = sem("mid_small_loaded")
        gathered = sem("y0_gathered")
        beta_ready, wexp_ready = sem("beta_ready"), sem("wexp_ready")
        x2_ready, lnz_ready, z_ready, y_ready, xb_ready = (sem(n) for n in (
            "x2_ready", "lnz_ready", "z_ready", "ysum_ready", "x_beta_ready"))
        x3_ready, lnf_ready, flat_ready = sem("x3_ready"), sem("lnf_ready"), sem("flat_ready")
        fT_full, fT_ready, fT_kept = sem("flatT_full"), sem("flatT_ready"), sem("flatT_kept")
        lg_full, lg_read, mask_ready, pos_full, pos_read = (sem(n) for n in (
            "lg1_full", "lg1_read", "mask1_ready", "pos1_full", "pos1_read"))
        slot_ready, scattered = sem("slot1_ready"), sem("flat_scattered")
        w_ready = sem("mid_zero_ready")
        groups_done = B - 1
        block = c.enter_context(nc.Block())

        def groups(eng, step):
            step(-1)
            with eng.Fori(0, groups_done) as g:
                step(g)
            step(B - 1)

        def prepared(g):
            return not isinstance(g, int) or g + 1 < B

        def routed(g):
            return not isinstance(g, int) or g >= 0

        def with_shared(g):
            return not isinstance(g, int)

        @block.sync
        def _(sp):
            sp.dma_start(gamma[:], A["L1_xattn_gamma"].partition_broadcast(P)).then_inc(small_loaded, 16)
            sp.dma_start(beta[:], A["L1_xattn_beta"].partition_broadcast(P)).then_inc(small_loaded, 16)
            sp.dma_start(wr[:], A["L1_ffn_Wr"].rearrange("(b p) e -> p b e", p=P)).then_inc(small_loaded, 16)
            sp.dma_start(bias_r[:], A["L1_ffn_router_bias"].partition_broadcast(P)).then_inc(small_loaded, 16)

        @block.gpsimd
        def _(pool):
            nc.gpsimd.memset(chosen[:], 0.0).then_inc(w_ready, 1)
            pool.wait_ge(T["s_zero1"], 16 * (E1 * CAP1 // (8 * P)))
            for g in range(-1, B):
                n = g + 1
                if n < B:
                    need(pool, x2_ready, TPB * n)
                    for j in range(TPB):
                        for k in range(2):
                            nc.gpsimd.indirect_dma_start(
                                y0[:, j, k, :], None, T["ytab0"],
                                bass.IndirectOffsetOnAxis(take0[:, n * TPB + j, k:k + 1], 0)).then_inc(gathered, 16)
                if g >= 0:
                    for j in range(TPB):
                        pool.wait_ge(fT_ready, TPB * g + j + 1)
                        nc.gpsimd.tensor_copy(flatT[:, g, :, j * P:j * P + P], flatTt[:, j % 2]).then_inc(fT_kept, 1)
                    for j in range(TPB):
                        pool.wait_ge(slot_ready, TPB * g + j + 1)
                        for k in range(TOP1):
                            nc.gpsimd.indirect_dma_start(
                                T["tab1"], bass.IndirectOffsetOnAxis(slot1[:, j, k:k + 1], 0), flat[:, j, :], None,
                                bounds_check=E1 * CAP1 - 1, oob_is_err=False).then_inc(scattered, 16)
                if n < B:
                    for j in range(TPB):
                        t = n * TPB + j
                        pool.wait_ge(z_ready, t + 1)
                        nc.gpsimd.tensor_tensor(z[:, j, :], z[:, j, :], summary[:, n, :], ALU.add).then_inc(y_ready, 1)
                        if t == 0:
                            pool.wait_ge(beta_ready, 1)
                        nc.gpsimd.tensor_tensor(x_sb[:, t, :], x_sb[:, t, :], beta[:], ALU.add).then_inc(xb_ready, 1)
            pool.wait_ge(scattered, 16 * TILES * TOP1)

        @block.tensor
        def _(pe):
            pe.wait_ge(small_loaded, 64)
            pe.wait_ge(T["s_ws"], 16 * 3 * NSH)
            pe.wait_ge(w_ready, 1)

            def route(g):
                for j in range(TPB):
                    need(pe, flat_ready, g * TPB + (j + 1))
                    if j >= 2:
                        need(pe, fT_ready, g * TPB + (j - 1))
                    for d in range(DB):
                        last = nc.tensor.transpose(pX[j % 2][:, d * P:d * P + P], flat[:, j, d * P:d * P + P], ident[:])
                    last.then_inc(fT_full, 1)
                    if j:
                        logit(g, j - 1)
                logit(g, TPB - 1)

            def logit(g, j):
                need(pe, fT_ready, g * TPB + (j + 1))
                if j:
                    need(pe, lg_read, g * TPB + j)
                for d in range(DB):
                    last = nc.tensor.matmul(pL[:, 0:E1], flatTt[:, j % 2, d, :], wr[:, d, :],
                                            start=(d == 0), stop=(d == DB - 1))
                last.then_inc(lg_full, 1)

            def positions(g, j):
                need(pe, mask_ready, g * TPB + (j + 1))
                if j:
                    need(pe, pos_read, g * TPB + j)
                nc.tensor.matmul(pC[:, 0:E1], before[:], mask[:, j, :], start=True, stop=False)
                nc.tensor.matmul(pC[:, 0:E1], onesb[:], chosen[:, j % 2, :], start=False, stop=True).then_inc(pos_full, 1)

            def step(g):
                if not routed(g):
                    return
                route(g)
                if with_shared(g):
                    need(pe, fT_kept, g * TPB + TPB)
                for n in range(SharedExperts.CHUNKS):
                    if with_shared(g):
                        shared.up(pe, g, g, n, pG, pU)
                    if n < TPB:
                        positions(g, n)
                if with_shared(g):
                    for j in range(TPB):
                        shared.down(pe, g, j, pX)
                    need(pe, shared.y_read, g * TPB + TPB)

            groups(pe, step)

        @block.scalar
        def _(act):
            act.wait_ge(w_ready, 1)
            act.wait_ge(wexp_ready, 1)
            nc.scalar.activation(wtmp[:, 1, :], wtmp[:, 0, :], ACT.Exp).then_inc(wexp_ready, 1)

            def step(g):
                if routed(g):
                    for j in range(TPB):
                        need(act, fT_full, g * TPB + (j + 1))
                        if j >= 2:
                            need(act, fT_kept, g * TPB + (j - 1))
                            need(act, lg_full, g * TPB + (j - 1))
                        nc.scalar.copy(flatTt[:, j % 2].rearrange("p d t -> p (d t)"), pX[j % 2][:]).then_inc(fT_ready, 1)
                for n in range(SharedExperts.CHUNKS):
                    if prepared(g) and n == 7:
                        need(act, scattered, (g + 1) * (TPB * TOP1 * 16))
                    if with_shared(g):
                        shared.gate(act, g, n, pG)
                    if prepared(g):
                        if n == 4:
                            need(act, lnz_ready, g * TPB + 2 * TPB, alone=1)
                            need(act, x3_ready, g * TPB + TPB)
                            for j in range(TPB):
                                nc.scalar.activation(z[:, j, :], row(x_sb, (g + 1) * TPB + j), ACT.Identity,
                                                     scale=lnz[:, j, 0:1], bias=lnz[:, j, 1:2]).then_inc(z_ready, 1)
                        if n == 7:
                            need(act, lnf_ready, g * TPB + 2 * TPB, alone=1)
                            for j in range(TPB):
                                nc.scalar.activation(flat[:, j, :], row(x_sb, (g + 1) * TPB + j), ACT.Identity,
                                                     scale=lnf[:, j, 0:1], bias=lnf[:, j, 1:2]).then_inc(flat_ready, 1)

            groups(act, step)

        @block.vector
        def _(dve):
            dve.wait_ge(small_loaded, 64)
            dve.wait_ge(w_ready, 1)
            nc.vector.tensor_tensor(wtmp[:, 0, :], top0[:, :, 1], top0[:, :, 0], ALU.subtract).then_inc(wexp_ready, 1)
            nc.vector.tensor_scalar(beta[:], beta[:], gates[:, 1:2], None, ALU.mult).then_inc(beta_ready, 1)
            dve.wait_ge(wexp_ready, 2)
            nc.vector.tensor_scalar(wtmp[:, 2, :], wtmp[:, 1, :], 1.0, None, ALU.add)
            dve.drain()
            nc.vector.reciprocal(wtmp[:, 0, :], wtmp[:, 2, :])
            dve.drain()
            nc.vector.tensor_scalar(wmix[:, :, 0], wtmp[:, 0, :], gates[:, 2:3], None, ALU.mult)
            dve.drain()
            nc.vector.tensor_tensor(wmix[:, :, 1], wmix[:, :, 0], wtmp[:, 1, :], ALU.mult)
            dve.drain()

            def choose(g, j):
                need(dve, lg_full, g * TPB + (j + 1))
                nc.vector.tensor_tensor(logits[:, j, :], pL[:, 0:E1], bias_r[:], ALU.add).then_inc(lg_read, 1)
                dve.drain()
                nc.vector.max(m8[:], logits[:, j, :])
                dve.drain()
                nc.vector.max_index(i8[:], m8[:], logits[:, j, :])
                nc.vector.tensor_copy(row(top1, g * TPB + j), m8[:, 0:TOP1])
                dve.drain()
                nc.vector.tensor_copy(idxf[:, j, :], i8[:, 0:TOP1])
                dve.drain()
                for k in range(TOP1):
                    nc.vector.tensor_scalar(onehot[:, j, k, :], iota_e[:], idxf[:, j, k:k + 1], None, ALU.is_equal)
                dve.drain()
                for k in range(2):
                    nc.vector.tensor_tensor(pair[:, k, :], onehot[:, j, 2 * k, :], onehot[:, j, 2 * k + 1, :], ALU.add)
                dve.drain()
                nc.vector.tensor_tensor(mask[:, j, :], pair[:, 0, :], pair[:, 1, :], ALU.add).then_inc(mask_ready, 1)

            def place(g, j):
                need(dve, pos_full, g * TPB + (j + 1))
                nc.vector.tensor_tensor(chosen[:, 1 - j % 2, :], chosen[:, j % 2, :], mask[:, j, :], ALU.add)
                for k in range(TOP1):
                    last = nc.vector.tensor_tensor_reduce(out=junk[:, k, :], in0=onehot[:, j, k, :], in1=pC[:, 0:E1],
                                                          scale=1.0, scalar=0.0, op0=ALU.mult, op1=ALU.add,
                                                          accum_out=posf[:, k:k + 1])
                last.then_inc(pos_read, 1)
                dve.drain()
                nc.vector.tensor_scalar(drop[:], posf[:], float(CAP1), float(E1 * CAP1), ALU.is_ge, ALU.mult)
                nc.vector.tensor_scalar(row(kept1, g * TPB + j), posf[:], float(CAP1), None, ALU.is_lt)
                nc.vector.scalar_tensor_tensor(slotf[:], idxf[:, j, :], float(CAP1), posf[:], ALU.mult, ALU.add)
                dve.drain()
                nc.vector.tensor_tensor(drop[:], slotf[:], drop[:], ALU.add)
                nc.vector.tensor_scalar(posf[:], posf[:], float(CAP1 - 1), None, ALU.min)
                dve.drain()
                nc.vector.scalar_tensor_tensor(row(take1, g * TPB + j), idxf[:, j, :], float(CAP1), posf[:],
                                               ALU.mult, ALU.add)
                nc.vector.tensor_copy(slot1[:, j, :], drop[:]).then_inc(slot_ready, 1)
                dve.drain()

            def scale_and_bias(ln, ready):
                nc.vector.tensor_copy(ln[:, :, 0], rstd[:])
                nc.vector.scalar_tensor_tensor(ln[:, :, 1], mv[:, :, 0], -1.0, rstd[:], ALU.mult,
                                               ALU.mult).then_inc(ready, TPB)

            def statistics():
                dve.drain()
                for j in range(TPB):
                    nc.vector.bn_aggr(mv[:, j, :], bn[:, j, :])
                dve.drain()
                rsqrt(nc, dve, rstd[:], mv[:, :, 1], half[:], (ve[:], nt[:]))

            def combine(g):
                need(dve, gathered, g * (TPB * 32) + TPB * 32 * 2)
                for k in range(2):
                    for j in range(TPB):
                        t = (g + 1) * TPB + j
                        last = nc.vector.scalar_tensor_tensor(row(x_sb, t), y0[:, j, k, :], row(wmix, t)[:, k:k + 1],
                                                              row(x_sb, t), ALU.mult, ALU.add)
                        if k:
                            last.then_inc(x2_ready, 1)
                    dve.drain()
                for j in range(TPB):
                    nc.vector.bn_stats(bn[:, j, :], row(x_sb, (g + 1) * TPB + j))

            def attend(g):
                dve.drain()
                nc.vector.tensor_scalar(rstd[:], rstd[:], gates[:, 1:2], None, ALU.mult)
                for j in range(TPB):
                    nc.vector.scalar_tensor_tensor(z[:, j, :], z[:, j, :], mv[:, j, 0:1], gamma[:],
                                                   ALU.subtract, ALU.mult)
                dve.drain()
                for j in range(TPB):
                    t = (g + 1) * TPB + j
                    need(dve, xb_ready, t + 1)
                    nc.vector.scalar_tensor_tensor(row(x_sb, t), z[:, j, :], rstd[:, j:j + 1], row(x_sb, t),
                                                   ALU.mult, ALU.add).then_inc(x3_ready, 1)

            def step(g):
                if routed(g):
                    for j in range(TPB):
                        choose(g, j)
                for n in range(SharedExperts.CHUNKS):
                    if with_shared(g):
                        shared.product(dve, g, n, pU)
                    if routed(g) and n < TPB:
                        place(g, n)
                    if prepared(g):
                        if n == 1:
                            combine(g)
                        if n == 2:
                            statistics()
                            need(dve, z_ready, g * TPB + TPB)
                            scale_and_bias(lnz, lnz_ready)
                        if n == 5:
                            for j in range(TPB):
                                need(dve, y_ready, g * TPB + (TPB + j + 1))
                                nc.vector.bn_stats(bn[:, j, :], z[:, j, :])
                            statistics()
                            attend(g)
                        if n == 6:
                            dve.drain()
                            for j in range(TPB):
                                nc.vector.bn_stats(bn[:, j, :], row(x_sb, (g + 1) * TPB + j))
                            statistics()
                            need(dve, flat_ready, g * TPB + TPB)
                            scale_and_bias(lnf, lnf_ready)
                if with_shared(g):
                    for j in range(TPB):
                        shared.add(dve, g, j, g * TPB + j, pX)

            groups(dve, step)


def experts(nc, A, T):
    c = ExitStack()
    with c:
        def sb(name, shape, dt=F32):
            return c.enter_context(nc.sbuf_tensor(name, shape, dt))

        def sem(name):
            return c.enter_context(nc.semaphore(name))

        bank, ident, top1, kept1, wt1 = T["bank"], T["ident"], T["top1"], T["kept1"], T["wt1"]
        RING = 4
        AHEAD = RING - 1
        xb = sb("m1_x", [P, RING, D])
        wg = sb("m1_wg", [P, RING, DB, H1])
        wu = sb("m1_wu", [P, RING, DB, H1])
        wd = sb("m1_wd", [P, RING, D])
        xT = sb("m1_xT", [P, 2, DB, CAP1])
        g = sb("m1_silu", [P, 2, CAP1])
        h = sb("m1_h", [P, 2, CAP1])
        y = sb("m1_y", [P, 2, D])
        wsum = sb("wsum", [P, TILES])
        x_loaded = [sem(f"m1_x_loaded_{n}") for n in range(RING)]
        w_loaded = [sem(f"m1_w_loaded_{n}") for n in range(RING)]
        stored = [sem("m1_stored_even"), sem("m1_stored_odd")]
        xT_full, xT_ready, h_full, g_ready, h_ready = (sem(n) for n in (
            "m1_xT_full", "m1_xT_ready", "m1_h_full", "m1_g_ready", "m1_h_ready"))
        y_full, y_ready = sem("m1_y_full"), sem("m1_y_ready")
        less_max, exp_ready = sem("m1_less_max"), sem("m1_exp_ready")
        pX, pH, pY = bank[0:2], bank[2:4], bank[4:6]
        block = c.enter_context(nc.Block())

        def weights(name, e):
            if isinstance(e, int):
                return A[name][e].rearrange("(p b) h -> p b h", b=DB)
            return A[name][bass.ds(e, 1)].rearrange("o (p b) h -> p (o b) h", b=DB)

        def back(e):
            return A["L1_ffn_Wd"][e] if isinstance(e, int) else \
                A["L1_ffn_Wd"][bass.ds(e, 1)].rearrange("o h d -> h (o d)")

        @block.sync
        def _(sp):
            def step(i, u, q):
                if valid(i + AHEAD, n=E1):
                    e, n = i + AHEAD, (q + AHEAD) % RING
                    need(sp, y_full, i)
                    sp.dma_start(xb[:, n, :], T["tab1"][bass.ds(e * CAP1, CAP1), :]).then_inc(x_loaded[n], 16)
                    sp.dma_start(wg[:, n], weights("L1_ffn_Wg", e)).then_inc(w_loaded[n], 16)
                    sp.dma_start(wu[:, n], weights("L1_ffn_Wu", e)).then_inc(w_loaded[n], 16)
                    sp.dma_start(wd[:, n, :], back(e)).then_inc(w_loaded[n], 16)
                if valid(i, n=E1):
                    need(sp, y_ready, i + 1)
                    sp.dma_start(T["ytab1"][bass.ds(i * CAP1, CAP1), :], y[:, q % 2, :]).then_inc(stored[q % 2], 16)

            steps(sp, step, E1, RING, AHEAD, 0)
            for s in range(2):
                sp.wait_ge(stored[s], 16 * E1 // 2)

        @block.tensor
        def _(pe):
            def step(i, u, q):
                s, o = q % 2, 1 - q % 2
                if valid(i + 1, n=E1):
                    n = (q + 1) % RING
                    need(pe, x_loaded[n], (u + (q + 1) // RING) * 16 + 16)
                    need(pe, xT_ready, i)
                    for b in range(DB):
                        last = nc.tensor.transpose(pX[o][:, b * P:b * P + P],
                                                   xb[:, n, :].rearrange("t (p b) -> t b p", b=DB)[:, b, :], ident[:])
                    last.then_inc(xT_full, 1)
                if valid(i, n=E1):
                    need(pe, w_loaded[q], u * 48 + 48)
                    need(pe, xT_ready, i + 1)
                    need(pe, h_ready, i - 1)
                    for k, w in enumerate((wg, wu)):
                        for b in range(DB):
                            last = nc.tensor.matmul(pH[s][:, k * CAP1:(k + 1) * CAP1], w[:, q, b, :], xT[:, s, b, :],
                                                    start=(b == 0), stop=(b == DB - 1))
                    last.then_inc(h_full, 1)
                if valid(i - 1, n=E1):
                    need(pe, h_ready, i)
                    need(pe, y_ready, i - 2)
                    nc.tensor.matmul(pY[o][:], h[:, o, :], wd[:, (q - 1) % RING, :],
                                     start=True, stop=True).then_inc(y_full, 1)

            steps(pe, step, E1, RING, 1, 1)

        @block.scalar
        def _(act):
            act.wait_ge(less_max, 1)
            nc.scalar.activation(wt1[:], wt1[:], ACT.Exp).then_inc(exp_ready, 1)

            def step(i, u, q):
                s, o = q % 2, 1 - q % 2
                if valid(i + 1, n=E1):
                    need(act, xT_full, i + 2)
                    need(act, h_full, i)
                    nc.scalar.copy(xT[:, o].rearrange("p d t -> p (d t)"), pX[o][:]).then_inc(xT_ready, 1)
                if valid(i, n=E1):
                    need(act, h_full, i + 1)
                    need(act, h_ready, i - 1)
                    nc.scalar.activation(g[:, s, :], pH[s][:, 0:CAP1], ACT.Silu).then_inc(g_ready, 1)

            steps(act, step, E1, RING, 1, 1)

        @block.vector
        def _(dve):
            shape = [P, TILES, TOP1]
            nc.vector.tensor_tensor(wt1[:], top1[:], top1[:, :, 0:1].broadcast_to(shape), ALU.subtract).then_inc(less_max, 1)
            dve.wait_ge(exp_ready, 1)
            nc.vector.tensor_reduce(wsum[:], wt1[:], AX.X, ALU.add)
            dve.drain()
            nc.vector.reciprocal(wsum[:], wsum[:])
            dve.drain()
            nc.vector.tensor_tensor(wt1[:], wt1[:], wsum[:].unsqueeze(2).broadcast_to(shape), ALU.mult)
            dve.drain()
            nc.vector.scalar_tensor_tensor(wt1[:], kept1[:], T["gates"][:, 3:4], wt1[:], ALU.mult, ALU.mult)
            dve.drain()

            def step(i, u, q):
                s, o = q % 2, 1 - q % 2
                if valid(i, n=E1):
                    need(dve, g_ready, i + 1)
                    need(dve, y_full, i - 1)
                    nc.vector.tensor_tensor(h[:, s, :], g[:, s, :], pH[s][:, CAP1:2 * CAP1], ALU.mult).then_inc(h_ready, 1)
                if valid(i - 1, n=E1):
                    need(dve, y_full, i)
                    need(dve, stored[o], (u * (RING // 2) + (q - 1) // 2) * 16)
                    nc.vector.tensor_copy(y[:, o, :], pY[o][:]).then_inc(y_ready, 1)

            steps(dve, step, E1, RING, 1, 1)


def finish(nc, A, T, out):
    c = ExitStack()
    with c:
        def sb(name, shape, dt=F32):
            return c.enter_context(nc.sbuf_tensor(name, shape, dt))

        def sem(name):
            return c.enter_context(nc.semaphore(name))

        x_sb, bank, take1, wt1 = T["x_sb"], T["bank"], T["take1"], T["wt1"]
        pY, pG, pU = bank[0:2], bank[4:6], bank[6:8]
        RING = 4
        G = B - 1
        y1 = sb("y1", [P, RING, TOP1, D])
        shared = SharedExperts(nc, T, c, "b")
        gathered = [sem(f"y1_gathered_{n}") for n in range(RING)]
        combined, stored = sem("combined"), sem("out_stored")
        out_v = out.rearrange("b (t p) d -> p (b t) d", p=P)
        block = c.enter_context(nc.Block())

        @block.sync
        def _(sp):
            for t in range(TILES):
                if t < G * TPB:
                    sp.wait_ge(combined, t + 1)
                else:
                    sp.wait_ge(shared.y_read, t - G * TPB + 1)
                sp.dma_start(out_v[:, t, :], x_sb[:, t, :]).then_inc(stored, 16)
            sp.wait_ge(stored, 16 * TILES)

        @block.gpsimd
        def _(pool):
            for t in range(TILES):
                need(pool, combined, t - RING + 1)
                for k in range(TOP1):
                    nc.gpsimd.indirect_dma_start(
                        y1[:, t % RING, k, :], None, T["ytab1"],
                        bass.IndirectOffsetOnAxis(take1[:, t, k:k + 1], 0)).then_inc(gathered[t % RING], 16)

        @block.tensor
        def _(pe):
            for n in range(SharedExperts.CHUNKS):
                shared.up(pe, 0, G, n, pG, pU)
            for j in range(TPB):
                shared.down(pe, 0, j, pY)

        @block.scalar
        def _(act):
            for n in range(SharedExperts.CHUNKS):
                shared.gate(act, 0, n, pG)

        @block.vector
        def _(dve):
            with dve.Fori(0, TILES // RING) as u:
                for q in range(RING):
                    if q % 2 == 0:
                        shared.product(dve, 0, u * 2 + q // 2, pU, odd=q // 2)
                    t = u * RING + q
                    need(dve, gathered[q], u * (16 * TOP1) + 16 * TOP1)
                    for k in range(TOP1):
                        last = nc.vector.scalar_tensor_tensor(row(x_sb, t), y1[:, q, k, :], row(wt1, t)[:, k:k + 1],
                                                              row(x_sb, t), ALU.mult, ALU.add)
                        if k < TOP1 - 1:
                            dve.drain()
                    last.then_inc(combined, 1)
            dve.drain()
            for j in range(TPB):
                shared.add(dve, 0, j, G * TPB + j, pY)


class SharedExperts:

    CHUNKS = NSH * HSH // P

    def __init__(self, nc, T, c, tag):
        self.nc, self.T = nc, T
        n = self.CHUNKS
        self.g = c.enter_context(nc.sbuf_tensor(f"sh_gate_{tag}", [P, 2, SEQ], F32))
        self.h = c.enter_context(nc.sbuf_tensor(f"sh_h_{tag}", [P, n, SEQ], F32))
        self.up_full, self.g_ready, self.h_ready, self.y_full, self.y_read = (
            c.enter_context(nc.semaphore(f"sh_{s}_{tag}")) for s in ("up_full", "g_ready", "h_ready", "y_full", "y_read"))

    def up(self, pe, r, g, n, pG, pU):
        nc, (sg, su, _), flatT = self.nc, self.T["ws"], self.T["flatT"]
        s, cols = n // (HSH // P), (n % (HSH // P)) * P
        if n >= 2:
            need(pe, self.h_ready, r * self.CHUNKS + (n - 1))
        for w, bank in ((sg, pG[n % 2]), (su, pU[n % 2])):
            for d in range(DB):
                rhs = flatT[:, g, d, :] if isinstance(g, int) else \
                    flatT[:, bass.ds(g, 1), d, :].rearrange("p o t -> p (o t)")
                last = nc.tensor.matmul(bank[:], w[:, s, d, cols:cols + P], rhs, start=(d == 0), stop=(d == DB - 1))
        last.then_inc(self.up_full, 1)

    def gate(self, act, r, n, pG):
        need(act, self.up_full, r * self.CHUNKS + (n + 1))
        if n >= 2:
            need(act, self.h_ready, r * self.CHUNKS + (n - 1))
        self.nc.scalar.activation(self.g[:, n % 2, :], pG[n % 2][:], ACT.Silu).then_inc(self.g_ready, 1)

    def product(self, dve, r, n, pU, odd=None):
        odd = n % 2 if odd is None else odd
        need(dve, self.g_ready, r * self.CHUNKS + (n + 1))
        self.nc.vector.tensor_tensor(row(self.h, n), self.g[:, odd, :], pU[odd][:], ALU.mult).then_inc(self.h_ready, 1)

    def down(self, pe, r, j, pY):
        nc, sd = self.nc, self.T["ws"][2]
        need(pe, self.h_ready, r * self.CHUNKS + self.CHUNKS)
        if j >= 2:
            need(pe, self.y_read, r * TPB + (j - 1))
        for n in range(self.CHUNKS):
            s, b = n // (HSH // P), n % (HSH // P)
            last = nc.tensor.matmul(pY[j % 2][:], self.h[:, n, j * P:j * P + P], sd[:, s, b, :],
                                    start=(n == 0), stop=(n == self.CHUNKS - 1))
        last.then_inc(self.y_full, 1)

    def add(self, dve, r, j, t, pY):
        x = row(self.T["x_sb"], t)
        need(dve, self.y_full, r * TPB + (j + 1))
        self.nc.vector.scalar_tensor_tensor(x, pY[j % 2][:], self.T["gates"][:, 3:4], x, ALU.mult,
                                            ALU.add).then_inc(self.y_read, 1)


INPUTS = (
    "x", "ctx_2048", "g_xattn", "g_ffn", "L0_ffn_w_gate", "L0_ffn_wi_0", "L0_ffn_wi_1", "L0_ffn_wo",
    "L1_xattn_decay", "L1_xattn_W_in", "L1_xattn_b_in", "L1_xattn_W_out", "L1_xattn_b_out",
    "L1_xattn_gamma", "L1_xattn_beta", "L1_ffn_Wr", "L1_ffn_router_bias", "L1_ffn_Wg", "L1_ffn_Wu",
    "L1_ffn_Wd", "L1_ffn_Sg", "L1_ffn_Su", "L1_ffn_Sd")


def kernel(**inputs):
    import numpy as np
    import concourse.bacc as bacc
    from concourse import mybir
    from concourse.bass_utils import run_bass_kernel_spmd

    nc = bacc.Bacc("TRN2", target_bir_lowering=False, num_devices=1)
    arrays, A = {}, {}
    for name in INPUTS:
        a = np.ascontiguousarray(inputs[name])
        if inputs[name].ndim == 0:
            a = a.reshape(1, 1)
        arrays[f"in_{name}"] = a
        A[name] = nc.dram_tensor(f"in_{name}", a.shape, mybir.dt.from_np(a.dtype), kind="ExternalInput").ap()
    out = nc.dram_tensor("out", inputs["x"].shape, mybir.dt.float32, kind="ExternalOutput").ap()
    build(nc, A, out)
    r = run_bass_kernel_spmd(nc, [arrays], core_ids=[0])
    return r.results[0]["out"]
```

```python
from contextlib import ExitStack

import concourse.bass as bass
from concourse import mybir

F32 = mybir.dt.float32
F32R = mybir.dt.float32r
BF16 = mybir.dt.bfloat16
I32 = mybir.dt.int32
U32 = mybir.dt.uint32
ALU = mybir.AluOpType
ACT = mybir.ActivationFunctionType
AX = mybir.AxisListType

P = 128
B, SEQ, D = 4, 512, 512
TILES = B * SEQ // P
TPB = SEQ // P
DB = D // P
HEAD = 64
E0, M0 = 8, 256
E1, H1, TOP1, CAP1 = 64, 128, 4, 128
NSH, HSH = 2, 512
LN_EPS = 1e-5
E0_STRIDE = B * SEQ + P
L0_TILES = 40
DUMMY_ROW = E0 * E0_STRIDE
TAB0_ROWS = DUMMY_ROW + E0 * P
RSQRT_MAGIC = float(0x5F3759DF)


def seen(k):
    return min(k + 1, TILES) if isinstance(k, int) else k + 1


def need(eng, sem, value, alone=0):
    if not isinstance(value, int):
        if alone:
            eng.wait_ge(sem, alone)
        eng.wait_ge(sem, value)
    elif value > 0:
        eng.wait_ge(sem, value)


def row(t, k):
    if isinstance(k, int):
        return t[:, k, :]
    return t[:, bass.ds(k, 1), :].rearrange("p o d -> p (o d)")


def valid(*tiles, n=TILES):
    return all(not isinstance(k, int) or 0 <= k < n for k in tiles)


def steps(eng, step, n, ring, lead, tail):
    first, last = max(-(-lead // ring), -(-4 // ring)), (n - lead) // ring
    for i in range(-lead, first * ring):
        step(i, i // ring, i % ring)
    with eng.Fori(first, last) as u:
        for c in range(ring):
            step(u * ring + c, u, c)
    for i in range(last * ring, n + tail):
        step(i, i // ring, i % ring)


def rsqrt(nc, dve, y, v, half, scratch):
    ve, t = scratch
    nc.vector.tensor_scalar(ve, v, LN_EPS, None, ALU.add)
    dve.drain()
    nc.vector.tensor_scalar(half.bitcast(I32), ve.bitcast(I32), 1, None, ALU.logical_shift_right)
    dve.drain()
    nc.vector.tensor_scalar(y.bitcast(I32), half.bitcast(I32), -1.0, RSQRT_MAGIC, ALU.mult, ALU.add)
    dve.drain()
    for _ in range(3):
        nc.vector.tensor_tensor(t, y, y, ALU.mult)
        dve.drain()
        nc.vector.scalar_tensor_tensor(t, t, -0.5, ve, ALU.mult, ALU.mult)
        dve.drain()
        nc.vector.scalar_tensor_tensor(y, t, 1.5, y, ALU.add, ALU.mult)
        dve.drain()


def build(nc, A, out):
    ctx = ExitStack()
    with ctx:
        def sb(name, shape, dt=F32, c=ctx, side=None):
            return c.enter_context(nc.sbuf_tensor(name, shape, dt, side=side))

        bank = [ctx.enter_context(nc.psum_tensor(f"bank{n}", [P, 512], F32)) for n in range(8)]

        x_sb = sb("x_sb", [P, TILES, D])
        ident = sb("ident", [P, P])
        identb = sb("identb", [P, P], BF16)
        onesb = sb("onesb", [P, P], BF16)
        before = sb("before", [P, P], BF16)
        iota_e = sb("iota_e", [P, E1])
        base0 = sb("base0", [P, E0])
        base1 = sb("base1", [P, E1])
        rowid = sb("rowid", [P, 1])
        gates = sb("gates", [P, 4])
        top0 = sb("top0", [P, TILES, 2])
        slot0 = sb("slot0", [P, TILES, 2], I32)
        take0 = sb("take0", [P, TILES, 2], I32)
        summary = sb("summary", [P, B, D])
        tinfo = sb("tinfo", [1, L0_TILES, 2], I32)

        tab0 = nc.dram_tensor("tab0", (TAB0_ROWS, D), F32, kind="Internal").ap()
        ytab0 = nc.dram_tensor("ytab0", (L0_TILES * P, D), F32, kind="Internal").ap()
        tab1 = nc.dram_tensor("tab1", (E1 * CAP1, D), F32, kind="Internal").ap()
        ytab1 = nc.dram_tensor("ytab1", (E1 * CAP1, D), F32, kind="Internal").ap()

        arena0 = ExitStack()
        later = ExitStack()
        with arena0:
            w01 = sb("w01", [P, E0 * DB, 2 * M0], F32, arena0, "right")
            wo0 = sb("wo0", [P, E0 * (M0 // P), D], F32, arena0, "right")
            s_w0 = arena0.enter_context(nc.semaphore("weights0_loaded"))
            s_zero1 = ctx.enter_context(nc.semaphore("table1_zeroed"))
            T = dict(locals())
            held = ExitStack()
            with held:
                T["ctx_sb"] = sb("ctx_sb", [P, TILES, D], F32, held)
                T["zeros"] = sb("zeros", [P, D], F32, held)
                T["chosen"] = sb("chosen", [P, 2, E0], BF16, held)
                T["ccol"] = sb("ccol", [P, 2, TPB], F32, held)
                T["ucol"] = sb("ucol", [P, DB, B], F32, held)
                T["ones"] = sb("ones", [P, E0], F32, held)
                attention(nc, A, T)
                summary_and_tiles(nc, A, T)
            later.__enter__()
            T["w_sd"] = sb("w_sd", [P, NSH, DB, HSH], F32, later)
            T["s_ws"] = later.enter_context(nc.semaphore("shared_weights_loaded"))
            staged = ExitStack()
            staged.__enter__()
            T["stage"] = sb("stage", [P, 2, NSH, DB * HSH], F32, staged)
            mixture0(nc, A, T)
        with later:
            with staged:
                T["w_hi"], T["w_lo"] = (sb(n, [P, 2, NSH, DB * HSH], F32R, later, "right") for n in ("w_hi", "w_lo"))
                T["flat_hi"], T["flat_lo"] = (sb(n, [P, DB, SEQ], F32R, later, "right") for n in ("flat_hi", "flat_lo"))
                for name, dt in (("top1", F32), ("take1", I32), ("wt1", F32), ("kept1", F32)):
                    T[name] = sb(name, [P, TILES, TOP1], dt, later, "right")
                middle(nc, A, T)
            experts(nc, A, T)
            finish(nc, A, T, out)


def attention(nc, A, T):
    c = ExitStack()
    with c:
        def sb(name, shape, dt=F32):
            return c.enter_context(nc.sbuf_tensor(name, shape, dt))

        def sem(name):
            return c.enter_context(nc.semaphore(name))

        x_sb, bank = T["x_sb"], T["bank"]
        ident, identb, onesb, before = T["ident"], T["identb"], T["onesb"], T["before"]
        gates, iota_e, base0, rowid = T["gates"], T["iota_e"], T["base0"], T["rowid"]
        w01, wo0, s_w0, s_zero1 = T["w01"], T["wo0"], T["s_w0"], T["s_zero1"]

        ctx_sb, zeros, chosen = T["ctx_sb"], T["zeros"], T["chosen"]
        k_sb = sb("k_sb", [P, 2, D])
        q_sb = sb("q_sb", [P, 2, D])
        kb = sb("kb", [P, 2, D], BF16)
        qb = sb("qb", [P, 2, D], BF16)
        vT = sb("vT", [P, 2, 4, 3, HEAD])
        negmax = sb("negmax", [P, 2, 8], BF16)
        probs = sb("probs", [P, 2, 2, D])
        attn = sb("attn", [P, D])
        xn = sb("xn", [P, 2, D])
        xnT = sb("xnT", [P, DB, P])
        bn = sb("bn", [P, 2, 6])
        mv = sb("mv", [P, 2, 2])
        rstd = sb("rstd", [P, 2])
        half, ve, nt = sb("half", [P, 2]), sb("ve", [P, 2]), sb("nt", [P, 2])
        ln1 = sb("ln1", [P, 2, 2])
        ln2 = sb("ln2", [P, 2, 2])
        logits = sb("logits", [P, E0])
        m8 = sb("m8", [P, 8])
        i8 = sb("i8", [P, 8], U32)
        idxf = sb("idxf", [P, 2])
        onehot = sb("onehot", [P, 2, E0])
        mask = sb("mask", [P, 2, E0], BF16)
        rows = sb("rows", [P, E0])
        junk = sb("junk", [P, 2, E0])
        slotf = sb("slotf", [P, 2])
        wg = sb("wg", [P, DB, E0])
        graw = sb("graw", [P, 4])
        ccol, ucol, ones = T["ccol"], T["ucol"], T["ones"]
        flip = xnT[:, 0, :]
        decay = sb("decay", [1, 4])
        kdec = sb("kdec", [1, 1])
        invt = sb("invt", [1, 1])
        crow = attn[0:1, :]
        wsel = sb("wsel", [P, B, TPB, B])
        urow = probs[0:B, 0, 0, :]

        s_xA, s_xB, s_cA, s_cB, s_small = (sem(n) for n in (
            "xA_loaded", "xB_loaded", "ctxA_loaded", "ctxB_loaded", "small_loaded"))
        consts_ready, zeros_ready, gates_ready = sem("consts_ready"), sem("zeros_ready"), sem("gates_ready")
        pm_full, pm_read = sem("pm_full"), sem("pm_read")
        k_ready, qkb_ready, q_ready = sem("k_ready"), sem("qkb_ready"), sem("q_ready")
        ln1_ready, ln2_ready, xn_ready = sem("ln1_ready"), sem("ln2_ready"), sem("xn_ready")
        vT_full, vT_ready = sem("vT_full"), sem("vT_ready")
        s_full, p_ready, p_used, qk_done = sem("s_full"), sem("p_ready"), sem("p_used"), sem("qk_done")
        sums_ready, po_read, x1_ready = sem("sums_ready"), sem("po_read"), sem("x1_ready")
        xnT_full, xnT_ready = sem("xnT_full"), sem("xnT_ready")
        lg_full, mask_ready, pos_full, pos_read = sem("lg_full"), sem("mask_ready"), sem("pos_full"), sem("pos_read")
        slot_ready = sem("slot_ready")
        scattered = [sem("scattered_even"), sem("scattered_odd")]
        dummy_zeroed = sem("dummy_zeroed")

        pS, pO, pM, pT = bank[0:2], bank[2:6], bank[6], bank[7]
        x_v = A["x"].rearrange("b (t p) d -> p (b t) d", p=P)
        c_v = A["ctx_2048"].rearrange("b (t p) d -> p (b t) d", p=P)
        NA = 3
        SMALL = 16 * 4
        crow_ready, col_full, col_ready = sem("crow_ready"), sem("col_full"), sem("col_ready")
        flip_full, wsel_ready = sem("flip_full"), sem("wsel_ready")
        u_full, urow_ready, uT_full = sem("u_full"), sem("urow_ready"), sem("uT_full")

        block = c.enter_context(nc.Block())

        @block.sync
        def _(sp):
            sp.dma_start(x_sb[:, 0:NA, :], x_v[:, 0:NA, :]).then_inc(s_xA, 16)
            sp.dma_start(ctx_sb[:, 0:NA, :], c_v[:, 0:NA, :]).then_inc(s_cA, 16)
            sp.dma_start(decay[0:1, 0:1], A["L1_xattn_decay"]).then_inc(s_small, 16)
            sp.dma_start(graw[:, 0:2], A["g_xattn"].partition_broadcast(P)).then_inc(s_small, 16)
            sp.dma_start(graw[:, 2:4], A["g_ffn"].partition_broadcast(P)).then_inc(s_small, 16)
            sp.dma_start(wg[:], A["L0_ffn_w_gate"].rearrange("(b p) e -> p b e", p=P)).then_inc(s_small, 16)
            sp.dma_start(x_sb[:, NA:, :], x_v[:, NA:, :]).then_inc(s_xB, 16)
            sp.dma_start(ctx_sb[:, NA:, :], c_v[:, NA:, :]).then_inc(s_cB, 16)
            w01_v = w01[:].rearrange("p (e b) m -> p e b m", e=E0)
            for name, at in (("L0_ffn_wi_0", 0), ("L0_ffn_wi_1", M0)):
                for e in range(E0):
                    sp.dma_start(w01_v[:, e, :, at:at + M0],
                                 A[name][e].rearrange("(b p) m -> p b m", p=P)).then_inc(s_w0, 16)
            sp.dma_start(wo0[:].rearrange("p (e b) d -> p e b d", e=E0),
                         A["L0_ffn_wo"].rearrange("e (b p) d -> p e b d", p=P)).then_inc(s_w0, 16)
            sp.wait_ge(zeros_ready, 1)
            reps = 8
            t1 = T["tab1"].rearrange("(n r p) d -> n p r d", p=P, r=reps)
            for n in range(E1 * CAP1 // (reps * P)):
                sp.dma_start(t1[n], zeros[:].unsqueeze(1).broadcast_to([P, reps, D])).then_inc(s_zero1, 16)
            sp.dma_start(T["tab0"][DUMMY_ROW:, :].rearrange("(r p) d -> p r d", p=P),
                         zeros[:].unsqueeze(1).broadcast_to([P, E0, D])).then_inc(dummy_zeroed, 16)
            sp.wait_ge(dummy_zeroed, 16)

        @block.gpsimd
        def _(pool):
            nc.gpsimd.memset(ident[:], 0.0)
            nc.gpsimd.memset(onesb[:], 1.0)
            nc.gpsimd.memset(zeros[:], 0.0)
            nc.gpsimd.memset(vT[:, :, :, 1, :], 1.0)
            nc.gpsimd.memset(chosen[:], 0.0)
            nc.gpsimd.memset(flip, 0.0)
            nc.gpsimd.memset(ones[:], 1.0)
            nc.gpsimd.memset(invt[:], 1.0 / SEQ)
            nc.gpsimd.memset(wsel[:], 0.0)
            nc.gpsimd.iota(iota_e[:], [[1, E1]], base=0, channel_multiplier=0, allow_small_or_imprecise_dtypes=True)
            nc.gpsimd.iota(base0[:], [[E0_STRIDE, E0]], base=0, channel_multiplier=0,
                           allow_small_or_imprecise_dtypes=True)
            nc.gpsimd.iota(T["base1"][:], [[CAP1, E1]], base=0, channel_multiplier=0,
                           allow_small_or_imprecise_dtypes=True)
            nc.gpsimd.iota(rowid[:], [[0, 1]], base=0, channel_multiplier=1, allow_small_or_imprecise_dtypes=True)
            pool.drain()
            nc.gpsimd.affine_select(ident[:], ident[:], [[-1, P]], ALU.not_equal, 1.0, base=0, channel_multiplier=1)
            nc.gpsimd.affine_select(flip, flip, [[1, P]], ALU.not_equal, 1.0, base=1 - P, channel_multiplier=1)
            nc.gpsimd.affine_select(before[:], onesb[:], [[1, P]], ALU.is_ge, 0.0, base=-1, channel_multiplier=-1)
            pool.drain()
            nc.gpsimd.tensor_copy(identb[:], ident[:])
            pool.drain()
            nc.gpsimd.engine_nop().then_inc(consts_ready, 1)
            nc.gpsimd.engine_nop().then_inc(zeros_ready, 1)
            for i in range(-2, TILES + 3):
                if valid(i + 1):
                    pool.wait_ge(s_cA if i + 1 < NA else s_cB, 16)
                    need(pool, qk_done, i)
                    nc.gpsimd.tensor_copy(k_sb[:, (i + 1) % 2, :], ctx_sb[:, i + 1, :]).then_inc(k_ready, 1)
                if valid(i - 1):
                    pool.wait_ge(po_read, i)
                    nc.gpsimd.tensor_tensor(x_sb[:, i - 1, :], x_sb[:, i - 1, :], attn[:],
                                            ALU.add).then_inc(x1_ready, 1)
                if valid(i + 2):
                    s = i % 2
                    need(pool, pm_full, 8 * (i + 1))
                    pool.wait_ge(s_cA if i + 2 < NA else s_cB, 16)
                    nc.gpsimd.tensor_copy(kb[:, s, :], ctx_sb[:, i + 2, :])
                    pool.wait_ge(ln1_ready, i + 3)
                    nc.gpsimd.tensor_scalar(qb[:, s, :], x_sb[:, i + 2, :], ln1[:, s, 0:1], ln1[:, s, 1:2],
                                            ALU.mult, ALU.add).then_inc(qkb_ready, 1)
                if valid(i - 3):
                    pool.wait_ge(slot_ready, i - 2)
                    for k in range(2):
                        nc.gpsimd.indirect_dma_start(
                            T["tab0"], bass.IndirectOffsetOnAxis(T["slot0"][:, i - 3, k:k + 1], 0),
                            xn[:, (i - 3) % 2, :], None).then_inc(scattered[(i - 3) % 2], 16)
            for s in range(2):
                pool.wait_ge(scattered[s], 16 * TILES)

        @block.tensor
        def _(pe):
            pe.wait_ge(consts_ready, 1)
            pe.wait_ge(s_small, SMALL)
            pe.wait_ge(crow_ready, 1)
            for j in range(TPB):
                last = nc.tensor.matmul(pM[:, j:j + 1], crow[0:1, j * P:j * P + P], ones[0:1, 0:1], start=True, stop=True)
            last.then_inc(col_full, 1)
            pe.wait_ge(col_ready, 1)
            nc.tensor.matmul(pM[:, 0:TPB], flip, ccol[:, 0, :], start=True, stop=True).then_inc(flip_full, 1)
            pe.wait_ge(wsel_ready, 1)

            def weighted_context():
                for t in range(TILES):
                    last = nc.tensor.matmul(pM[0:B, :], wsel[:, t // TPB, t % TPB, :], ctx_sb[:, t, :],
                                            start=(t == 0), stop=(t == TILES - 1))
                last.then_inc(u_full, 1)

            def context_columns():
                pe.wait_ge(urow_ready, 1)
                for n in range(DB):
                    last = nc.tensor.transpose(pM[:, n * B:n * B + B], urow[:, n * P:n * P + P], ident[0:B, 0:B])
                last.then_inc(uT_full, 1)

            def scores(i, s, sb_):
                for h in range(2):
                    need(pe, p_ready, i * 8 + (sb_ * 2 + h - 1))
                    kh = slice(HEAD * h, HEAD * h + HEAD)
                    last = nc.tensor.matmul(pS[h][:], k_sb[kh, s, sb_ * P:sb_ * P + P], q_sb[kh, s, :],
                                            start=True, stop=False)
                if sb_ == 3:
                    last.then_inc(qk_done, 1)
                for h in range(2):
                    for t in range(4):
                        m = h * 4 + t
                        last = nc.tensor.matmul(pS[h][:, t * P:t * P + P],
                                                negmax[:, s, m:m + 1].broadcast_to([P, P]), identb[:],
                                                start=False, stop=(t == 3))
                    last.then_inc(s_full, 1)

            def values(k, s, sb_):
                for h in range(2):
                    need(pe, p_ready, k * 8 + (sb_ * 2 + h + 1))
                    nc.tensor.matmul(pO[s * 2 + h][:], vT[:, s, sb_, h:h + 2, :].rearrange("p a c -> p (a c)"),
                                     probs[:, sb_ % 2, h, :], start=(sb_ == 0), stop=(sb_ == 3)).then_inc(p_used, 1)

            def rough(k, s, m):
                h, t = m // 4, m % 4
                need(pe, pm_read, k * 8 + m)
                hp = slice(HEAD * h, HEAD * h + HEAD)
                nc.tensor.matmul(pM[:], qb[hp, s, t * P:t * P + P], kb[hp, s, :],
                                 start=True, stop=True).then_inc(pm_full, 1)

            def step(i, u, odd):
                s, o = odd, 1 - odd
                if valid(i):
                    need(pe, q_ready, i + 1)
                    need(pe, k_ready, i + 1)
                    need(pe, pm_read, i * 8 + 8)
                for b in range(4):
                    if valid(i):
                        scores(i, s, b)
                    if valid(i + 1):
                        if b == 0:
                            need(pe, qkb_ready, i + 2)
                        rough(i + 1, o, 2 * b)
                    if b == 0 and valid(i - 1):
                        values(i - 1, o, 3)
                    if b > 0 and valid(i):
                        if b == 1:
                            need(pe, po_read, i - 1)
                            need(pe, vT_ready, i + 1)
                        values(i, s, b - 1)
                    if valid(i + 1):
                        rough(i + 1, o, 2 * b + 1)
                    if isinstance(i, int) and b == 1:
                        if i == TILES:
                            weighted_context()
                        if i == TILES + 1:
                            context_columns()
                    if b == 0 and valid(i - 2):
                        need(pe, pos_read, i - 2)
                        need(pe, vT_ready, seen(i))
                        need(pe, xn_ready, i - 1)
                        for t in range(DB):
                            last = nc.tensor.transpose(pT[:, t * P:t * P + P], xn[:, s, t * P:t * P + P], ident[:])
                        last.then_inc(xnT_full, 1)
                    if b == 1 and valid(i + 1):
                        need(pe, k_ready, i + 2)
                        if valid(i - 2):
                            need(pe, xnT_ready, i - 1)
                        else:
                            need(pe, vT_ready, i + 1)
                        for t in range(4):
                            last = nc.tensor.transpose(pT[:, t * P:t * P + P], k_sb[:, o, t * P:t * P + P], ident[:])
                        last.then_inc(vT_full, 1)
                    if b == 2 and valid(i - 2):
                        need(pe, vT_ready, seen(i + 1))
                        need(pe, xnT_ready, i - 1)
                        for d in range(DB):
                            last = nc.tensor.matmul(pT[:, 0:E0], xnT[:, d, :], wg[:, d, :],
                                                    start=(d == 0), stop=(d == DB - 1))
                        last.then_inc(lg_full, 1)
                    if b == 3 and valid(i - 2):
                        need(pe, mask_ready, i - 1)
                        nc.tensor.matmul(pT[:, 0:E0], before[:], mask[:, s, :], start=True, stop=False)
                        nc.tensor.matmul(pT[:, 0:E0], onesb[:], chosen[:, s, :], start=False,
                                         stop=True).then_inc(pos_full, 1)

            steps(pe, step, TILES, 2, 2, 2)

        @block.scalar
        def _(act):
            act.wait_ge(s_small, SMALL)
            nc.scalar.activation(decay[0:1, 1:2], decay[0:1, 0:1], ACT.Exp, scale=-1.0)
            nc.scalar.activation(gates[:], graw[:], ACT.Tanh).then_inc(gates_ready, 1)

            def step(i, u, odd):
                s, o = odd, 1 - odd
                for b in range(4):
                    if valid(i):
                        for h in range(2):
                            n = b * 2 + h
                            need(act, p_used, i * 8 + (n - 3))
                            need(act, s_full, i * 8 + (n + 1))
                            nc.scalar.activation(probs[:, b % 2, h, :], pS[h][:], ACT.Exp,
                                                 scale=1.0 / HEAD).then_inc(p_ready, 1)
                    if b == 0 and valid(i - 1):
                        need(act, x1_ready, i - 1)
                        need(act, p_used, i * 8)
                        nc.scalar.copy(attn[0:HEAD, :], pO[o * 2][HEAD:P, :])
                        nc.scalar.copy(attn[HEAD:P, :], pO[o * 2 + 1][0:HEAD, :]).then_inc(sums_ready, 1)
                    if b == 0 and valid(i - 2):
                        need(act, xnT_full, i - 1)
                        nc.scalar.copy(xnT[:].rearrange("p d t -> p (d t)"), pT[:]).then_inc(xnT_ready, 1)
                    if b == 2 and valid(i + 1):
                        need(act, p_used, i * 8)
                        need(act, vT_full, i + 2)
                        pv = pT[:].rearrange("p (t a c) -> p t a c", t=4, a=2)
                        nc.scalar.copy(vT[:, o, :, 0, :], pv[:, :, 0, :])
                        nc.scalar.copy(vT[:, o, :, 2, :], pv[:, :, 1, :]).then_inc(vT_ready, 1)
                    if b == 3 and valid(i + 1):
                        need(act, ln1_ready, i + 2, alone=1)
                        need(act, qk_done, i)
                        nc.scalar.activation(q_sb[:, o, :], row(x_sb, i + 1), ACT.Identity,
                                             scale=ln1[:, o, 0:1], bias=ln1[:, o, 1:2]).then_inc(q_ready, 1)
                    if b == 3 and valid(i - 1):
                        half_ = u + (odd - 1) // 2
                        need(act, ln2_ready, i, alone=1)
                        need(act, scattered[o], half_ * 32)
                        nc.scalar.activation(xn[:, o, :], row(x_sb, i - 1), ACT.Identity,
                                             scale=ln2[:, o, 0:1], bias=ln2[:, o, 1:2]).then_inc(xn_ready, 1)
                    if isinstance(i, int) and i == TILES and b == 3:
                        act.wait_ge(u_full, 1)
                        nc.scalar.copy(urow, pM[0:B, :]).then_inc(urow_ready, 1)
                    if isinstance(i, int) and i == TILES + 1 and b == 3:
                        act.wait_ge(uT_full, 1)
                        nc.scalar.copy(ucol[:].rearrange("p n b -> p (n b)"), pM[:, 0:DB * B])

            steps(act, step, TILES, 2, 2, 2)

        @block.vector
        def _(dve):
            dve.wait_ge(consts_ready, 1)
            dve.wait_ge(gates_ready, 1)
            nc.vector.tensor_scalar(decay[0:1, 2:3], decay[0:1, 1:2], 1.0, None, ALU.add)
            dve.drain()
            nc.vector.reciprocal(kdec[:], decay[0:1, 2:3])
            dve.drain()
            nc.vector.tensor_tensor_scan(crow, kdec[:].broadcast_to([1, SEQ]), invt[:].broadcast_to([1, SEQ]),
                                         0.0, ALU.mult, ALU.add).then_inc(crow_ready, 1)
            dve.wait_ge(col_full, 1)
            nc.vector.tensor_copy(ccol[:, 0, :], pM[:, 0:TPB]).then_inc(col_ready, 1)
            dve.wait_ge(flip_full, 1)
            for j in range(TPB):
                nc.vector.tensor_copy(ccol[:, 1, j:j + 1], pM[:, TPB - 1 - j:TPB - j])
            dve.drain()
            for b in range(B):
                last = nc.vector.tensor_copy(wsel[:, b, :, b], ccol[:, 1, :])
            last.then_inc(wsel_ready, 1)

            def rough_max(k, s, m):
                need(dve, pm_full, k * 8 + (m + 1))
                if m == 0:
                    need(dve, s_full, k * 8 - 8)
                nc.vector.tensor_reduce(negmax[:, s, m:m + 1], pM[:], AX.X, ALU.max,
                                        negate=True).then_inc(pm_read, 1)

            def choose(k, s):
                need(dve, lg_full, k + 1)
                nc.vector.tensor_copy(logits[:], pT[:, 0:E0])
                dve.drain()
                nc.vector.max(m8[:], logits[:])
                dve.drain()
                nc.vector.max_index(i8[:], m8[:], logits[:])
                nc.vector.tensor_copy(row(T["top0"], k), m8[:, 0:2])
                dve.drain()
                nc.vector.tensor_copy(idxf[:], i8[:, 0:2])
                dve.drain()
                for c_ in range(2):
                    nc.vector.tensor_scalar(onehot[:, c_, :], iota_e[:, 0:E0], idxf[:, c_:c_ + 1], None, ALU.is_equal)
                dve.drain()
                nc.vector.tensor_tensor(mask[:, s, :], onehot[:, 0, :], onehot[:, 1, :],
                                        ALU.add).then_inc(mask_ready, 1)

            def place(k, s):
                need(dve, pos_full, k + 1)
                nc.vector.tensor_tensor(rows[:], pT[:, 0:E0], base0[:], ALU.add).then_inc(pos_read, 1)
                nc.vector.tensor_tensor(chosen[:, 1 - s, :], chosen[:, s, :], mask[:, s, :], ALU.add)
                dve.drain()
                for c_ in range(2):
                    nc.vector.tensor_tensor_reduce(out=junk[:, c_, :], in0=onehot[:, c_, :], in1=rows[:], scale=1.0,
                                                   scalar=0.0, op0=ALU.mult, op1=ALU.add,
                                                   accum_out=slotf[:, c_:c_ + 1])
                dve.drain()
                nc.vector.tensor_copy(row(T["slot0"], k), slotf[:]).then_inc(slot_ready, 1)

            def step(i, u, odd):
                s, o = odd, 1 - odd
                if isinstance(i, int) and i == NA - 2:
                    dve.wait_ge(s_xB, 16)
                cols = [n for n, k in enumerate((i - 1, i + 2)) if valid(k)]
                for m in range(8):
                    if valid(i + 1):
                        rough_max(i + 1, o, m)
                    if m == 0 and valid(i - 3):
                        place(i - 3, o)
                    if m == 1 and valid(i - 1):
                        dve.drain()
                        need(dve, sums_ready, i)
                        nc.vector.reciprocal(attn[:], attn[:])
                    if m == 2 and valid(i - 1):
                        dve.drain()
                        for h in range(2):
                            hp = slice(HEAD * h, HEAD * h + HEAD)
                            last = nc.vector.scalar_tensor_tensor(attn[hp, :], pO[o * 2 + h][hp, :], gates[hp, 0:1],
                                                                  attn[hp, :], ALU.mult, ALU.mult)
                        last.then_inc(po_read, 1)
                    if m == 3 and cols:
                        dve.drain()
                        if valid(i + 2):
                            if isinstance(i, int):
                                dve.wait_ge(s_xA, 16)
                            nc.vector.bn_stats(bn[:, 1, :], row(x_sb, i + 2))
                        if valid(i - 1):
                            need(dve, x1_ready, i, alone=1)
                            nc.vector.bn_stats(bn[:, 0, :], row(x_sb, i - 1))
                        dve.drain()
                        for n in cols:
                            nc.vector.bn_aggr(mv[:, n, :], bn[:, n, :])
                    if m == 4 and cols:
                        a, z = cols[0], cols[-1] + 1
                        dve.drain()
                        rsqrt(nc, dve, rstd[:, a:z], mv[:, a:z, 1], half[:, a:z], (ve[:, a:z], nt[:, a:z]))
                        if valid(i + 2):
                            need(dve, q_ready, i + 1)
                            need(dve, qkb_ready, i + 1)
                            nc.vector.tensor_copy(ln1[:, s, 0:1], rstd[:, 1:2])
                            nc.vector.scalar_tensor_tensor(ln1[:, s, 1:2], mv[:, 1, 0:1], -1.0, rstd[:, 1:2],
                                                           ALU.mult, ALU.mult).then_inc(ln1_ready, 1)
                        if valid(i - 1):
                            need(dve, xn_ready, i - 2)
                            nc.vector.tensor_copy(ln2[:, o, 0:1], rstd[:, 0:1])
                            nc.vector.scalar_tensor_tensor(ln2[:, o, 1:2], mv[:, 0, 0:1], -1.0, rstd[:, 0:1],
                                                           ALU.mult, ALU.mult).then_inc(ln2_ready, 1)
                    if m == 6 and valid(i - 2):
                        choose(i - 2, s)

            steps(dve, step, TILES, 2, 2, 3)


def summary_and_tiles(nc, A, T):
    c = ExitStack()
    with c:
        def sb(name, shape, dt=F32):
            return c.enter_context(nc.sbuf_tensor(name, shape, dt))

        def sem(name):
            return c.enter_context(nc.semaphore(name))

        bank, ident, onesb = T["bank"], T["ident"], T["onesb"]
        pS, pO, pM, pT = bank[0:2], bank[2:6], bank[6], bank[7]
        base0, rowid, chosen, zeros = T["base0"], T["rowid"], T["chosen"], T["zeros"]
        ccol, ucol, ones = T["ccol"], T["ucol"], T["ones"]
        iota_i = sb("iota_i", [1, L0_TILES])
        cnt = sb("cnt", [P, E0])
        padf = sb("padf", [P, E0])
        padrow = sb("padrow", [P, E0], I32)
        ntf = sb("ntf", [P, E0])
        nti = sb("nti", [P, E0], I32)
        cum = sb("cum", [1, E0])
        texp = sb("texp", [1, L0_TILES])
        tskip = sb("tskip", [1, L0_TILES])
        trow = sb("trow", [1, L0_TILES])
        win = sb("win", [P, DB, D])
        wout = sb("wout", [P, DB, D])
        winT = sb("winT", [P, DB, D])
        woutT = sb("woutT", [P, DB, D])
        bin_col = sb("bin_col", [P, DB])
        bout_col = sb("bout_col", [P, DB])
        csum = sb("csum", [P, 1])
        mstate = sb("mstate", [P, DB, B])
        scol = sb("scol", [P, DB, B])
        usum = sb("usum", [P, 4 * TILES])
        big = sb("big", [P, L0_TILES * E0])
        past = big[0:1, 0:L0_TILES * E0].rearrange("p (t e) -> p t e", e=E0)
        slotf = usum[:, 2 * TILES:4 * TILES]

        s_sw = sem("summary_weights_loaded")
        consts_ready = sem("summary_consts_ready")
        cnt_full, pad_ready, padded = sem("cnt_full"), sem("pad_ready"), sem("padded")
        sum_full, m_full, m_ready = sem("weights_sum_full"), sem("m_full"), sem("m_ready")
        s_full, scol_ready, wT_full, wT_ready = sem("s_full"), sem("scol_ready"), sem("wT_full"), sem("wT_ready")
        rows_full = sem("summary_rows_full")

        block = c.enter_context(nc.Block())

        @block.sync
        def _(sp):
            sp.dma_start(win[:], A["L1_xattn_W_in"].rearrange("(b p) d -> p b d", p=P)).then_inc(s_sw, 16)
            sp.dma_start(wout[:], A["L1_xattn_W_out"].rearrange("(b p) d -> p b d", p=P)).then_inc(s_sw, 16)
            sp.dma_start(bin_col[:], A["L1_xattn_b_in"].rearrange("(b p) -> p b", p=P),
                         allow_slow_non_contiguous=True).then_inc(s_sw, 16)
            sp.dma_start(bout_col[:], A["L1_xattn_b_out"].rearrange("(b p) -> p b", p=P),
                         allow_slow_non_contiguous=True).then_inc(s_sw, 16)

        @block.gpsimd
        def _(pool):
            nc.gpsimd.iota(iota_i[:], [[1, L0_TILES]], base=0, channel_multiplier=0,
                           allow_small_or_imprecise_dtypes=True)
            pool.drain()
            nc.gpsimd.engine_nop().then_inc(consts_ready, 1)
            pool.wait_ge(pad_ready, 1)
            for e in range(E0):
                nc.gpsimd.indirect_dma_start(T["tab0"], bass.IndirectOffsetOnAxis(padrow[:, e:e + 1], 0),
                                             zeros[:, 0:D], None).then_inc(padded, 16)
            pool.wait_ge(padded, 16 * E0)

        @block.tensor
        def _(pe):
            nc.tensor.matmul(pT[:, 0:E0], onesb[:], chosen[:, TILES % 2, :], start=True, stop=True).then_inc(cnt_full, 1)

            for j in range(TPB):
                last = nc.tensor.matmul(pS[0][:, 0:1], ccol[:, 1, j:j + 1].broadcast_to([P, P]), ones[:, 0:1],
                                        start=(j == 0), stop=(j == TPB - 1))
            last.then_inc(sum_full, 1)
            pe.wait_ge(s_sw, 64)
            pe.wait_ge(pad_ready, 1)
            for n in range(2 * DB):
                w, k = (win, n) if n < DB else (wout, n - DB)
                if n >= 2:
                    pe.wait_ge(wT_ready, n - 1)
                for q in range(DB):
                    last = nc.tensor.transpose((pM, pT)[n % 2][:, q * P:q * P + P], w[:, q, k * P:k * P + P], ident[:])
                last.then_inc(wT_full, 1)
            pe.wait_ge(wT_ready, 2 * DB)
            for wT, x, ready, full, bank_ in ((winT, ucol, None, m_full, pO[0]), (woutT, mstate, m_ready, s_full, pO[1])):
                if ready:
                    pe.wait_ge(ready, 1)
                for q in range(DB):
                    for n in range(DB):
                        last = nc.tensor.matmul(bank_[:, q * B:q * B + B], wT[:, n, q * P:q * P + P], x[:, n, :],
                                                start=(n == 0), stop=(n == DB - 1))
                last.then_inc(full, 1)
            pe.wait_ge(scol_ready, 1)
            for b in range(B):
                for q in range(DB):
                    last = nc.tensor.matmul(pO[b][:, q * P:q * P + P], scol[:, q, b:b + 1].broadcast_to([P, P]), ident[:],
                                            start=True, stop=True)
                last.then_inc(rows_full, 1)

        @block.scalar
        def _(act):
            for n in range(2 * DB):
                wT, k = (winT, n) if n < DB else (woutT, n - DB)
                act.wait_ge(wT_full, n + 1)
                nc.scalar.copy(wT[:, k, :], (pM, pT)[n % 2][:]).then_inc(wT_ready, 1)
            for b in range(B):
                act.wait_ge(rows_full, b + 1)
                nc.scalar.copy(T["summary"][:, b, :], pO[b][:])

        @block.vector
        def _(dve):
            dve.wait_ge(consts_ready, 1)
            dve.wait_ge(cnt_full, 1)
            nc.vector.tensor_copy(cnt[:], pT[:, 0:E0])
            dve.drain()
            nc.vector.scalar_tensor_tensor(padf[:], cnt[:], rowid[:, 0:1], base0[:], ALU.add, ALU.add)
            nc.vector.tensor_scalar(ntf[:], cnt[:], float(P - 1), None, ALU.add)
            dve.drain()
            nc.vector.tensor_copy(padrow[:], padf[:]).then_inc(pad_ready, 1)

            nc.vector.tensor_copy(nti[:], ntf[:])
            dve.drain()
            nc.vector.tensor_scalar(nti[:], nti[:], 7, None, ALU.logical_shift_right)
            dve.drain()
            nc.vector.tensor_copy(ntf[:], nti[:])
            dve.drain()
            nc.vector.tensor_tensor_scan(cum[:], ones[0:1, 0:E0], ntf[0:1, :], 0.0, ALU.mult, ALU.add)
            dve.drain()
            nc.vector.tensor_tensor(past, iota_i[:].unsqueeze(2).broadcast_to([1, L0_TILES, E0]),
                                    cum[:].unsqueeze(1).broadcast_to([1, L0_TILES, E0]), ALU.is_ge)
            dve.drain()
            nc.vector.tensor_reduce(texp[:], past, AX.X, ALU.add)
            dve.drain()
            nc.vector.tensor_tensor(past, past, ntf[0:1, :].unsqueeze(1).broadcast_to([1, L0_TILES, E0]), ALU.mult)
            dve.drain()
            nc.vector.tensor_reduce(tskip[:], past, AX.X, ALU.add)
            nc.vector.tensor_scalar(trow[:], texp[:], float(E0_STRIDE), None, ALU.mult)
            dve.drain()
            nc.vector.tensor_tensor(tskip[:], iota_i[:], tskip[:], ALU.subtract)
            dve.drain()
            nc.vector.scalar_tensor_tensor(trow[:], tskip[:], float(P), trow[:], ALU.mult, ALU.add)
            dve.drain()
            nc.vector.tensor_copy(T["tinfo"][0:1, :, 0], trow[:])
            nc.vector.tensor_scalar(T["tinfo"][0:1, :, 1], texp[:], float(E0 - 1), None, ALU.min)

            ge = big[:, 0:2 * TILES * (E0 - 1)].rearrange("p (t e) -> p t e", e=E0 - 1)
            shape = [P, 2 * TILES, E0 - 1]
            nc.vector.tensor_copy(slotf, T["slot0"][:].rearrange("p t k -> p (t k)"))
            nc.vector.tensor_scalar(ntf[:], ntf[:], float(P), float(-E0_STRIDE), ALU.mult, ALU.add)
            dve.drain()
            nc.vector.tensor_tensor(ge, slotf.unsqueeze(2).broadcast_to(shape),
                                    base0[:, 1:E0].unsqueeze(1).broadcast_to(shape), ALU.is_ge)
            dve.drain()
            nc.vector.tensor_tensor(ge, ge, ntf[:, 0:E0 - 1].unsqueeze(1).broadcast_to(shape), ALU.mult)
            dve.drain()
            nc.vector.tensor_reduce(usum[:, 0:2 * TILES], ge, AX.X, ALU.add)
            dve.drain()
            nc.vector.tensor_tensor(T["take0"][:].rearrange("p t k -> p (t k)"), slotf, usum[:, 0:2 * TILES], ALU.add)
            dve.drain()

            dve.wait_ge(sum_full, 1)
            nc.vector.tensor_copy(csum[:], pS[0][:, 0:1])
            dve.drain()
            dve.wait_ge(s_sw, 64)
            nc.vector.tensor_scalar(bin_col[:], bin_col[:], csum[:, 0:1], None, ALU.mult)
            dve.drain()
            for full, bank_, bias, x, ready in ((m_full, pO[0], bin_col, mstate, m_ready),
                                                (s_full, pO[1], bout_col, scol, scol_ready)):
                dve.wait_ge(full, 1)
                nc.vector.tensor_tensor(x[:], bank_[:, 0:DB * B].rearrange("p (n b) -> p n b", b=B),
                                        bias[:].unsqueeze(2).broadcast_to([P, DB, B]), ALU.add).then_inc(ready, 1)


def mixture0(nc, A, T):
    c = ExitStack()
    with c:
        def sb(name, shape, dt=F32):
            return c.enter_context(nc.sbuf_tensor(name, shape, dt))

        def sem(name):
            return c.enter_context(nc.semaphore(name))

        bank, ident, tinfo, w01, wo0 = T["bank"], T["ident"], T["tinfo"], T["w01"], T["wo0"]
        N, MB = L0_TILES, M0 // P
        RING = 4
        AHEAD = RING - 1
        xb = sb("m0_x", [P, RING, D])
        xT = sb("m0_xT", [P, 2, DB, P])
        act_g = sb("m0_silu", [P, M0])
        inter = sb("m0_inter", [P, 2, M0])
        interT = sb("m0_interT", [P, 2, MB, P])
        y = sb("m0_y", [P, 2, D])
        x_loaded = [sem(f"m0_x_loaded_{n}") for n in range(RING)]
        stored = [sem("m0_stored_even"), sem("m0_stored_odd")]
        xT_full, xT_ready, h_full, g_ready = sem("xT_full"), sem("xT_ready"), sem("h_full"), sem("g_ready")
        in_ready, inT_full, inT_ready = sem("in_ready"), sem("inT_full"), sem("inT_ready")
        y_full, y_ready = sem("y_full"), sem("y_ready")
        pX, pH, pI, pY = bank[0:2], bank[2:4], bank[4:6], bank[6:8]
        block = c.enter_context(nc.Block())

        @block.sync
        def _(sp):
            def first_row(i):
                at = tinfo[0:1, i, 0:1] if isinstance(i, int) else \
                    tinfo[0:1, bass.ds(i, 1), 0:1].rearrange("p o d -> p (o d)")
                return sp.value_load(at, min_val=0, max_val=TAB0_ROWS - P)

            def step(i, u, q):
                if valid(i + AHEAD, n=N):
                    slot = (q + AHEAD) % RING
                    need(sp, xT_full, i)
                    sp.dma_start(xb[:, slot, :],
                                 T["tab0"][bass.ds(first_row(i + AHEAD), P), :]).then_inc(x_loaded[slot], 16)
                if valid(i - 1, n=N):
                    need(sp, y_ready, i)
                    sp.dma_start(T["ytab0"][bass.ds((i - 1) * P, P), :],
                                 y[:, (q - 1) % 2, :]).then_inc(stored[(q - 1) % 2], 16)

            steps(sp, step, N, RING, AHEAD, 1)
            for s in range(2):
                sp.wait_ge(stored[s], 16 * N // 2)

        @block.tensor
        def _(pe):
            pe.wait_ge(T["s_w0"], 16 * (2 * E0 + 1))

            def step(i, u, q):
                s, o = q % 2, 1 - q % 2
                if valid(i - 1, n=N):
                    need(pe, in_ready, i)
                    need(pe, inT_ready, i - 2)
                    for m in range(MB):
                        last = nc.tensor.transpose(pI[o][:, m * P:m * P + P], inter[:, o, m * P:m * P + P], ident[:])
                    last.then_inc(inT_full, 1)
                if valid(i, n=N):
                    e = expert(pe, tinfo, i)
                    need(pe, xT_ready, i + 1)
                    need(pe, in_ready, i - 1)
                    for d in range(DB):
                        last = nc.tensor.matmul(pH[s][:], xT[:, s, d, :], row(w01, e * DB + d),
                                                start=(d == 0), stop=(d == DB - 1))
                    last.then_inc(h_full, 1)
                if valid(i + 1, n=N):
                    n = (q + 1) % RING
                    need(pe, x_loaded[n], (u + (q + 1) // RING) * 16 + 16)
                    need(pe, xT_ready, i)
                    for d in range(DB):
                        last = nc.tensor.transpose(pX[o][:, d * P:d * P + P], xb[:, n, d * P:d * P + P], ident[:])
                    last.then_inc(xT_full, 1)
                if valid(i - 1, n=N):
                    e = expert(pe, tinfo, i - 1)
                    need(pe, inT_ready, i)
                    need(pe, y_ready, i - 2)
                    for m in range(MB):
                        last = nc.tensor.matmul(pY[o][:], interT[:, o, m, :], row(wo0, e * MB + m),
                                                start=(m == 0), stop=(m == MB - 1))
                    last.then_inc(y_full, 1)

            steps(pe, step, N, RING, 1, 1)

        @block.scalar
        def _(act):
            act.wait_ge(xT_full, 1)
            stage = T["stage"][:].rearrange("p w s (b h) -> p w s b h", b=DB)
            for w, name in ((stage[:, 0], "L1_ffn_Sg"), (stage[:, 1], "L1_ffn_Su"), (T["w_sd"], "L1_ffn_Sd")):
                for s in range(NSH):
                    act.dma_start(w[:, s], A[name][s].rearrange("(b p) h -> p b h", p=P)).then_inc(T["s_ws"], 16)

            def step(i, u, q):
                s, o = q % 2, 1 - q % 2
                if valid(i, n=N):
                    need(act, h_full, i + 1)
                    need(act, in_ready, i)
                    nc.scalar.activation(act_g[:], pH[s][:, 0:M0], ACT.Silu).then_inc(g_ready, 1)
                if valid(i + 1, n=N):
                    need(act, xT_full, i + 2)
                    need(act, h_full, i)
                    nc.scalar.copy(xT[:, o].rearrange("p d t -> p (d t)"), pX[o][:]).then_inc(xT_ready, 1)
                if valid(i - 1, n=N):
                    need(act, y_full, i)
                    need(act, stored[o], (u * (RING // 2) + (q - 1) // 2) * 16)
                    nc.scalar.copy(y[:, o, :], pY[o][:]).then_inc(y_ready, 1)

            steps(act, step, N, RING, 1, 1)

        @block.vector
        def _(dve):
            def step(i, u, q):
                s, o = q % 2, 1 - q % 2
                if valid(i - 1, n=N):
                    need(dve, inT_full, i)
                    need(dve, y_full, i - 2)
                    nc.vector.tensor_copy(interT[:, o].rearrange("p m t -> p (m t)"),
                                          pI[o][:, 0:M0]).then_inc(inT_ready, 1)
                if valid(i, n=N):
                    need(dve, g_ready, i + 1)
                    need(dve, inT_full, i - 1)
                    nc.vector.tensor_tensor(inter[:, s, :], act_g[:], pH[s][:, M0:2 * M0],
                                            ALU.mult).then_inc(in_ready, 1)

            steps(dve, step, N, RING, 1, 1)


def expert(eng, tinfo, i):
    at = tinfo[0:1, i, 1:2] if isinstance(i, int) else tinfo[0:1, bass.ds(i, 1), 1:2].rearrange("p o d -> p (o d)")
    return eng.value_load(at, min_val=0, max_val=E0 - 1)


def middle(nc, A, T):
    c = ExitStack()
    with c:
        def sb(name, shape, dt=F32):
            return c.enter_context(nc.sbuf_tensor(name, shape, dt))

        def sem(name):
            return c.enter_context(nc.semaphore(name))

        x_sb, bank, ident, onesb, before = T["x_sb"], T["bank"], T["ident"], T["onesb"], T["before"]
        gates, iota_e, summary = T["gates"], T["iota_e"], T["summary"]
        flat_hi, flat_lo, w_hi, w_lo, stage = T["flat_hi"], T["flat_lo"], T["w_hi"], T["w_lo"], T["stage"]
        top0, take0, top1, take1, kept1 = T["top0"], T["take0"], T["top1"], T["take1"], T["kept1"]
        pX, pL, pC, pG, pU = bank[0:2], bank[2], bank[3], bank[4:6], bank[6:8]

        y0 = sb("y0", [P, TPB, 2, D])
        hidden = stage[:, 0].rearrange("p s (n t) -> p (s n) t", t=SEQ)
        z = stage[:, 1, 0, :].rearrange("p (j d) -> p j d", j=TPB)
        flat = stage[:, 1, 1, :].rearrange("p (j d) -> p j d", j=TPB)
        flatTt = sb("flatTt", [P, 2, DB, P])
        wr = sb("wr", [P, DB, E1])
        bias_r = sb("bias_r", [P, E1])
        gamma = sb("gamma", [P, D])
        beta = sb("beta", [P, D])
        wmix = sb("wmix", [P, TILES, 2])
        wtmp = sb("wtmp", [P, 3, TILES])
        bn = sb("bn1", [P, TPB, 6])
        mv = sb("mv1", [P, TPB, 2])
        rstd = sb("rstd1", [P, TPB])
        half, ve, nt = sb("half1", [P, TPB]), sb("ve1", [P, TPB]), sb("nt1", [P, TPB])
        lnz = sb("lnz", [P, TPB, 2])
        lnf = sb("lnf", [P, TPB, 2])
        logits = sb("logits1", [P, TPB, E1])
        m8 = sb("m81", [P, 8])
        i8 = sb("i81", [P, 8], U32)
        idxf = sb("idxf1", [P, TPB, TOP1])
        onehot = sb("onehot1", [P, TPB, TOP1, E1], BF16)
        pair = sb("pair1", [P, 2, E1])
        mask = sb("mask1", [P, TPB, E1], BF16)
        chosen = sb("chosen1", [P, 2, E1], BF16)
        junk = sb("junk1", [P, TOP1, E1])
        posf = sb("posf", [P, TOP1])
        drop = sb("drop", [P, TOP1])
        slotf = sb("slotf1", [P, TOP1])
        slot1 = sb("slot1", [P, TPB, TOP1], I32)
        shared = SharedExperts(nc, T, c, "a", hidden)
        hi_ready, lo_ready = sem("w_hi_ready"), sem("w_lo_ready")

        small_loaded = sem("mid_small_loaded")
        gathered = sem("y0_gathered")
        beta_ready, wexp_ready = sem("beta_ready"), sem("wexp_ready")
        x2_ready, lnz_ready, z_ready, y_ready, xb_ready = (sem(n) for n in (
            "x2_ready", "lnz_ready", "z_ready", "ysum_ready", "x_beta_ready"))
        x3_ready, lnf_ready, flat_ready = sem("x3_ready"), sem("lnf_ready"), sem("flat_ready")
        fT_full, fT_ready, fT_kept = sem("flatT_full"), sem("flatT_ready"), sem("flatT_kept")
        lg_full, lg_read, mask_ready, pos_full, pos_read = (sem(n) for n in (
            "lg1_full", "lg1_read", "mask1_ready", "pos1_full", "pos1_read"))
        slot_ready, scattered = sem("slot1_ready"), sem("flat_scattered")
        w_ready = sem("mid_zero_ready")
        groups_done = B - 1
        block = c.enter_context(nc.Block())

        def groups(eng, step):
            step(-1)
            with eng.Fori(0, groups_done) as g:
                step(g)
            step(B - 1)

        def prepared(g):
            return not isinstance(g, int) or g + 1 < B

        def routed(g):
            return not isinstance(g, int) or g >= 0

        def with_shared(g):
            return not isinstance(g, int)

        @block.sync
        def _(sp):
            sp.dma_start(gamma[:], A["L1_xattn_gamma"].partition_broadcast(P)).then_inc(small_loaded, 16)
            sp.dma_start(beta[:], A["L1_xattn_beta"].partition_broadcast(P)).then_inc(small_loaded, 16)
            sp.dma_start(wr[:], A["L1_ffn_Wr"].rearrange("(b p) e -> p b e", p=P)).then_inc(small_loaded, 16)
            sp.dma_start(bias_r[:], A["L1_ffn_router_bias"].partition_broadcast(P)).then_inc(small_loaded, 16)

        @block.gpsimd
        def _(pool):
            nc.gpsimd.memset(chosen[:], 0.0).then_inc(w_ready, 1)
            pool.wait_ge(T["s_zero1"], 16 * (E1 * CAP1 // (8 * P)))
            for g in range(-1, B):
                n = g + 1
                if n < B:
                    need(pool, x2_ready, TPB * n)
                    for j in range(TPB):
                        for k in range(2):
                            nc.gpsimd.indirect_dma_start(
                                y0[:, j, k, :], None, T["ytab0"],
                                bass.IndirectOffsetOnAxis(take0[:, n * TPB + j, k:k + 1], 0)).then_inc(gathered, 16)
                def dispatch(tiles):
                    for j in tiles:
                        pool.wait_ge(slot_ready, TPB * g + j + 1)
                        for k in range(TOP1):
                            nc.gpsimd.indirect_dma_start(
                                T["tab1"], bass.IndirectOffsetOnAxis(slot1[:, j, k:k + 1], 0), flat[:, j, :], None,
                                bounds_check=E1 * CAP1 - 1, oob_is_err=False).then_inc(scattered, 16)

                if g >= 0:
                    for j in range(TPB):
                        pool.wait_ge(fT_ready, TPB * g + j + 1)
                        cols = slice(j * P, j * P + P)
                        nc.gpsimd.tensor_tensor(flat_lo[:, :, cols], flatTt[:, j % 2], flat_hi[:, :, cols],
                                                ALU.subtract).then_inc(fT_kept, 1)
                    dispatch(range(TPB // 2))
                if n < B:
                    for j in range(TPB):
                        t = n * TPB + j
                        pool.wait_ge(z_ready, t + 1)
                        nc.gpsimd.tensor_tensor(z[:, j, :], z[:, j, :], summary[:, n, :], ALU.add).then_inc(y_ready, 1)
                        if t == 0:
                            pool.wait_ge(beta_ready, 1)
                        nc.gpsimd.tensor_tensor(x_sb[:, t, :], x_sb[:, t, :], beta[:], ALU.add).then_inc(xb_ready, 1)
                if g >= 0:
                    dispatch(range(TPB // 2, TPB))
            pool.wait_ge(scattered, 16 * TILES * TOP1)

        @block.tensor
        def _(pe):
            pe.wait_ge(small_loaded, 64)
            pe.wait_ge(lo_ready, 2 * NSH)
            pe.wait_ge(w_ready, 1)

            def route(g):
                for j in range(TPB):
                    need(pe, flat_ready, g * TPB + (j + 1))
                    if j >= 2:
                        need(pe, fT_ready, g * TPB + (j - 1))
                    for d in range(DB):
                        last = nc.tensor.transpose(pX[j % 2][:, d * P:d * P + P], flat[:, j, d * P:d * P + P], ident[:])
                    last.then_inc(fT_full, 1)
                    if j:
                        logit(g, j - 1)
                logit(g, TPB - 1)

            def logit(g, j):
                need(pe, fT_ready, g * TPB + (j + 1))
                if j:
                    need(pe, lg_read, g * TPB + j)
                for d in range(DB):
                    last = nc.tensor.matmul(pL[:, 0:E1], flatTt[:, j % 2, d, :], wr[:, d, :],
                                            start=(d == 0), stop=(d == DB - 1))
                last.then_inc(lg_full, 1)

            def positions(g, j):
                need(pe, mask_ready, g * TPB + (j + 1))
                if j:
                    need(pe, pos_read, g * TPB + j)
                nc.tensor.matmul(pC[:, 0:E1], before[:], mask[:, j, :], start=True, stop=False)
                nc.tensor.matmul(pC[:, 0:E1], onesb[:], chosen[:, j % 2, :], start=False, stop=True).then_inc(pos_full, 1)

            def step(g):
                if not routed(g):
                    return
                route(g)
                if with_shared(g):
                    need(pe, fT_kept, g * TPB + TPB)
                for n in range(SharedExperts.CHUNKS):
                    if with_shared(g):
                        shared.up(pe, g, n, pG, pU)
                    if n < TPB:
                        positions(g, n)
                if with_shared(g):
                    for j in range(TPB):
                        shared.down(pe, g, j, pX)
                    need(pe, shared.y_read, g * TPB + TPB)

            groups(pe, step)

        @block.scalar
        def _(act):
            act.wait_ge(w_ready, 1)
            act.wait_ge(wexp_ready, 1)
            nc.scalar.activation(wtmp[:, 1, :], wtmp[:, 0, :], ACT.Exp).then_inc(wexp_ready, 1)
            act.wait_ge(T["s_ws"], 16 * 3 * NSH)
            for w in range(2):
                for s in range(NSH):
                    nc.scalar.copy(w_hi[:, w, s, :], stage[:, w, s, :]).then_inc(hi_ready, 1)
            act.wait_ge(lo_ready, 2 * NSH)

            def step(g):
                if routed(g):
                    for j in range(TPB):
                        need(act, fT_full, g * TPB + (j + 1))
                        if j >= 2:
                            need(act, fT_kept, g * TPB + (j - 1))
                            need(act, lg_full, g * TPB + (j - 1))
                        nc.scalar.copy(flat_hi[:, :, j * P:j * P + P], pX[j % 2][:].rearrange("p (d t) -> p d t", d=DB))
                        nc.scalar.copy(flatTt[:, j % 2].rearrange("p d t -> p (d t)"), pX[j % 2][:]).then_inc(fT_ready, 1)
                for n in range(SharedExperts.CHUNKS):
                    if prepared(g) and n == 7:
                        need(act, scattered, (g + 1) * (TPB * TOP1 * 16))
                    if with_shared(g):
                        shared.gate(act, g, n, pG)
                    if prepared(g):
                        if n == 3:
                            need(act, lnz_ready, g * TPB + 2 * TPB, alone=1)
                            need(act, x3_ready, g * TPB + TPB)
                            for j in range(TPB):
                                nc.scalar.activation(z[:, j, :], row(x_sb, (g + 1) * TPB + j), ACT.Identity,
                                                     scale=lnz[:, j, 0:1], bias=lnz[:, j, 1:2]).then_inc(z_ready, 1)
                        if n == 7:
                            need(act, lnf_ready, g * TPB + 2 * TPB, alone=1)
                            for j in range(TPB):
                                nc.scalar.activation(flat[:, j, :], row(x_sb, (g + 1) * TPB + j), ACT.Identity,
                                                     scale=lnf[:, j, 0:1], bias=lnf[:, j, 1:2]).then_inc(flat_ready, 1)

            groups(act, step)

        @block.vector
        def _(dve):
            dve.wait_ge(small_loaded, 64)
            dve.wait_ge(w_ready, 1)
            nc.vector.tensor_tensor(wtmp[:, 0, :], top0[:, :, 1], top0[:, :, 0], ALU.subtract).then_inc(wexp_ready, 1)
            nc.vector.tensor_scalar(beta[:], beta[:], gates[:, 1:2], None, ALU.mult).then_inc(beta_ready, 1)
            for n, (w, s) in enumerate((w, s) for w in range(2) for s in range(NSH)):
                dve.wait_ge(hi_ready, n + 1)
                nc.vector.tensor_tensor(w_lo[:, w, s, :], stage[:, w, s, :], w_hi[:, w, s, :],
                                        ALU.subtract).then_inc(lo_ready, 1)
            dve.wait_ge(wexp_ready, 2)
            nc.vector.tensor_scalar(wtmp[:, 2, :], wtmp[:, 1, :], 1.0, None, ALU.add)
            dve.drain()
            nc.vector.reciprocal(wtmp[:, 0, :], wtmp[:, 2, :])
            dve.drain()
            nc.vector.tensor_scalar(wmix[:, :, 0], wtmp[:, 0, :], gates[:, 2:3], None, ALU.mult)
            dve.drain()
            nc.vector.tensor_tensor(wmix[:, :, 1], wmix[:, :, 0], wtmp[:, 1, :], ALU.mult)
            dve.drain()

            def choose(g, j):
                need(dve, lg_full, g * TPB + (j + 1))
                nc.vector.tensor_tensor(logits[:, j, :], pL[:, 0:E1], bias_r[:], ALU.add).then_inc(lg_read, 1)
                dve.drain()
                nc.vector.max(m8[:], logits[:, j, :])
                dve.drain()
                nc.vector.max_index(i8[:], m8[:], logits[:, j, :])
                nc.vector.tensor_copy(row(top1, g * TPB + j), m8[:, 0:TOP1])
                dve.drain()
                nc.vector.tensor_copy(idxf[:, j, :], i8[:, 0:TOP1])
                dve.drain()
                for k in range(TOP1):
                    nc.vector.tensor_scalar(onehot[:, j, k, :], iota_e[:], idxf[:, j, k:k + 1], None, ALU.is_equal)
                dve.drain()
                for k in range(2):
                    nc.vector.tensor_tensor(pair[:, k, :], onehot[:, j, 2 * k, :], onehot[:, j, 2 * k + 1, :], ALU.add)
                dve.drain()
                nc.vector.tensor_tensor(mask[:, j, :], pair[:, 0, :], pair[:, 1, :], ALU.add).then_inc(mask_ready, 1)

            def place(g, j):
                need(dve, pos_full, g * TPB + (j + 1))
                nc.vector.tensor_tensor(chosen[:, 1 - j % 2, :], chosen[:, j % 2, :], mask[:, j, :], ALU.add)
                for k in range(TOP1):
                    last = nc.vector.tensor_tensor_reduce(out=junk[:, k, :], in0=onehot[:, j, k, :], in1=pC[:, 0:E1],
                                                          scale=1.0, scalar=0.0, op0=ALU.mult, op1=ALU.add,
                                                          accum_out=posf[:, k:k + 1])
                last.then_inc(pos_read, 1)
                dve.drain()
                nc.vector.tensor_scalar(drop[:], posf[:], float(CAP1), float(E1 * CAP1), ALU.is_ge, ALU.mult)
                nc.vector.tensor_scalar(row(kept1, g * TPB + j), posf[:], float(CAP1), None, ALU.is_lt)
                nc.vector.scalar_tensor_tensor(slotf[:], idxf[:, j, :], float(CAP1), posf[:], ALU.mult, ALU.add)
                dve.drain()
                nc.vector.tensor_tensor(drop[:], slotf[:], drop[:], ALU.add)
                nc.vector.tensor_scalar(posf[:], posf[:], float(CAP1 - 1), None, ALU.min)
                dve.drain()
                nc.vector.scalar_tensor_tensor(row(take1, g * TPB + j), idxf[:, j, :], float(CAP1), posf[:],
                                               ALU.mult, ALU.add)
                nc.vector.tensor_copy(slot1[:, j, :], drop[:]).then_inc(slot_ready, 1)
                dve.drain()

            def scale_and_bias(ln, ready):
                nc.vector.tensor_copy(ln[:, :, 0], rstd[:])
                nc.vector.scalar_tensor_tensor(ln[:, :, 1], mv[:, :, 0], -1.0, rstd[:], ALU.mult,
                                               ALU.mult).then_inc(ready, TPB)

            def statistics():
                dve.drain()
                for j in range(TPB):
                    nc.vector.bn_aggr(mv[:, j, :], bn[:, j, :])
                dve.drain()
                rsqrt(nc, dve, rstd[:], mv[:, :, 1], half[:], (ve[:], nt[:]))

            def combine(g, k):
                dve.drain()
                if k == 0:
                    need(dve, gathered, g * (TPB * 32) + TPB * 32 * 2)
                for j in range(TPB):
                    t = (g + 1) * TPB + j
                    last = nc.vector.scalar_tensor_tensor(row(x_sb, t), y0[:, j, k, :], row(wmix, t)[:, k:k + 1],
                                                          row(x_sb, t), ALU.mult, ALU.add)
                    if k:
                        last.then_inc(x2_ready, 1)

            def attend(g):
                dve.drain()
                nc.vector.tensor_scalar(rstd[:], rstd[:], gates[:, 1:2], None, ALU.mult)
                for j in range(TPB):
                    nc.vector.scalar_tensor_tensor(z[:, j, :], z[:, j, :], mv[:, j, 0:1], gamma[:],
                                                   ALU.subtract, ALU.mult)
                dve.drain()
                for j in range(TPB):
                    t = (g + 1) * TPB + j
                    need(dve, xb_ready, t + 1)
                    nc.vector.scalar_tensor_tensor(row(x_sb, t), z[:, j, :], rstd[:, j:j + 1], row(x_sb, t),
                                                   ALU.mult, ALU.add).then_inc(x3_ready, 1)

            def step(g):
                if routed(g):
                    for j in range(TPB):
                        choose(g, j)
                for n in range(SharedExperts.CHUNKS):
                    if with_shared(g):
                        shared.product(dve, g, n, pU)
                    if routed(g) and n < TPB:
                        place(g, n)
                    if prepared(g):
                        if n < 2:
                            combine(g, n)
                        if n == 2:
                            dve.drain()
                            for j in range(TPB):
                                nc.vector.bn_stats(bn[:, j, :], row(x_sb, (g + 1) * TPB + j))
                            statistics()
                            need(dve, z_ready, g * TPB + TPB)
                            scale_and_bias(lnz, lnz_ready)
                        if n == 5:
                            for j in range(TPB):
                                need(dve, y_ready, g * TPB + (TPB + j + 1))
                                nc.vector.bn_stats(bn[:, j, :], z[:, j, :])
                            statistics()
                        if n == 6:
                            attend(g)
                        if n == 7:
                            dve.drain()
                            for j in range(TPB):
                                nc.vector.bn_stats(bn[:, j, :], row(x_sb, (g + 1) * TPB + j))
                            statistics()
                            need(dve, flat_ready, g * TPB + TPB)
                            scale_and_bias(lnf, lnf_ready)
                if with_shared(g):
                    for j in range(TPB):
                        shared.add(dve, g, j, g * TPB + j, pX)

            groups(dve, step)


def experts(nc, A, T):
    c = ExitStack()
    with c:
        def sb(name, shape, dt=F32):
            return c.enter_context(nc.sbuf_tensor(name, shape, dt))

        def sem(name):
            return c.enter_context(nc.semaphore(name))

        bank, ident, top1, kept1, wt1 = T["bank"], T["ident"], T["top1"], T["kept1"], T["wt1"]
        RING = 4
        AHEAD = RING - 1
        xb = sb("m1_x", [P, RING, D])
        wg = sb("m1_wg", [P, RING, DB, H1])
        wu = sb("m1_wu", [P, RING, DB, H1])
        wd = sb("m1_wd", [P, RING, D])
        xT = sb("m1_xT", [P, 2, DB, CAP1])
        g = sb("m1_silu", [P, 2, CAP1])
        h = sb("m1_h", [P, 2, CAP1])
        y = sb("m1_y", [P, 2, D])
        wsum = sb("wsum", [P, TILES])
        x_loaded = [sem(f"m1_x_loaded_{n}") for n in range(RING)]
        w_loaded = [sem(f"m1_w_loaded_{n}") for n in range(RING)]
        stored = [sem("m1_stored_even"), sem("m1_stored_odd")]
        xT_full, xT_ready, h_full, g_ready, h_ready = (sem(n) for n in (
            "m1_xT_full", "m1_xT_ready", "m1_h_full", "m1_g_ready", "m1_h_ready"))
        y_full, y_ready = sem("m1_y_full"), sem("m1_y_ready")
        less_max, exp_ready = sem("m1_less_max"), sem("m1_exp_ready")
        pX, pH, pY = bank[0:2], bank[2:4], bank[4:6]
        block = c.enter_context(nc.Block())

        def weights(name, e):
            if isinstance(e, int):
                return A[name][e].rearrange("(p b) h -> p b h", b=DB)
            return A[name][bass.ds(e, 1)].rearrange("o (p b) h -> p (o b) h", b=DB)

        def back(e):
            return A["L1_ffn_Wd"][e] if isinstance(e, int) else \
                A["L1_ffn_Wd"][bass.ds(e, 1)].rearrange("o h d -> h (o d)")

        @block.sync
        def _(sp):
            def step(i, u, q):
                if valid(i + AHEAD, n=E1):
                    e, n = i + AHEAD, (q + AHEAD) % RING
                    need(sp, y_full, i)
                    sp.dma_start(xb[:, n, :], T["tab1"][bass.ds(e * CAP1, CAP1), :]).then_inc(x_loaded[n], 16)
                    sp.dma_start(wg[:, n], weights("L1_ffn_Wg", e)).then_inc(w_loaded[n], 16)
                    sp.dma_start(wu[:, n], weights("L1_ffn_Wu", e)).then_inc(w_loaded[n], 16)
                    sp.dma_start(wd[:, n, :], back(e)).then_inc(w_loaded[n], 16)
                if valid(i, n=E1):
                    need(sp, y_ready, i + 1)
                    sp.dma_start(T["ytab1"][bass.ds(i * CAP1, CAP1), :], y[:, q % 2, :]).then_inc(stored[q % 2], 16)

            steps(sp, step, E1, RING, AHEAD, 0)
            for s in range(2):
                sp.wait_ge(stored[s], 16 * E1 // 2)

        @block.tensor
        def _(pe):
            def step(i, u, q):
                s, o = q % 2, 1 - q % 2
                if valid(i + 1, n=E1):
                    n = (q + 1) % RING
                    need(pe, x_loaded[n], (u + (q + 1) // RING) * 16 + 16)
                    need(pe, xT_ready, i)
                    for b in range(DB):
                        last = nc.tensor.transpose(pX[o][:, b * P:b * P + P],
                                                   xb[:, n, :].rearrange("t (p b) -> t b p", b=DB)[:, b, :], ident[:])
                    last.then_inc(xT_full, 1)
                if valid(i, n=E1):
                    need(pe, w_loaded[q], u * 48 + 48)
                    need(pe, xT_ready, i + 1)
                    need(pe, h_ready, i - 1)
                    for k, w in enumerate((wg, wu)):
                        for b in range(DB):
                            last = nc.tensor.matmul(pH[s][:, k * CAP1:(k + 1) * CAP1], w[:, q, b, :], xT[:, s, b, :],
                                                    start=(b == 0), stop=(b == DB - 1))
                    last.then_inc(h_full, 1)
                if valid(i - 1, n=E1):
                    need(pe, h_ready, i)
                    need(pe, y_ready, i - 2)
                    nc.tensor.matmul(pY[o][:], h[:, o, :], wd[:, (q - 1) % RING, :],
                                     start=True, stop=True).then_inc(y_full, 1)

            steps(pe, step, E1, RING, 1, 1)

        @block.scalar
        def _(act):
            act.wait_ge(less_max, 1)
            nc.scalar.activation(wt1[:], wt1[:], ACT.Exp).then_inc(exp_ready, 1)

            def step(i, u, q):
                s, o = q % 2, 1 - q % 2
                if valid(i + 1, n=E1):
                    need(act, xT_full, i + 2)
                    need(act, h_full, i)
                    nc.scalar.copy(xT[:, o].rearrange("p d t -> p (d t)"), pX[o][:]).then_inc(xT_ready, 1)
                if valid(i, n=E1):
                    need(act, h_full, i + 1)
                    need(act, h_ready, i - 1)
                    nc.scalar.activation(g[:, s, :], pH[s][:, 0:CAP1], ACT.Silu).then_inc(g_ready, 1)

            steps(act, step, E1, RING, 1, 1)

        @block.vector
        def _(dve):
            shape = [P, TILES, TOP1]
            nc.vector.tensor_tensor(wt1[:], top1[:], top1[:, :, 0:1].broadcast_to(shape), ALU.subtract).then_inc(less_max, 1)
            dve.wait_ge(exp_ready, 1)
            nc.vector.tensor_reduce(wsum[:], wt1[:], AX.X, ALU.add)
            dve.drain()
            nc.vector.reciprocal(wsum[:], wsum[:])
            dve.drain()
            nc.vector.tensor_tensor(wt1[:], wt1[:], wsum[:].unsqueeze(2).broadcast_to(shape), ALU.mult)
            dve.drain()
            nc.vector.scalar_tensor_tensor(wt1[:], kept1[:], T["gates"][:, 3:4], wt1[:], ALU.mult, ALU.mult)
            dve.drain()

            def step(i, u, q):
                s, o = q % 2, 1 - q % 2
                if valid(i, n=E1):
                    need(dve, g_ready, i + 1)
                    need(dve, y_full, i - 1)
                    nc.vector.tensor_tensor(h[:, s, :], g[:, s, :], pH[s][:, CAP1:2 * CAP1], ALU.mult).then_inc(h_ready, 1)
                if valid(i - 1, n=E1):
                    need(dve, y_full, i)
                    need(dve, stored[o], (u * (RING // 2) + (q - 1) // 2) * 16)
                    nc.vector.tensor_copy(y[:, o, :], pY[o][:]).then_inc(y_ready, 1)

            steps(dve, step, E1, RING, 1, 1)


def finish(nc, A, T, out):
    c = ExitStack()
    with c:
        def sb(name, shape, dt=F32):
            return c.enter_context(nc.sbuf_tensor(name, shape, dt))

        def sem(name):
            return c.enter_context(nc.semaphore(name))

        x_sb, bank, take1, wt1 = T["x_sb"], T["bank"], T["take1"], T["wt1"]
        pY, pG, pU = bank[0:2], bank[4:6], bank[6:8]
        RING = 4
        G = B - 1
        y1 = sb("y1", [P, RING, TOP1, D])
        shared = SharedExperts(nc, T, c, "b")
        gathered = [sem(f"y1_gathered_{n}") for n in range(RING)]
        combined, stored = sem("combined"), sem("out_stored")
        out_v = out.rearrange("b (t p) d -> p (b t) d", p=P)
        block = c.enter_context(nc.Block())

        @block.sync
        def _(sp):
            for t in range(TILES):
                if t < G * TPB:
                    sp.wait_ge(combined, t + 1)
                else:
                    sp.wait_ge(shared.y_read, t - G * TPB + 1)
                sp.dma_start(out_v[:, t, :], x_sb[:, t, :]).then_inc(stored, 16)
            sp.wait_ge(stored, 16 * TILES)

        @block.gpsimd
        def _(pool):
            for t in range(TILES):
                need(pool, combined, t - RING + 1)
                for k in range(TOP1):
                    nc.gpsimd.indirect_dma_start(
                        y1[:, t % RING, k, :], None, T["ytab1"],
                        bass.IndirectOffsetOnAxis(take1[:, t, k:k + 1], 0)).then_inc(gathered[t % RING], 16)

        @block.tensor
        def _(pe):
            for n in range(SharedExperts.CHUNKS):
                shared.up(pe, 0, n, pG, pU)
            for j in range(TPB):
                shared.down(pe, 0, j, pY)

        @block.scalar
        def _(act):
            for n in range(SharedExperts.CHUNKS):
                shared.gate(act, 0, n, pG)

        @block.vector
        def _(dve):
            with dve.Fori(0, TILES // RING) as u:
                for q in range(RING):
                    if q % 2 == 0:
                        shared.product(dve, 0, u * 2 + q // 2, pU, odd=q // 2)
                    t = u * RING + q
                    need(dve, gathered[q], u * (16 * TOP1) + 16 * TOP1)
                    for k in range(TOP1):
                        last = nc.vector.scalar_tensor_tensor(row(x_sb, t), y1[:, q, k, :], row(wt1, t)[:, k:k + 1],
                                                              row(x_sb, t), ALU.mult, ALU.add)
                        if k < TOP1 - 1:
                            dve.drain()
                    last.then_inc(combined, 1)
            dve.drain()
            for j in range(TPB):
                shared.add(dve, 0, j, G * TPB + j, pY)


class SharedExperts:

    CHUNKS = NSH * HSH // P

    def __init__(self, nc, T, c, tag, hidden=None):
        self.nc, self.T = nc, T
        n = self.CHUNKS
        self.g = c.enter_context(nc.sbuf_tensor(f"sh_gate_{tag}", [P, 2, SEQ], F32))
        self.h = c.enter_context(nc.sbuf_tensor(f"sh_h_{tag}", [P, n, SEQ], F32)) if hidden is None else hidden
        self.up_full, self.g_ready, self.h_ready, self.y_full, self.y_read = (
            c.enter_context(nc.semaphore(f"sh_{s}_{tag}")) for s in ("up_full", "g_ready", "h_ready", "y_full", "y_read"))

    def up(self, pe, r, n, pG, pU):
        nc, T = self.nc, self.T
        s, at = n // (HSH // P), (n % (HSH // P)) * P
        if n >= 2:
            need(pe, self.h_ready, r * self.CHUNKS + (n - 1))
        for k, bank in ((0, pG[n % 2]), (1, pU[n % 2])):
            for d in range(DB):
                cols = slice(d * HSH + at, d * HSH + at + P)
                for part, (w, x) in enumerate(((T["w_hi"], T["flat_hi"]), (T["w_hi"], T["flat_lo"]), (T["w_lo"], T["flat_hi"]))):
                    last = nc.tensor.matmul(bank[:], w[:, k, s, cols], x[:, d, :], start=(d == 0 and part == 0),
                                            stop=(d == DB - 1 and part == 2))
        last.then_inc(self.up_full, 1)

    def gate(self, act, r, n, pG):
        need(act, self.up_full, r * self.CHUNKS + (n + 1))
        if n >= 2:
            need(act, self.h_ready, r * self.CHUNKS + (n - 1))
        self.nc.scalar.activation(self.g[:, n % 2, :], pG[n % 2][:], ACT.Silu).then_inc(self.g_ready, 1)

    def product(self, dve, r, n, pU, odd=None):
        odd = n % 2 if odd is None else odd
        need(dve, self.g_ready, r * self.CHUNKS + (n + 1))
        self.nc.vector.tensor_tensor(row(self.h, n), self.g[:, odd, :], pU[odd][:], ALU.mult).then_inc(self.h_ready, 1)

    def down(self, pe, r, j, pY):
        nc, sd = self.nc, self.T["w_sd"]
        need(pe, self.h_ready, r * self.CHUNKS + self.CHUNKS)
        if j >= 2:
            need(pe, self.y_read, r * TPB + (j - 1))
        for n in range(self.CHUNKS):
            s, b = n // (HSH // P), n % (HSH // P)
            last = nc.tensor.matmul(pY[j % 2][:], self.h[:, n, j * P:j * P + P], sd[:, s, b, :],
                                    start=(n == 0), stop=(n == self.CHUNKS - 1))
        last.then_inc(self.y_full, 1)

    def add(self, dve, r, j, t, pY):
        x = row(self.T["x_sb"], t)
        need(dve, self.y_full, r * TPB + (j + 1))
        self.nc.vector.scalar_tensor_tensor(x, pY[j % 2][:], self.T["gates"][:, 3:4], x, ALU.mult,
                                            ALU.add).then_inc(self.y_read, 1)


INPUTS = (
    "x", "ctx_2048", "g_xattn", "g_ffn", "L0_ffn_w_gate", "L0_ffn_wi_0", "L0_ffn_wi_1", "L0_ffn_wo",
    "L1_xattn_decay", "L1_xattn_W_in", "L1_xattn_b_in", "L1_xattn_W_out", "L1_xattn_b_out",
    "L1_xattn_gamma", "L1_xattn_beta", "L1_ffn_Wr", "L1_ffn_router_bias", "L1_ffn_Wg", "L1_ffn_Wu",
    "L1_ffn_Wd", "L1_ffn_Sg", "L1_ffn_Su", "L1_ffn_Sd")


def kernel(**inputs):
    import numpy as np
    import concourse.bacc as bacc
    from concourse import mybir
    from concourse.bass_utils import run_bass_kernel_spmd

    nc = bacc.Bacc("TRN2", target_bir_lowering=False, num_devices=1)
    arrays, A = {}, {}
    for name in INPUTS:
        a = np.ascontiguousarray(inputs[name])
        if inputs[name].ndim == 0:
            a = a.reshape(1, 1)
        arrays[f"in_{name}"] = a
        A[name] = nc.dram_tensor(f"in_{name}", a.shape, mybir.dt.from_np(a.dtype), kind="ExternalInput").ap()
    out = nc.dram_tensor("out", inputs["x"].shape, mybir.dt.float32, kind="ExternalOutput").ap()
    build(nc, A, out)
    r = run_bass_kernel_spmd(nc, [arrays], core_ids=[0])
    return r.results[0]["out"]
```

```python
from contextlib import ExitStack

import concourse.bass as bass
from concourse import mybir

F32 = mybir.dt.float32
F32R = mybir.dt.float32r
BF16 = mybir.dt.bfloat16
I32 = mybir.dt.int32
U32 = mybir.dt.uint32
ALU = mybir.AluOpType
ACT = mybir.ActivationFunctionType
AX = mybir.AxisListType

P = 128
B, SEQ, D = 4, 512, 512
TILES = B * SEQ // P
TPB = SEQ // P
DB = D // P
HEAD = 64
E0, M0 = 8, 256
E1, H1, TOP1, CAP1 = 64, 128, 4, 128
NSH, HSH = 2, 512
LN_EPS = 1e-5
E0_STRIDE = B * SEQ + P
L0_TILES = 40
DUMMY_ROW = E0 * E0_STRIDE
TAB0_ROWS = DUMMY_ROW + E0 * P
ZERO_CHUNKS = 2 * E0
W_RING = 8
W_EARLY = 5
RSQRT_MAGIC = float(0x5F3759DF)


def seen(k):
    return min(k + 1, TILES) if isinstance(k, int) else k + 1


def need(eng, sem, value, alone=0):
    if not isinstance(value, int):
        if alone:
            eng.wait_ge(sem, alone)
        eng.wait_ge(sem, value)
    elif value > 0:
        eng.wait_ge(sem, value)


def row(t, k):
    if isinstance(k, int):
        return t[:, k, :]
    return t[:, bass.ds(k, 1), :].rearrange("p o d -> p (o d)")


def valid(*tiles, n=TILES):
    return all(not isinstance(k, int) or 0 <= k < n for k in tiles)


def steps(eng, step, n, ring, lead, tail):
    first, last = max(-(-lead // ring), -(-4 // ring)), (n - lead) // ring
    for i in range(-lead, first * ring):
        step(i, i // ring, i % ring)
    with eng.Fori(first, last) as u:
        for c in range(ring):
            step(u * ring + c, u, c)
    for i in range(last * ring, n + tail):
        step(i, i // ring, i % ring)


def rsqrt_guess(nc, dve, y, v, half, ve):
    nc.vector.tensor_scalar(ve, v, LN_EPS, None, ALU.add)
    dve.drain()
    nc.vector.tensor_scalar(half.bitcast(I32), ve.bitcast(I32), 1, None, ALU.logical_shift_right)
    dve.drain()
    return nc.vector.tensor_scalar(y.bitcast(I32), half.bitcast(I32), -1.0, RSQRT_MAGIC, ALU.mult, ALU.add)


def newton(ops, eng, y, ve, t):
    ops.tensor_tensor(t, y, y, ALU.mult)
    eng.drain()
    ops.tensor_tensor(t, t, ve, ALU.mult)
    eng.drain()
    ops.tensor_scalar(t, t, -0.5, 1.5, ALU.mult, ALU.add)
    eng.drain()
    ops.tensor_tensor(y, y, t, ALU.mult)
    eng.drain()


def rsqrt(nc, dve, y, v, half, scratch):
    ve, t = scratch
    rsqrt_guess(nc, dve, y, v, half, ve)
    dve.drain()
    for _ in range(3):
        nc.vector.tensor_tensor(t, y, y, ALU.mult)
        dve.drain()
        nc.vector.scalar_tensor_tensor(t, t, -0.5, ve, ALU.mult, ALU.mult)
        dve.drain()
        nc.vector.scalar_tensor_tensor(y, t, 1.5, y, ALU.add, ALU.mult)
        dve.drain()


def build(nc, A, out):
    ctx = ExitStack()
    with ctx:
        def sb(name, shape, dt=F32, c=ctx, side=None):
            return c.enter_context(nc.sbuf_tensor(name, shape, dt, side=side))

        bank = [ctx.enter_context(nc.psum_tensor(f"bank{n}", [P, 512], F32)) for n in range(8)]

        x_sb = sb("x_sb", [P, TILES, D])
        ident = sb("ident", [P, P])
        identb = sb("identb", [P, P], BF16)
        onesb = sb("onesb", [P, P], BF16)
        before = sb("before", [P, P], BF16)
        iota_e = sb("iota_e", [P, E1])
        base0 = sb("base0", [P, E0])
        base1 = sb("base1", [P, E1])
        rowid = sb("rowid", [P, 1])
        gates = sb("gates", [P, 4])
        top0 = sb("top0", [P, TILES, 2])
        slot0 = sb("slot0", [P, TILES, 2], I32)
        take0 = sb("take0", [P, TILES, 2], I32)
        summary = sb("summary", [P, B, D])
        mstate = sb("mstate", [P, DB, B])
        bout_col = sb("bout_col", [P, DB])
        tinfo = sb("tinfo", [1, L0_TILES, 2], I32)

        tab0 = nc.dram_tensor("tab0", (TAB0_ROWS, D), F32, kind="Internal").ap()
        ytab0 = nc.dram_tensor("ytab0", (L0_TILES * P, D), F32, kind="Internal").ap()
        tab1 = nc.dram_tensor("tab1", (E1 * CAP1, D), F32, kind="Internal").ap()
        ytab1 = nc.dram_tensor("ytab1", (E1 * CAP1, D), F32, kind="Internal").ap()

        arena0 = ExitStack()
        later = ExitStack()
        with arena0:
            w01 = sb("w01", [P, E0 * DB, 2 * M0], F32, arena0, "right")
            wo0 = sb("wo0", [P, E0 * (M0 // P), D], F32, arena0, "right")
            s_w0 = arena0.enter_context(nc.semaphore("weights0_loaded"))
            s_padded = ctx.enter_context(nc.semaphore("table0_padded"))
            s_zero1 = ctx.enter_context(nc.semaphore("table1_zeroed"))
            T = dict(locals())
            held = ExitStack()
            with held:
                T["zeros"] = sb("zeros", [P, D], F32, held)
                T["chosen"] = sb("chosen", [P, 2, E0], BF16, held)
                T["ccol"] = sb("ccol", [P, 2, TPB], F32, held)
                T["ucol"] = sb("ucol", [P, DB, B], F32, held)
                T["ones"] = sb("ones", [P, E0], F32, held)
                T["win"], T["wout"] = (sb(n, [P, DB, D], F32, held) for n in ("win", "wout"))
                T["bin_col"] = sb("bin_col", [P, DB], F32, held)
                T["s_sw"] = held.enter_context(nc.semaphore("summary_weights_loaded"))
                attention(nc, A, T)
                summary_and_tiles(nc, A, T)
            later.__enter__()
            T["s_ws"] = later.enter_context(nc.semaphore("shared_weights_loaded"))
            staged = ExitStack()
            staged.__enter__()
            T["stage_up"] = sb("stage_up", [P, NSH, DB * HSH], F32, staged)
            mixture0(nc, A, T)
        with later:
            with staged:
                T["stage_gate"] = sb("stage_gate", [P, NSH, DB * HSH], F32, staged)
                T["y0"] = sb("y0", [P, TPB, 2, D], F32, staged)
                T["s_w1"] = [staged.enter_context(nc.semaphore(f"m1_loaded_{n}")) for n in range(W_RING)]
                T["w_hi"], T["w_lo"] = (sb(n, [P, 2, NSH, DB * HSH], F32R, later, "right") for n in ("w_hi", "w_lo"))
                T["w_sd"] = sb("w_sd", [P, NSH, DB, HSH], F32, later, "right")
                T["flat_hi"], T["flat_lo"] = (sb(n, [P, DB, SEQ], F32R, later, "right") for n in ("flat_hi", "flat_lo"))
                for name, dt in (("top1", F32), ("take1", I32), ("wt1", F32), ("kept1", F32)):
                    T[name] = sb(name, [P, TILES, TOP1], dt, later, "right")
                middle(nc, A, T)
                experts(nc, A, T)
            finish(nc, A, T, out)


def attention(nc, A, T):
    c = ExitStack()
    with c:
        def sb(name, shape, dt=F32):
            return c.enter_context(nc.sbuf_tensor(name, shape, dt))

        def sem(name):
            return c.enter_context(nc.semaphore(name))

        x_sb, bank = T["x_sb"], T["bank"]
        ident, identb, onesb, before = T["ident"], T["identb"], T["onesb"], T["before"]
        gates, iota_e, base0, rowid = T["gates"], T["iota_e"], T["base0"], T["rowid"]
        w01, wo0, s_w0, s_zero1 = T["w01"], T["wo0"], T["s_w0"], T["s_zero1"]

        zeros, chosen = T["zeros"], T["chosen"]
        kd = T["wout"][:].rearrange("p (s h) d -> p s h d", s=2)
        k_hi = sb("k_hi", [P, 2, 2, D], F32R)
        k_lo = sb("k_lo", [P, 2, 2, D], F32R)
        q_parts = sb("q_parts", [P, 2, 2, D], F32R)
        q = sb("q", [P, D])
        vT = sb("vT", [P, 2, 4, 3, HEAD])
        negmax = sb("negmax", [P, 2, 8], BF16)
        probs = T["win"][:].rearrange("p (s h) d -> p s h d", s=2)
        attn = sb("attn", [P, D])
        numer = sb("numer", [P, D])
        xn = sb("xn", [P, 2, D])
        xnT = sb("xnT", [P, DB, P])
        bn = sb("bn", [P, 2, 6])
        mv = sb("mv", [P, 2, 2])
        rstd = sb("rstd", [P, 2])
        half, ve, nt = sb("half", [P, 2]), sb("ve", [P, 2]), sb("nt", [P, 2])
        ln1 = sb("ln1", [P, 2, 2])
        ln2 = sb("ln2", [P, 2, 2])
        logits = sb("logits", [P, E0])
        m8 = sb("m8", [P, 8])
        i8 = sb("i8", [P, 8], U32)
        idxf = sb("idxf", [P, 2])
        onehot = sb("onehot", [P, 2, E0])
        mask = sb("mask", [P, 2, E0], BF16)
        rows = sb("rows", [P, E0])
        junk = sb("junk", [P, 2, E0])
        slotf = sb("slotf", [P, 2])
        wg = sb("wg", [P, DB, E0])
        graw = sb("graw", [P, 4])
        ccol, ucol, ones = T["ccol"], T["ucol"], T["ones"]
        flip = xnT[:, 0, :]
        decay = sb("decay", [1, 4])
        kdec = sb("kdec", [1, 1])
        invt = sb("invt", [1, 1])
        crow = attn[0:1, :]
        wsel = sb("wsel", [P, B, TPB, B])
        urow = sb("urow", [B, D])

        s_xA, s_xB, s_small = sem("xA_loaded"), sem("xB_loaded"), sem("small_loaded")
        kd_loaded = [sem("kd_loaded_even"), sem("kd_loaded_odd")]
        consts_ready, zeros_ready, gates_ready = sem("consts_ready"), sem("zeros_ready"), sem("gates_ready")
        pm_full, pm_read = sem("pm_full"), sem("pm_read")
        k_hi_ready, k_lo_ready, q_ready = sem("k_hi_ready"), sem("k_lo_ready"), sem("q_ready")
        q_hi_ready, q_split, recip_ready = sem("q_hi_ready"), sem("q_split"), sem("recip_ready")
        guess_ready, ln2_ready, xn_ready = sem("guess_ready"), sem("ln2_ready"), sem("xn_ready")
        ctx_loaded = [sem(f"ctx_loaded_{n}") for n in range(4)]
        ctx_used, newton_done = sem("ctx_used"), sem("newton_done")
        vT_full, vT_ready = sem("vT_full"), sem("vT_ready")
        s_full, p_ready, p_used, qk_done = sem("s_full"), sem("p_ready"), sem("p_used"), sem("qk_done")
        sums_ready, po_read, x1_ready = sem("sums_ready"), sem("po_read"), sem("x1_ready")
        xnT_full, xnT_ready = sem("xnT_full"), sem("xnT_ready")
        lg_full, mask_ready, pos_full, pos_read = sem("lg_full"), sem("mask_ready"), sem("pos_full"), sem("pos_read")
        slot_ready = sem("slot_ready")
        scattered = [sem("scattered_even"), sem("scattered_odd")]
        dummy_zeroed = sem("dummy_zeroed")

        pS, pO, pM, pT = bank[0:2], bank[2:6], bank[6], bank[7]
        x_v = A["x"].rearrange("b (t p) d -> p (b t) d", p=P)
        ctx_ring = T["wout"]
        c_v = A["ctx_2048"].rearrange("b (t p) d -> p (b t) d", p=P)
        NA = 3
        SMALL = 16 * 4
        crow_ready, col_full, col_ready = sem("crow_ready"), sem("col_full"), sem("col_ready")
        flip_full, wsel_ready = sem("flip_full"), sem("wsel_ready")
        urow_ready, uT_full = sem("urow_ready"), sem("uT_full")

        block = c.enter_context(nc.Block())

        def load_k(eng, t, slot):
            at = A["ctx_2048"].rearrange("b (g h c) d -> (b g) h c d", h=2, c=HEAD)
            src = at[t] if isinstance(t, int) else at[bass.ds(t, 1)].rearrange("o h c d -> h (o c) d")
            for h in range(2):
                for half_ in range(2):
                    eng.dma_start(kd[half_ * HEAD:half_ * HEAD + HEAD, slot, h, :], src[h]).then_inc(kd_loaded[slot], 16)

        @block.sync
        def _(sp):
            sp.dma_start(x_sb[:, 0:NA, :], x_v[:, 0:NA, :]).then_inc(s_xA, 16)
            sp.dma_start(decay[0:1, 0:1], A["L1_xattn_decay"]).then_inc(s_small, 16)
            sp.dma_start(graw[:, 0:2], A["g_xattn"].partition_broadcast(P)).then_inc(s_small, 16)
            sp.dma_start(graw[:, 2:4], A["g_ffn"].partition_broadcast(P)).then_inc(s_small, 16)
            sp.dma_start(wg[:], A["L0_ffn_w_gate"].rearrange("(b p) e -> p b e", p=P)).then_inc(s_small, 16)
            for t in range(2):
                load_k(sp, t, t)
            sp.dma_start(x_sb[:, NA:, :], x_v[:, NA:, :]).then_inc(s_xB, 16)
            sp.wait_ge(zeros_ready, 1)
            sp.dma_start(T["tab0"][DUMMY_ROW:, :].rearrange("(r p) d -> p r d", p=P),
                         zeros[:].unsqueeze(1).broadcast_to([P, E0, D])).then_inc(dummy_zeroed, 16)
            t1 = T["tab1"].rearrange("(n r p) d -> n p r d", p=P, n=ZERO_CHUNKS)
            w01_v = w01[:].rearrange("p (e b) m -> p e b m", e=E0)
            wo0_v = wo0[:].rearrange("p (e b) d -> p e b d", e=E0)

            def pick(t, u):
                return t[u] if isinstance(u, int) else t[bass.ds(u, 1)].rearrange("o r d -> (o r) d")

            def behind(u):
                at = [w01_v[:, u, :, 0:M0], w01_v[:, u, :, M0:2 * M0], wo0_v[:, u]] if isinstance(u, int) else [
                    x.rearrange("p o b m -> p (o b) m") for x in (
                        w01_v[:, bass.ds(u, 1), :, 0:M0], w01_v[:, bass.ds(u, 1), :, M0:2 * M0], wo0_v[:, bass.ds(u, 1)])]
                for x, name in zip(at, ("L0_ffn_wi_0", "L0_ffn_wi_1", "L0_ffn_wo")):
                    sp.dma_start(x, pick(A[name], u).rearrange("(b p) m -> p b m", p=P)).then_inc(s_w0, 16)
                for n in range(2):
                    chunk = t1[u * 2 + n] if isinstance(u, int) else \
                        t1[bass.ds(u * 2 + n, 1)].rearrange("o p r d -> p (o r) d")
                    sp.dma_start(chunk, zeros[:].unsqueeze(1).broadcast_to(
                        [P, E1 * CAP1 // (ZERO_CHUNKS * P), D])).then_inc(s_zero1, 16)

            behind(0)
            with sp.Fori(1, TILES // 2) as u:
                for n in range(2):
                    t = u * 2 + n
                    sp.wait_ge(vT_full, t - 1)
                    sp.wait_ge(k_lo_ready, t - 1)
                    load_k(sp, t, n)
                behind(u)
            sp.wait_ge(dummy_zeroed, 16)
            sp.wait_ge(vT_full, TILES)
            sp.wait_ge(k_lo_ready, TILES)
            for t in range(TILES):
                need(sp, ctx_used, t - 3)
                sp.dma_start(ctx_ring[:, t % 4, :], c_v[:, t, :]).then_inc(ctx_loaded[t % 4], 16)
            sp.wait_ge(p_used, 8 * TILES)
            sp.dma_start(T["win"][:], A["L1_xattn_W_in"].rearrange("(b p) d -> p b d", p=P)).then_inc(T["s_sw"], 16)
            sp.wait_ge(ctx_used, TILES)
            sp.dma_start(T["wout"][:], A["L1_xattn_W_out"].rearrange("(b p) d -> p b d", p=P)).then_inc(T["s_sw"], 16)
            for col, name in (("bin_col", "L1_xattn_b_in"), ("bout_col", "L1_xattn_b_out")):
                sp.dma_start(T[col][:], A[name].rearrange("(b p) -> p b", p=P),
                             allow_slow_non_contiguous=True).then_inc(T["s_sw"], 16)

        @block.gpsimd
        def _(pool):
            nc.gpsimd.memset(ident[:], 0.0)
            nc.gpsimd.memset(onesb[:], 1.0)
            nc.gpsimd.memset(zeros[:], 0.0)
            nc.gpsimd.memset(vT[:, :, :, 1, :], 1.0)
            nc.gpsimd.memset(chosen[:], 0.0)
            nc.gpsimd.memset(flip, 0.0)
            nc.gpsimd.memset(ones[:], 1.0)
            nc.gpsimd.memset(invt[:], 1.0 / SEQ)
            nc.gpsimd.memset(wsel[:], 0.0)
            nc.gpsimd.iota(iota_e[:], [[1, E1]], base=0, channel_multiplier=0, allow_small_or_imprecise_dtypes=True)
            nc.gpsimd.iota(base0[:], [[E0_STRIDE, E0]], base=0, channel_multiplier=0,
                           allow_small_or_imprecise_dtypes=True)
            nc.gpsimd.iota(T["base1"][:], [[CAP1, E1]], base=0, channel_multiplier=0,
                           allow_small_or_imprecise_dtypes=True)
            nc.gpsimd.iota(rowid[:], [[0, 1]], base=0, channel_multiplier=1, allow_small_or_imprecise_dtypes=True)
            pool.drain()
            nc.gpsimd.affine_select(ident[:], ident[:], [[-1, P]], ALU.not_equal, 1.0, base=0, channel_multiplier=1)
            nc.gpsimd.affine_select(flip, flip, [[1, P]], ALU.not_equal, 1.0, base=1 - P, channel_multiplier=1)
            nc.gpsimd.affine_select(before[:], onesb[:], [[1, P]], ALU.is_ge, 0.0, base=-1, channel_multiplier=-1)
            pool.drain()
            nc.gpsimd.tensor_copy(identb[:], ident[:])
            pool.drain()
            nc.gpsimd.engine_nop().then_inc(consts_ready, 1)
            nc.gpsimd.engine_nop().then_inc(zeros_ready, 1)
            for i in range(-3, TILES + 3):
                if valid(i - 3):
                    pool.wait_ge(slot_ready, i - 2)
                    for k in range(2):
                        nc.gpsimd.indirect_dma_start(
                            T["tab0"], bass.IndirectOffsetOnAxis(T["slot0"][:, i - 3, k:k + 1], 0),
                            xn[:, (i - 3) % 2, :], None).then_inc(scattered[(i - 3) % 2], 16)
                if valid(i + 2):
                    s = i % 2
                    need(pool, q_split, i + 2)
                    nc.gpsimd.tensor_scalar(q[:], x_sb[:, i + 2, :], ln1[:, s, 0:1], ln1[:, s, 1:2],
                                            ALU.mult, ALU.add).then_inc(q_ready, 1)
                if valid(i - 1):
                    pool.wait_ge(po_read, i)
                    pool.wait_ge(recip_ready, 2 * i)
                    nc.gpsimd.tensor_tensor(attn[:], attn[:], numer[:], ALU.mult)
                    pool.drain()
                    nc.gpsimd.tensor_tensor(x_sb[:, i - 1, :], x_sb[:, i - 1, :], attn[:],
                                            ALU.add).then_inc(x1_ready, 1)
                cols = [n for n, k in enumerate((i - 1, i + 3)) if valid(k)]
                if cols:
                    a, z = cols[0], cols[-1] + 1
                    pool.wait_ge(guess_ready, i + 4)
                    for _ in range(3):
                        newton(nc.gpsimd, pool, rstd[:, a:z], ve[:, a:z], nt[:, a:z])
                    for n, ln in ((0, ln2[:, (i - 1) % 2]), (1, ln1[:, (i + 3) % 2])):
                        if n in cols:
                            if n == 0:
                                need(pool, xn_ready, i - 2)
                            nc.gpsimd.tensor_copy(ln[:, 0:1], rstd[:, n:n + 1])
                            last = nc.gpsimd.tensor_scalar(ln[:, 1:2], mv[:, n, 0:1], rstd[:, n:n + 1], -1.0,
                                                           ALU.mult, ALU.mult)
                            if n == 0:
                                last.then_inc(ln2_ready, 1)
                    pool.drain()
                    nc.gpsimd.engine_nop().then_inc(newton_done, 1)
                if valid(i + 2):
                    s = i % 2
                    pool.wait_ge(k_hi_ready, i + 3)
                    for h in range(2):
                        last = nc.gpsimd.tensor_tensor(k_lo[:, s, h, :], kd[:, s, h, :], k_hi[:, s, h, :], ALU.subtract)
                    last.then_inc(k_lo_ready, 1)
            for s in range(2):
                pool.wait_ge(scattered[s], 16 * TILES)

        @block.tensor
        def _(pe):
            pe.wait_ge(consts_ready, 1)
            pe.wait_ge(s_small, SMALL)
            pe.wait_ge(crow_ready, 1)
            for j in range(TPB):
                last = nc.tensor.matmul(pM[:, j:j + 1], crow[0:1, j * P:j * P + P], ones[0:1, 0:1], start=True, stop=True)
            last.then_inc(col_full, 1)
            pe.wait_ge(col_ready, 1)
            nc.tensor.matmul(pM[:, 0:TPB], flip, ccol[:, 0, :], start=True, stop=True).then_inc(flip_full, 1)
            pe.wait_ge(wsel_ready, 1)

            def weighted_context():
                for t in range(TILES):
                    pe.wait_ge(ctx_loaded[t % 4], 16 * (t // 4 + 1))
                    last = nc.tensor.matmul(pM[0:B, :], wsel[:, t // TPB, t % TPB, :], ctx_ring[:, t % 4, :],
                                            start=(t == 0), stop=(t == TILES - 1)).then_inc(ctx_used, 1)

            def context_columns():
                pe.wait_ge(urow_ready, 1)
                for n in range(DB):
                    last = nc.tensor.transpose(pM[:, n * B:n * B + B], urow[:, n * P:n * P + P], ident[0:B, 0:B])
                last.then_inc(uT_full, 1)

            def scores(i, s, sb_):
                for h in range(2):
                    need(pe, p_ready, i * 8 + (sb_ * 2 + h - 1))
                    for part in (k_hi, k_lo):
                        last = nc.tensor.matmul(pS[h][:], part[:, s, h, sb_ * P:sb_ * P + P], q_parts[:, s, h, :],
                                                start=(part is k_hi), stop=False)
                if sb_ == 3:
                    last.then_inc(qk_done, 1)
                if sb_ == 0:
                    need(pe, pm_read, i * 8 + 8)
                for h in range(2):
                    for t in range(4):
                        m = h * 4 + t
                        last = nc.tensor.matmul(pS[h][:, t * P:t * P + P],
                                                negmax[:, s, m:m + 1].broadcast_to([P, P]), identb[:],
                                                start=False, stop=(t == 3))
                    last.then_inc(s_full, 1)

            def values(k, s, sb_, h):
                need(pe, p_ready, k * 8 + (sb_ * 2 + h + 1))
                nc.tensor.matmul(pO[s * 2 + h][:], vT[:, s, sb_, h:h + 2, :].rearrange("p a c -> p (a c)"),
                                 probs[:, sb_ % 2, h, :], start=(sb_ == 0), stop=(sb_ == 3)).then_inc(p_used, 1)

            def rough(k, s, m):
                h, t = m // 4, m % 4
                need(pe, pm_read, k * 8 + m)
                nc.tensor.matmul(pM[:], q_parts[:, s, h, t * P:t * P + P], k_hi[:, s, h, :],
                                 start=True, stop=True).then_inc(pm_full, 1)

            def step(i, u, odd):
                s, o = odd, 1 - odd
                if valid(i):
                    need(pe, q_split, i + 1)
                    need(pe, k_lo_ready, i + 1)
                for b in range(4):
                    if valid(i):
                        scores(i, s, b)
                    if b == 0 and valid(i - 3):
                        need(pe, mask_ready, i - 2)
                        nc.tensor.matmul(pT[:, 0:E0], before[:], mask[:, o, :], start=True, stop=False)
                        nc.tensor.matmul(pT[:, 0:E0], onesb[:], chosen[:, o, :], start=False,
                                         stop=True).then_inc(pos_full, 1)
                    if b > 0 and valid(i + 1):
                        rough(i + 1, o, (None, 1, 3, 5)[b])
                    if b == 1 and valid(i):
                        need(pe, po_read, i - 1)
                        need(pe, vT_ready, i + 1)
                    for h in range(2):
                        if b == 0 and valid(i - 1):
                            values(i - 1, o, 3, h)
                        if b > 0 and valid(i):
                            values(i, s, b - 1, h)
                        if b == 3 and h == 0 and valid(i + 1):
                            rough(i + 1, o, 6)
                    if valid(i + 1):
                        if b == 0:
                            need(pe, q_split, i + 2)
                            need(pe, k_hi_ready, i + 2)
                        if b == 1 and valid(i - 2):
                            need(pe, xnT_ready, i - 1)
                        elif b == 1:
                            need(pe, vT_ready, i + 1)
                        rough(i + 1, o, (0, 2, 4, 7)[b])
                    if isinstance(i, int) and b == 1:
                        if i == TILES:
                            weighted_context()
                        if i == TILES + 1:
                            context_columns()
                    if b == 0 and valid(i - 2):
                        need(pe, pos_read, i - 2)
                        need(pe, vT_ready, seen(i))
                        need(pe, xn_ready, i - 1)
                        for t in range(DB):
                            last = nc.tensor.transpose(pT[:, t * P:t * P + P], xn[:, s, t * P:t * P + P], ident[:])
                        last.then_inc(xnT_full, 1)
                    if b == 1 and valid(i + 1):
                        for t in range(4):
                            for h in range(2):
                                last = nc.tensor.transpose(pT[:, t * P + h * HEAD:t * P + h * HEAD + HEAD],
                                                           kd[0:HEAD, o, h, t * P:t * P + P], ident[0:HEAD, 0:HEAD])
                        last.then_inc(vT_full, 1)
                    if b == 2 and valid(i - 2):
                        need(pe, vT_ready, seen(i + 1))
                        need(pe, xnT_ready, i - 1)
                        for d in range(DB):
                            last = nc.tensor.matmul(pT[:, 0:E0], xnT[:, d, :], wg[:, d, :],
                                                    start=(d == 0), stop=(d == DB - 1))
                        last.then_inc(lg_full, 1)

            steps(pe, step, TILES, 2, 2, 3)

        @block.scalar
        def _(act):
            act.wait_ge(s_small, SMALL)
            nc.scalar.activation(decay[0:1, 1:2], decay[0:1, 0:1], ACT.Exp, scale=-1.0)
            nc.scalar.activation(gates[:], graw[:], ACT.Tanh).then_inc(gates_ready, 1)

            def step(i, u, odd):
                s, o = odd, 1 - odd
                for b in range(4):
                    if valid(i):
                        for h in range(2):
                            n = b * 2 + h
                            need(act, p_used, i * 8 + (n - 3))
                            need(act, s_full, i * 8 + (n + 1))
                            nc.scalar.activation(probs[:, b % 2, h, :], pS[h][:], ACT.Exp,
                                                 scale=1.0 / HEAD).then_inc(p_ready, 1)
                    if b == 0 and valid(i - 1):
                        need(act, x1_ready, i - 1)
                        need(act, p_used, i * 8)
                        nc.scalar.copy(attn[0:HEAD, :], pO[o * 2][HEAD:P, :])
                        nc.scalar.copy(attn[HEAD:P, :], pO[o * 2 + 1][0:HEAD, :]).then_inc(sums_ready, 1)
                    if b == 1 and valid(i - 1):
                        for h in range(2):
                            hp = slice(HEAD * h, HEAD * h + HEAD)
                            last = nc.scalar.activation(numer[hp, :], pO[o * 2 + h][hp, :], ACT.Copy, scale=gates[hp, 0:1])
                        last.then_inc(po_read, 1)
                    if b == 0 and valid(i - 2):
                        need(act, xnT_full, i - 1)
                        nc.scalar.copy(xnT[:].rearrange("p d t -> p (d t)"), pT[:]).then_inc(xnT_ready, 1)
                    if b == 2 and valid(i + 1):
                        need(act, p_used, i * 8)
                        need(act, vT_full, i + 2)
                        pv = pT[:].rearrange("p (t a c) -> p t a c", t=4, a=2)
                        nc.scalar.copy(vT[:, o, :, 0, :], pv[:, :, 0, :])
                        nc.scalar.copy(vT[:, o, :, 2, :], pv[:, :, 1, :]).then_inc(vT_ready, 1)
                    if b == 3 and valid(i + 2):
                        need(act, qk_done, i + 1)
                        need(act, q_ready, i + 3)
                        for h in range(2):
                            hp = slice(HEAD * h, HEAD * h + HEAD)
                            last = nc.scalar.copy(q_parts[hp, s, h, :], q[hp, :])
                        last.then_inc(q_hi_ready, 1)
                        need(act, kd_loaded[s], 64 * u + 128)
                        for h in range(2):
                            last = nc.scalar.copy(k_hi[:, s, h, :], kd[:, s, h, :])
                        last.then_inc(k_hi_ready, 1)
                    if b == 3 and valid(i - 1):
                        half_ = u + (odd - 1) // 2
                        need(act, ln2_ready, i, alone=1)
                        need(act, scattered[o], half_ * 32)
                        nc.scalar.activation(xn[:, o, :], row(x_sb, i - 1), ACT.Identity,
                                             scale=ln2[:, o, 0:1], bias=ln2[:, o, 1:2]).then_inc(xn_ready, 1)
                    if isinstance(i, int) and i == TILES and b == 3:
                        act.wait_ge(ctx_used, TILES)
                        nc.scalar.copy(urow[:], pM[0:B, :]).then_inc(urow_ready, 1)
                    if isinstance(i, int) and i == TILES + 1 and b == 3:
                        act.wait_ge(uT_full, 1)
                        nc.scalar.copy(ucol[:].rearrange("p n b -> p (n b)"), pM[:, 0:DB * B])

            steps(act, step, TILES, 2, 2, 2)

        @block.vector
        def _(dve):
            dve.wait_ge(consts_ready, 1)
            def state_weights():
                dve.wait_ge(gates_ready, 1)
                nc.vector.tensor_scalar(decay[0:1, 2:3], decay[0:1, 1:2], 1.0, None, ALU.add)
                dve.drain()
                nc.vector.reciprocal(kdec[:], decay[0:1, 2:3])
                dve.drain()
                nc.vector.tensor_tensor_scan(crow, kdec[:].broadcast_to([1, SEQ]), invt[:].broadcast_to([1, SEQ]),
                                             0.0, ALU.mult, ALU.add).then_inc(crow_ready, 1)
                dve.wait_ge(col_full, 1)
                nc.vector.tensor_copy(ccol[:, 0, :], pM[:, 0:TPB]).then_inc(col_ready, 1)
                dve.wait_ge(flip_full, 1)
                for j in range(TPB):
                    nc.vector.tensor_copy(ccol[:, 1, j:j + 1], pM[:, TPB - 1 - j:TPB - j])
                dve.drain()
                for b in range(B):
                    last = nc.vector.tensor_copy(wsel[:, b, :, b], ccol[:, 1, :])
                last.then_inc(wsel_ready, 1)

            def rough_max(k, s, m):
                need(dve, pm_full, k * 8 + (m + 1))
                if m == 0:
                    need(dve, s_full, k * 8 - 8)
                nc.vector.tensor_reduce(negmax[:, s, m:m + 1], pM[:], AX.X, ALU.max,
                                        negate=True).then_inc(pm_read, 1)

            def largest(k):
                need(dve, lg_full, k + 1)
                nc.vector.tensor_copy(logits[:], pT[:, 0:E0])
                dve.drain()
                nc.vector.max(m8[:], logits[:])

            def choose(k, s):
                dve.drain()
                nc.vector.max_index(i8[:], m8[:], logits[:])
                nc.vector.tensor_copy(row(T["top0"], k), m8[:, 0:2])
                dve.drain()
                nc.vector.tensor_copy(idxf[:], i8[:, 0:2])
                dve.drain()
                for c_ in range(2):
                    nc.vector.tensor_scalar(onehot[:, c_, :], iota_e[:, 0:E0], idxf[:, c_:c_ + 1], None, ALU.is_equal)
                dve.drain()
                nc.vector.tensor_tensor(mask[:, s, :], onehot[:, 0, :], onehot[:, 1, :],
                                        ALU.add).then_inc(mask_ready, 1)

            def place(k, s):
                need(dve, pos_full, k + 1)
                nc.vector.tensor_tensor(rows[:], pT[:, 0:E0], base0[:], ALU.add).then_inc(pos_read, 1)
                nc.vector.tensor_tensor(chosen[:, 1 - s, :], chosen[:, s, :], mask[:, s, :], ALU.add)
                dve.drain()
                for c_ in range(2):
                    nc.vector.tensor_tensor_reduce(out=junk[:, c_, :], in0=onehot[:, c_, :], in1=rows[:], scale=1.0,
                                                   scalar=0.0, op0=ALU.mult, op1=ALU.add,
                                                   accum_out=slotf[:, c_:c_ + 1])
                dve.drain()
                nc.vector.tensor_copy(row(T["slot0"], k), slotf[:]).then_inc(slot_ready, 1)

            def step(i, u, odd):
                s, o = odd, 1 - odd
                if isinstance(i, int) and i == NA - 3:
                    dve.wait_ge(s_xB, 16)
                cols = [n for n, k in enumerate((i - 1, i + 3)) if valid(k)]
                for m in range(8):
                    if m == 0 and valid(i - 3):
                        place(i - 3, o)
                    if valid(i + 1):
                        rough_max(i + 1, o, m)
                    if m < 2 and valid(i - 1):
                        dve.drain()
                        need(dve, sums_ready, i)
                        cols_ = slice(m * D // 2, (m + 1) * D // 2)
                        nc.vector.reciprocal(attn[:, cols_], attn[:, cols_]).then_inc(recip_ready, 1)
                    if m == 3 and cols:
                        a, z = cols[0], cols[-1] + 1
                        need(dve, newton_done, i + 3)
                        if valid(i + 3):
                            if isinstance(i, int):
                                dve.wait_ge(s_xA, 16)
                            nc.vector.bn_stats(bn[:, 1, :], row(x_sb, i + 3))
                        if valid(i - 1):
                            need(dve, x1_ready, i, alone=1)
                            nc.vector.bn_stats(bn[:, 0, :], row(x_sb, i - 1))
                        dve.drain()
                        for n in cols:
                            nc.vector.bn_aggr(mv[:, n, :], bn[:, n, :])
                        dve.drain()
                        rsqrt_guess(nc, dve, rstd[:, a:z], mv[:, a:z, 1], half[:, a:z], ve[:, a:z]).then_inc(guess_ready, 1)
                    if m == 5 and valid(i - 2):
                        largest(i - 2)
                    if m == 6 and valid(i - 2):
                        choose(i - 2, s)
                if isinstance(i, int) and i == -3:
                    state_weights()
                if valid(i + 2):
                    need(dve, q_hi_ready, i + 3)
                    for h in range(2):
                        hp, other = (slice(HEAD * n, HEAD * n + HEAD) for n in (h, 1 - h))
                        last = nc.vector.tensor_tensor(q_parts[other, s, h, :], q[hp, :], q_parts[hp, s, h, :], ALU.subtract)
                    last.then_inc(q_split, 1)

            steps(dve, step, TILES, 2, 3, 3)


def summary_and_tiles(nc, A, T):
    c = ExitStack()
    with c:
        def sb(name, shape, dt=F32):
            return c.enter_context(nc.sbuf_tensor(name, shape, dt))

        def sem(name):
            return c.enter_context(nc.semaphore(name))

        bank, ident, onesb = T["bank"], T["ident"], T["onesb"]
        pS, pO, pM, pT = bank[0:2], bank[2:6], bank[6], bank[7]
        base0, rowid, chosen, zeros = T["base0"], T["rowid"], T["chosen"], T["zeros"]
        ccol, ucol, ones = T["ccol"], T["ucol"], T["ones"]
        iota_i = sb("iota_i", [1, L0_TILES])
        cnt = sb("cnt", [P, E0])
        padf = sb("padf", [P, E0])
        padrow = sb("padrow", [P, E0], I32)
        ntf = sb("ntf", [P, E0])
        nti = sb("nti", [P, E0], I32)
        cum = sb("cum", [1, E0])
        texp = sb("texp", [1, L0_TILES])
        tskip = sb("tskip", [1, L0_TILES])
        trow = sb("trow", [1, L0_TILES])
        win, wout = T["win"], T["wout"]
        winT = sb("winT", [P, DB, D])
        woutT = T["summary"]
        bin_col, mstate = T["bin_col"], T["mstate"]
        csum = sb("csum", [P, 1])
        usum = sb("usum", [P, 4 * TILES])
        big = sb("big", [P, L0_TILES * E0])
        past = big[0:1, 0:L0_TILES * E0].rearrange("p (t e) -> p t e", e=E0)
        slotf = usum[:, 2 * TILES:4 * TILES]

        s_sw = T["s_sw"]
        consts_ready = sem("summary_consts_ready")
        cnt_full, pad_ready = sem("cnt_full"), sem("pad_ready")
        sum_full, m_full = sem("weights_sum_full"), sem("m_full")
        wT_full, wT_ready = sem("wT_full"), sem("wT_ready")

        block = c.enter_context(nc.Block())

        @block.gpsimd
        def _(pool):
            nc.gpsimd.iota(iota_i[:], [[1, L0_TILES]], base=0, channel_multiplier=0,
                           allow_small_or_imprecise_dtypes=True)
            pool.drain()
            nc.gpsimd.engine_nop().then_inc(consts_ready, 1)
            pool.wait_ge(pad_ready, 1)
            for e in range(E0):
                nc.gpsimd.indirect_dma_start(T["tab0"], bass.IndirectOffsetOnAxis(padrow[:, e:e + 1], 0),
                                             zeros[:, 0:D], None).then_inc(T["s_padded"], 16)

        @block.tensor
        def _(pe):
            nc.tensor.matmul(pT[:, 0:E0], onesb[:], chosen[:, TILES % 2, :], start=True, stop=True).then_inc(cnt_full, 1)

            for j in range(TPB):
                last = nc.tensor.matmul(pS[0][:, 0:1], ccol[:, 1, j:j + 1].broadcast_to([P, P]), ones[:, 0:1],
                                        start=(j == 0), stop=(j == TPB - 1))
            last.then_inc(sum_full, 1)
            pe.wait_ge(s_sw, 64)
            for n in range(2 * DB):
                w, k = (win, n) if n < DB else (wout, n - DB)
                if n >= 4:
                    pe.wait_ge(wT_ready, n - 3)
                for q in range(DB):
                    last = nc.tensor.transpose(pO[n % 4][:, q * P:q * P + P], w[:, q, k * P:k * P + P], ident[:])
                last.then_inc(wT_full, 1)
            pe.wait_ge(wT_ready, DB)
            for q in range(DB):
                for n in range(DB):
                    last = nc.tensor.matmul(pM[:, q * B:q * B + B], winT[:, n, q * P:q * P + P], ucol[:, n, :],
                                            start=(n == 0), stop=(n == DB - 1))
            last.then_inc(m_full, 1)

        @block.scalar
        def _(act):
            for n in range(2 * DB):
                wT, k = (winT, n) if n < DB else (woutT, n - DB)
                act.wait_ge(wT_full, n + 1)
                nc.scalar.copy(wT[:, k, :], pO[n % 4][:]).then_inc(wT_ready, 1)

        @block.vector
        def _(dve):
            dve.wait_ge(consts_ready, 1)
            dve.wait_ge(cnt_full, 1)
            nc.vector.tensor_copy(cnt[:], pT[:, 0:E0])
            dve.drain()
            nc.vector.scalar_tensor_tensor(padf[:], cnt[:], rowid[:, 0:1], base0[:], ALU.add, ALU.add)
            nc.vector.tensor_scalar(ntf[:], cnt[:], float(P - 1), None, ALU.add)
            dve.drain()
            nc.vector.tensor_copy(padrow[:], padf[:]).then_inc(pad_ready, 1)

            nc.vector.tensor_copy(nti[:], ntf[:])
            dve.drain()
            nc.vector.tensor_scalar(nti[:], nti[:], 7, None, ALU.logical_shift_right)
            dve.drain()
            nc.vector.tensor_copy(ntf[:], nti[:])
            dve.drain()
            nc.vector.tensor_tensor_scan(cum[:], ones[0:1, 0:E0], ntf[0:1, :], 0.0, ALU.mult, ALU.add)
            dve.drain()
            nc.vector.tensor_tensor(past, iota_i[:].unsqueeze(2).broadcast_to([1, L0_TILES, E0]),
                                    cum[:].unsqueeze(1).broadcast_to([1, L0_TILES, E0]), ALU.is_ge)
            dve.drain()
            nc.vector.tensor_reduce(texp[:], past, AX.X, ALU.add)
            dve.drain()
            nc.vector.tensor_tensor(past, past, ntf[0:1, :].unsqueeze(1).broadcast_to([1, L0_TILES, E0]), ALU.mult)
            dve.drain()
            nc.vector.tensor_reduce(tskip[:], past, AX.X, ALU.add)
            nc.vector.tensor_scalar(trow[:], texp[:], float(E0_STRIDE), None, ALU.mult)
            dve.drain()
            nc.vector.tensor_tensor(tskip[:], iota_i[:], tskip[:], ALU.subtract)
            dve.drain()
            nc.vector.scalar_tensor_tensor(trow[:], tskip[:], float(P), trow[:], ALU.mult, ALU.add)
            dve.drain()
            nc.vector.tensor_copy(T["tinfo"][0:1, :, 0], trow[:])
            nc.vector.tensor_scalar(T["tinfo"][0:1, :, 1], texp[:], float(E0 - 1), None, ALU.min)

            ge = big[:, 0:2 * TILES * (E0 - 1)].rearrange("p (t e) -> p t e", e=E0 - 1)
            shape = [P, 2 * TILES, E0 - 1]
            nc.vector.tensor_copy(slotf, T["slot0"][:].rearrange("p t k -> p (t k)"))
            nc.vector.tensor_scalar(ntf[:], ntf[:], float(P), float(-E0_STRIDE), ALU.mult, ALU.add)
            dve.drain()
            nc.vector.tensor_tensor(ge, slotf.unsqueeze(2).broadcast_to(shape),
                                    base0[:, 1:E0].unsqueeze(1).broadcast_to(shape), ALU.is_ge)
            dve.drain()
            nc.vector.tensor_tensor(ge, ge, ntf[:, 0:E0 - 1].unsqueeze(1).broadcast_to(shape), ALU.mult)
            dve.drain()
            nc.vector.tensor_reduce(usum[:, 0:2 * TILES], ge, AX.X, ALU.add)
            dve.drain()
            nc.vector.tensor_tensor(T["take0"][:].rearrange("p t k -> p (t k)"), slotf, usum[:, 0:2 * TILES], ALU.add)
            dve.drain()

            dve.wait_ge(sum_full, 1)
            nc.vector.tensor_copy(csum[:], pS[0][:, 0:1])
            dve.drain()
            dve.wait_ge(s_sw, 64)
            nc.vector.tensor_scalar(bin_col[:], bin_col[:], csum[:, 0:1], None, ALU.mult)
            dve.drain()
            dve.wait_ge(m_full, 1)
            nc.vector.tensor_tensor(mstate[:], pM[:, 0:DB * B].rearrange("p (n b) -> p n b", b=B),
                                    bin_col[:].unsqueeze(2).broadcast_to([P, DB, B]), ALU.add)


def mixture0(nc, A, T):
    c = ExitStack()
    with c:
        def sb(name, shape, dt=F32):
            return c.enter_context(nc.sbuf_tensor(name, shape, dt))

        def sem(name):
            return c.enter_context(nc.semaphore(name))

        bank, ident, tinfo, w01, wo0 = T["bank"], T["ident"], T["tinfo"], T["w01"], T["wo0"]
        N, MB = L0_TILES, M0 // P
        RING = 4
        AHEAD = RING - 1
        HALF = DB // 2
        xb = sb("m0_x", [P, RING, D])
        x_hi, x_lo = (sb(f"m0_xT_{n}", [P, 2, DB, P], F32R) for n in ("hi", "lo"))
        up_hi, up_lo = (sb(f"m0_up_{n}", [P, DB, 2 * M0], F32R) for n in ("hi", "lo"))
        dn_hi, dn_lo = (sb(f"m0_down_{n}", [P, MB, D], F32R) for n in ("hi", "lo"))
        act_g = sb("m0_silu", [P, M0])
        inter = sb("m0_inter", [P, 2, M0])
        in_hi, in_lo = (sb(f"m0_interT_{n}", [P, 2, MB, P], F32R) for n in ("hi", "lo"))
        y = sb("m0_y", [P, 2, D])
        x_loaded = [sem(f"m0_x_loaded_{n}") for n in range(RING)]
        stored = [sem("m0_stored_even"), sem("m0_stored_odd")]
        xT_full, x_hi_ready, x_lo_ready = sem("xT_full"), sem("x_hi_ready"), sem("x_lo_ready")
        up_hi_ready, up_lo_ready = sem("up_hi_ready"), sem("up_lo_ready")
        dn_hi_ready, dn_lo_ready = sem("down_hi_ready"), sem("down_lo_ready")
        half_used, h_full, g_ready = sem("up_half_used"), sem("h_full"), sem("g_ready")
        in_ready, inT_full, inT_ready = sem("in_ready"), sem("inT_full"), sem("inT_ready")
        dn_used, y_full, y_ready = sem("down_block_used"), sem("y_full"), sem("y_ready")
        pX, pH, pI, pY = bank[0:2], bank[2:4], bank[4:6], bank[6:8]
        block = c.enter_context(nc.Block())

        def blocks(w, first, n):
            return w[:, bass.ds(first, n), :]

        @block.sync
        def _(sp):
            def first_row(i):
                at = tinfo[0:1, i, 0:1] if isinstance(i, int) else \
                    tinfo[0:1, bass.ds(i, 1), 0:1].rearrange("p o d -> p (o d)")
                return sp.value_load(at, min_val=0, max_val=TAB0_ROWS - P)

            def step(i, u, q):
                if valid(i + AHEAD, n=N):
                    slot = (q + AHEAD) % RING
                    need(sp, xT_full, i)
                    sp.dma_start(xb[:, slot, :],
                                 T["tab0"][bass.ds(first_row(i + AHEAD), P), :]).then_inc(x_loaded[slot], 16)
                if isinstance(i, int) and i == 0:
                    for k in range(NSH):
                        sp.dma_start(T["stage_up"][:, k].rearrange("p (b h) -> p b h", b=DB),
                                     A["L1_ffn_Su"][k].rearrange("(b p) h -> p b h", p=P)).then_inc(T["s_ws"], 16)
                if valid(i - 1, n=N):
                    need(sp, y_ready, i)
                    sp.dma_start(T["ytab0"][bass.ds((i - 1) * P, P), :],
                                 y[:, (q - 1) % 2, :]).then_inc(stored[(q - 1) % 2], 16)

            sp.wait_ge(T["s_padded"], 16 * E0)
            steps(sp, step, N, RING, AHEAD, 1)
            for s in range(2):
                sp.wait_ge(stored[s], 16 * N // 2)

        @block.gpsimd
        def _(pool):
            def step(i, u, q):
                e = expert(pool, tinfo, i)
                for m in range(MB):
                    need(pool, dn_hi_ready, i * MB + (m + 1))
                    nc.gpsimd.tensor_tensor(dn_lo[:, m, :], row(wo0, e * MB + m), dn_hi[:, m, :],
                                            ALU.subtract).then_inc(dn_lo_ready, 1)

            steps(pool, step, N, RING, 0, 0)

        @block.tensor
        def _(pe):
            def step(i, u, q):
                s, o = q % 2, 1 - q % 2
                if valid(i + 1, n=N):
                    n = (q + 1) % RING
                    need(pe, x_loaded[n], (u + (q + 1) // RING) * 16 + 16)
                    need(pe, x_lo_ready, i)
                    for d in range(DB):
                        last = nc.tensor.transpose(pX[o][:, d * P:d * P + P], xb[:, n, d * P:d * P + P], ident[:])
                    last.then_inc(xT_full, 1)

                def up(half):
                    need(pe, up_lo_ready, 2 * i + (half + 1))
                    for d in range(half * HALF, half * HALF + HALF):
                        for part, (x, w) in enumerate(((x_hi, up_hi), (x_lo, up_hi), (x_hi, up_lo))):
                            last = nc.tensor.matmul(pH[s][:], x[:, s, d, :], w[:, d, :], start=(d == 0 and part == 0),
                                                    stop=(d == DB - 1 and part == 2))
                    last.then_inc(h_full if half else half_used, 1)

                if valid(i, n=N):
                    need(pe, x_lo_ready, i + 1)
                    need(pe, in_ready, i - 1)
                    up(0)
                if valid(i - 1, n=N):
                    need(pe, in_ready, i)
                    need(pe, inT_ready, i - 2)
                    for m in range(MB):
                        last = nc.tensor.transpose(pI[o][:, m * P:m * P + P], inter[:, o, m * P:m * P + P], ident[:])
                    last.then_inc(inT_full, 1)
                if valid(i, n=N):
                    up(1)
                if valid(i - 1, n=N):
                    need(pe, inT_ready, i)
                    need(pe, y_ready, i - 2)
                    for m in range(MB):
                        need(pe, dn_lo_ready, (i - 1) * MB + (m + 1))
                        for part, (h, w) in enumerate(((in_hi, dn_hi), (in_lo, dn_hi), (in_hi, dn_lo))):
                            last = nc.tensor.matmul(pY[o][:], h[:, o, m, :], w[:, m, :], start=(m == 0 and part == 0),
                                                    stop=(m == MB - 1 and part == 2))
                        last.then_inc(y_full if m == MB - 1 else dn_used, 1)

            steps(pe, step, N, RING, 1, 1)

        @block.scalar
        def _(act):
            act.wait_ge(T["s_w0"], 16 * 3 * E0)

            def step(i, u, q):
                s, o = q % 2, 1 - q % 2
                if valid(i + 1, n=N):
                    need(act, xT_full, i + 2)
                    need(act, h_full, i)
                    nc.scalar.copy(x_hi[:, o].rearrange("p d t -> p (d t)"), pX[o][:]).then_inc(x_hi_ready, 1)
                    need(act, half_used, i + 1)
                    e = expert(act, tinfo, i + 1)
                    nc.scalar.copy(up_hi[:, 0:HALF, :], blocks(w01, e * DB, HALF)).then_inc(up_hi_ready, 1)
                if valid(i, n=N):
                    need(act, h_full, i + 1)
                    need(act, in_ready, i)
                    nc.scalar.activation(act_g[:], pH[s][:, 0:M0], ACT.Silu).then_inc(g_ready, 1)
                if valid(i + 1, n=N):
                    nc.scalar.copy(up_hi[:, HALF:DB, :], blocks(w01, e * DB + HALF, HALF)).then_inc(up_hi_ready, 1)
                if valid(i, n=N):
                    e = expert(act, tinfo, i)
                    for m in range(MB):
                        need(act, y_full if m == MB - 1 else dn_used, i)
                        nc.scalar.copy(dn_hi[:, m, :], row(wo0, e * MB + m)).then_inc(dn_hi_ready, 1)
                if valid(i - 1, n=N):
                    need(act, y_full, i)
                    need(act, stored[o], (u * (RING // 2) + (q - 1) // 2) * 16)
                    nc.scalar.copy(y[:, o, :], pY[o][:]).then_inc(y_ready, 1)

            steps(act, step, N, RING, 1, 1)

        @block.vector
        def _(dve):
            def split_up(i, e, half):
                at = slice(half * HALF, half * HALF + HALF)
                need(dve, up_hi_ready, 2 * i + (half + 1))
                nc.vector.tensor_tensor(up_lo[:, at, :], blocks(w01, e * DB + half * HALF, HALF), up_hi[:, at, :],
                                        ALU.subtract).then_inc(up_lo_ready, 1)

            def step(i, u, q):
                s, o = q % 2, 1 - q % 2
                if valid(i - 1, n=N):
                    need(dve, inT_full, i)
                    need(dve, y_full, i - 2)
                    hi = in_hi[:, o].rearrange("p m t -> p (m t)")
                    nc.vector.tensor_copy(hi, pI[o][:, 0:M0])
                    dve.drain()
                    nc.vector.tensor_tensor(in_lo[:, o].rearrange("p m t -> p (m t)"), pI[o][:, 0:M0], hi,
                                            ALU.subtract).then_inc(inT_ready, 1)
                if valid(i + 1, n=N):
                    need(dve, x_hi_ready, i + 2)
                    nc.vector.tensor_tensor(x_lo[:, o].rearrange("p d t -> p (d t)"), pX[o][:],
                                            x_hi[:, o].rearrange("p d t -> p (d t)"), ALU.subtract).then_inc(x_lo_ready, 1)
                    e = expert(dve, tinfo, i + 1)
                    split_up(i + 1, e, 0)
                if valid(i, n=N):
                    need(dve, g_ready, i + 1)
                    need(dve, inT_full, i - 1)
                    nc.vector.tensor_tensor(inter[:, s, :], act_g[:], pH[s][:, M0:2 * M0],
                                            ALU.mult).then_inc(in_ready, 1)
                if valid(i + 1, n=N):
                    split_up(i + 1, e, 1)

            steps(dve, step, N, RING, 1, 1)


def expert(eng, tinfo, i):
    at = tinfo[0:1, i, 1:2] if isinstance(i, int) else tinfo[0:1, bass.ds(i, 1), 1:2].rearrange("p o d -> p (o d)")
    return eng.value_load(at, min_val=0, max_val=E0 - 1)


def middle(nc, A, T):
    c = ExitStack()
    with c:
        def sb(name, shape, dt=F32):
            return c.enter_context(nc.sbuf_tensor(name, shape, dt))

        def sem(name):
            return c.enter_context(nc.semaphore(name))

        x_sb, bank, ident, onesb, before = T["x_sb"], T["bank"], T["ident"], T["onesb"], T["before"]
        gates, iota_e, summary = T["gates"], T["iota_e"], T["summary"]
        flat_hi, flat_lo, w_hi, w_lo = T["flat_hi"], T["flat_lo"], T["w_hi"], T["w_lo"]
        stage = T["stage_gate"], T["stage_up"]
        top0, take0, top1, take1, kept1 = T["top0"], T["take0"], T["top1"], T["take1"], T["kept1"]
        pX, pL, pC, pG, pU = bank[0:2], bank[2], bank[3], bank[4:6], bank[6:8]
        pY = pG + pU

        y0 = T["y0"]
        hidden = stage[0][:].rearrange("p s (n t) -> p (s n) t", t=SEQ)
        z = stage[1][:, 0, :].rearrange("p (j d) -> p j d", j=TPB)
        flat = stage[1][:, 1, :].rearrange("p (j d) -> p j d", j=TPB)
        flatTt = z.rearrange("p j (d t) -> p j d t", d=DB)
        wr = sb("wr", [P, DB, E1])
        bias_r = sb("bias_r", [P, E1])
        gamma = sb("gamma", [P, D])
        beta = sb("beta", [P, D])
        wmix = sb("wmix", [P, TILES, 2])
        wtmp = sb("wtmp", [P, 3, TILES])
        bn = sb("bn1", [P, TPB, 6])
        mv = sb("mv1", [P, TPB, 2])
        rstd = sb("rstd1", [P, TPB])
        half, ve, nt = sb("half1", [P, TPB]), sb("ve1", [P, TPB]), sb("nt1", [P, TPB])
        lnz = sb("lnz", [P, TPB, 2])
        lnf = sb("lnf", [P, TPB, 2])
        logits = sb("logits1", [P, TPB, E1])
        m8 = sb("m81", [P, 8])
        i8 = sb("i81", [P, 8], U32)
        idxf = sb("idxf1", [P, TPB, TOP1])
        onehot = sb("onehot1", [P, TPB, TOP1, E1], BF16)
        pair = sb("pair1", [P, 2, E1])
        mask = sb("mask1", [P, TPB, E1], BF16)
        chosen = sb("chosen1", [P, 2, E1], BF16)
        junk = sb("junk1", [P, TOP1, E1])
        posf = sb("posf", [P, TOP1])
        woutT, mstate = summary, T["mstate"]
        scol = sb("scol", [P, DB, B])
        drop = sb("drop", [P, TOP1])
        slotf = sb("slotf1", [P, TOP1])
        slot1 = sb("slot1", [P, TPB, TOP1], I32)
        shared = SharedExperts(nc, T, c, "a", hidden)
        hi_ready, lo_ready, gate_lo_ready = sem("w_hi_ready"), sem("w_lo_ready"), sem("w_gate_lo_ready")

        s_full, scol_ready, rows_full, summary_ready = (sem(n) for n in (
            "s_full", "scol_ready", "summary_rows_full", "summary_ready"))
        small_loaded, gate_loaded, sd_loaded = (sem(n) for n in (
            "mid_small_loaded", "shared_gate_loaded", "shared_back_loaded"))
        gathered = [sem(f"y0_gathered_{j}") for j in range(TPB)]
        beta_ready, wexp_ready = sem("beta_ready"), sem("wexp_ready")
        x2_ready, lnz_ready, z_ready, y_ready, xb_ready = (sem(n) for n in (
            "x2_ready", "lnz_ready", "z_ready", "ysum_ready", "x_beta_ready"))
        x3_ready, lnf_ready, flat_ready = sem("x3_ready"), sem("lnf_ready"), sem("flat_ready")
        fT_full, fT_ready, fT_kept = sem("flatT_full"), sem("flatT_ready"), sem("flatT_kept")
        lg_full, mask_ready, pos_full, pos_read = (sem(n) for n in (
            "lg1_full", "mask1_ready", "pos1_full", "pos1_read"))
        slot_ready, scattered = sem("slot1_ready"), sem("flat_scattered")
        w_ready = sem("mid_zero_ready")
        SPLITS = [(w, s) for w in (1, 0) for s in range(NSH)]
        PLACED = {0: 0, 1: 1, 3: 2, 4: 3}
        groups_done = B - 1
        block = c.enter_context(nc.Block())

        def groups(eng, step):
            step(-1)
            with eng.Fori(0, groups_done) as g:
                step(g)
            step(B - 1)

        def turned(g, j):
            return (pX + pG)[j] if isinstance(g, int) else pX[j % 2]

        def logits_of(j):
            return (pL, pC)[j // 2][:, j % 2 * E1:j % 2 * E1 + E1]

        def split_weights(ops, eng, n):
            w, s = SPLITS[n]
            eng.wait_ge(hi_ready, n + 1)
            return ops.tensor_tensor(w_lo[:, w, s, :], stage[w][:, s, :], w_hi[:, w, s, :], ALU.subtract)

        def prepared(g):
            return not isinstance(g, int) or g + 1 < B

        def routed(g):
            return not isinstance(g, int) or g >= 0

        def with_shared(g):
            return not isinstance(g, int)

        @block.sync
        def _(sp):
            sp.dma_start(gamma[:], A["L1_xattn_gamma"].partition_broadcast(P)).then_inc(small_loaded, 16)
            sp.dma_start(beta[:], A["L1_xattn_beta"].partition_broadcast(P)).then_inc(small_loaded, 16)
            sp.dma_start(wr[:], A["L1_ffn_Wr"].rearrange("(b p) e -> p b e", p=P)).then_inc(small_loaded, 16)
            sp.dma_start(bias_r[:], A["L1_ffn_router_bias"].partition_broadcast(P)).then_inc(small_loaded, 16)
            sp.wait_ge(gathered[TPB - 1], 16 * 2)
            for s in range(NSH):
                sp.dma_start(stage[0][:, s].rearrange("p (b h) -> p b h", b=DB),
                             A["L1_ffn_Sg"][s].rearrange("(b p) h -> p b h", p=P)).then_inc(gate_loaded, 16)
            for s in range(NSH):
                sp.dma_start(T["w_sd"][:, s], A["L1_ffn_Sd"][s].rearrange("(b p) h -> p b h", p=P)).then_inc(sd_loaded, 16)

            free = {0: ((x2_ready, TILES),), 2: ((lg_full, TILES), (fT_kept, TILES)),
                    3: ((shared.y_full, groups_done * TPB),)}
            for e in range(W_EARLY):
                for used, count in free.get(e, ()):
                    sp.wait_ge(used, count)
                load_expert(sp, A, T, e, e)

        @block.gpsimd
        def _(pool):
            nc.gpsimd.memset(chosen[:], 0.0).then_inc(w_ready, 1)
            pool.wait_ge(T["s_zero1"], 16 * ZERO_CHUNKS)
            for g in range(-1, B):
                n = g + 1
                if n < B:
                    need(pool, x2_ready, TPB * n)
                    for j in range(TPB):
                        for k in range(2):
                            nc.gpsimd.indirect_dma_start(
                                y0[:, j, k, :], None, T["ytab0"],
                                bass.IndirectOffsetOnAxis(take0[:, n * TPB + j, k:k + 1], 0)).then_inc(gathered[j], 16)
                def dispatch(tiles):
                    for j in tiles:
                        pool.wait_ge(slot_ready, TPB * g + j + 1)
                        for k in range(TOP1):
                            nc.gpsimd.indirect_dma_start(
                                T["tab1"], bass.IndirectOffsetOnAxis(slot1[:, j, k:k + 1], 0), flat[:, j, :], None,
                                bounds_check=E1 * CAP1 - 1, oob_is_err=False).then_inc(scattered, 16)

                if g >= 0:
                    dispatch(range(TPB // 2))
                if n < B:
                    for j in range(TPB):
                        t = n * TPB + j
                        if t == 0:
                            pool.wait_ge(summary_ready, B)
                        pool.wait_ge(z_ready, t + 1)
                        nc.gpsimd.tensor_tensor(z[:, j, :], z[:, j, :], summary[:, n, :], ALU.add).then_inc(y_ready, 1)
                    for j in range(TPB):
                        t = n * TPB + j
                        if t == 0:
                            pool.wait_ge(beta_ready, 1)
                        nc.gpsimd.tensor_tensor(x_sb[:, t, :], x_sb[:, t, :], beta[:], ALU.add).then_inc(xb_ready, 1)
                if g >= 0:
                    dispatch(range(TPB // 2, TPB))
                if n == 0:
                    for k in range(NSH, 2 * NSH):
                        split_weights(nc.gpsimd, pool, k).then_inc(gate_lo_ready, 1)
                if 0 < n < B:
                    for j in range(TPB):
                        pool.wait_ge(fT_ready, TPB * n + j + 1)
                        cols = slice(j * P, j * P + P)
                        nc.gpsimd.tensor_tensor(flat_lo[:, :, cols], flatTt[:, j], flat_hi[:, :, cols],
                                                ALU.subtract).then_inc(fT_kept, 1)
            pool.wait_ge(scattered, 16 * TILES * TOP1)

        @block.tensor
        def _(pe):
            for q in range(DB):
                for n in range(DB):
                    last = nc.tensor.matmul(pC[:, q * B:q * B + B], woutT[:, n, q * P:q * P + P], mstate[:, n, :],
                                            start=(n == 0), stop=(n == DB - 1))
            last.then_inc(s_full, 1)
            pe.wait_ge(scol_ready, 1)
            for b in range(B):
                for q in range(DB):
                    last = nc.tensor.matmul(pY[b][:, q * P:q * P + P], scol[:, q, b:b + 1].broadcast_to([P, P]), ident[:],
                                            start=True, stop=True)
                last.then_inc(rows_full, 1)
            pe.wait_ge(small_loaded, 64)
            pe.wait_ge(sd_loaded, 16 * NSH)
            pe.wait_ge(lo_ready, NSH)
            pe.wait_ge(gate_lo_ready, NSH)
            pe.wait_ge(w_ready, 1)

            def transposed(g, j):
                need(pe, flat_ready, g * TPB + (j + 1))
                if j >= 2 and not isinstance(g, int):
                    need(pe, fT_ready, g * TPB + (j - 1))
                for d in range(DB):
                    last = nc.tensor.transpose(turned(g, j)[:, d * P:d * P + P], flat[:, j, d * P:d * P + P], ident[:])
                last.then_inc(fT_full, 1)

            def logit(g, j):
                need(pe, fT_ready, g * TPB + (j + 1))
                if j == 0:
                    need(pe, pos_read, g * TPB)
                for d in range(DB):
                    last = nc.tensor.matmul(logits_of(j), flatTt[:, j, d, :], wr[:, d, :],
                                            start=(d == 0), stop=(d == DB - 1))
                last.then_inc(lg_full, 1)

            def positions(g, j):
                need(pe, mask_ready, g * TPB + (j + 1))
                if j:
                    need(pe, pos_read, g * TPB + j)
                nc.tensor.matmul(pL[:, 0:E1], before[:], mask[:, j, :], start=True, stop=False)
                nc.tensor.matmul(pL[:, 0:E1], onesb[:], chosen[:, j % 2, :], start=False, stop=True).then_inc(pos_full, 1)

            def step(g):
                for n in range(SharedExperts.CHUNKS):
                    if with_shared(g):
                        if n == 0:
                            need(pe, fT_kept, g * TPB + TPB)
                        shared.up(pe, g, n, pG, pU)
                    if routed(g) and n in PLACED:
                        positions(g, PLACED[n])
                between = ((), ((transposed, 0), (transposed, 1)), ((logit, 0), (logit, 1), (transposed, 2), (transposed, 3)),
                           ((logit, 2), (logit, 3)))
                if isinstance(g, int) and g == -1:
                    between = (), (), [(transposed, k) for k in range(TPB)], [(logit, k) for k in range(TPB)]
                for j in range(TPB):
                    if with_shared(g):
                        shared.down(pe, g, j, pY)
                    if prepared(g):
                        for run, k in between[j]:
                            run(g + 1, k)
                if with_shared(g):
                    need(pe, shared.y_read, g * TPB + TPB)

            groups(pe, step)

        @block.scalar
        def _(act):
            def exp_logits():
                act.wait_ge(wexp_ready, 1)
                nc.scalar.activation(wtmp[:, 1, :], wtmp[:, 0, :], ACT.Exp).then_inc(wexp_ready, 1)

            exp_logits()

            def first_part(which):
                for w, s in which:
                    nc.scalar.copy(w_hi[:, w, s, :], stage[w][:, s, :]).then_inc(hi_ready, 1)

            act.wait_ge(T["s_ws"], 16 * NSH)
            first_part(SPLITS[:NSH])
            for b in range(B):
                act.wait_ge(rows_full, b + 1)
                nc.scalar.copy(summary[:, b, :], pY[b][:]).then_inc(summary_ready, 1)
            act.wait_ge(lo_ready, 1)

            def step(g):
                for n in range(SharedExperts.CHUNKS):
                    if with_shared(g):
                        shared.gate(act, g, n, pG)
                    if prepared(g):
                        if n == 3:
                            need(act, lnz_ready, g * TPB + 2 * TPB, alone=1)
                            need(act, x3_ready, g * TPB + TPB)
                            for j in range(TPB):
                                nc.scalar.activation(z[:, j, :], row(x_sb, (g + 1) * TPB + j), ACT.Identity,
                                                     scale=lnz[:, j, 0:1], bias=lnz[:, j, 1:2]).then_inc(z_ready, 1)
                            if isinstance(g, int):
                                act.wait_ge(gate_loaded, 16 * NSH)
                                first_part(SPLITS[NSH:])
                        if n == 7:
                            need(act, lnf_ready, g * TPB + 2 * TPB, alone=1)
                            for j in range(TPB):
                                nc.scalar.activation(flat[:, j, :], row(x_sb, (g + 1) * TPB + j), ACT.Identity,
                                                     scale=lnf[:, j, 0:1], bias=lnf[:, j, 1:2]).then_inc(flat_ready, 1)

                if prepared(g):
                    for j in range(TPB):
                        need(act, fT_full, g * TPB + (TPB + j + 1))
                        bank = turned(g, j)
                        nc.scalar.copy(flat_hi[:, :, j * P:j * P + P], bank[:].rearrange("p (d t) -> p d t", d=DB))
                        nc.scalar.copy(flatTt[:, j].rearrange("p d t -> p (d t)"), bank[:]).then_inc(fT_ready, 1)

            groups(act, step)

        @block.vector
        def _(dve):
            nc.vector.tensor_tensor(wtmp[:, 0, :], top0[:, :, 1], top0[:, :, 0], ALU.subtract).then_inc(wexp_ready, 1)
            def split(n):
                split_weights(nc.vector, dve, n).then_inc(lo_ready, 1)

            split(0)
            dve.wait_ge(wexp_ready, 2)
            nc.vector.tensor_scalar(wtmp[:, 2, :], wtmp[:, 1, :], 1.0, None, ALU.add)
            dve.drain()
            nc.vector.reciprocal(wtmp[:, 0, :], wtmp[:, 2, :])
            dve.drain()
            nc.vector.tensor_scalar(wmix[:, :, 0], wtmp[:, 0, :], gates[:, 2:3], None, ALU.mult)
            dve.drain()
            nc.vector.tensor_tensor(wmix[:, :, 1], wmix[:, :, 0], wtmp[:, 1, :], ALU.mult)
            dve.wait_ge(s_full, 1)
            nc.vector.tensor_tensor(scol[:], pC[:, 0:DB * B].rearrange("p (n b) -> p n b", b=B),
                                    T["bout_col"][:].unsqueeze(2).broadcast_to([P, DB, B]), ALU.add).then_inc(scol_ready, 1)
            dve.drain()

            def choose(g, j):
                if j % 2 == 0:
                    need(dve, lg_full, g * TPB + (j + 2))
                    for k in (j, j + 1):
                        nc.vector.tensor_tensor(logits[:, k, :], logits_of(k), bias_r[:], ALU.add)
                    dve.drain()
                nc.vector.max(m8[:], logits[:, j, :])
                dve.drain()
                nc.vector.max_index(i8[:], m8[:], logits[:, j, :])
                nc.vector.tensor_copy(row(top1, g * TPB + j), m8[:, 0:TOP1])
                dve.drain()
                nc.vector.tensor_copy(idxf[:, j, :], i8[:, 0:TOP1])
                dve.drain()
                for k in range(TOP1):
                    nc.vector.tensor_scalar(onehot[:, j, k, :], iota_e[:], idxf[:, j, k:k + 1], None, ALU.is_equal)
                dve.drain()
                for k in range(2):
                    nc.vector.tensor_tensor(pair[:, k, :], onehot[:, j, 2 * k, :], onehot[:, j, 2 * k + 1, :], ALU.add)
                dve.drain()
                nc.vector.tensor_tensor(mask[:, j, :], pair[:, 0, :], pair[:, 1, :], ALU.add).then_inc(mask_ready, 1)

            def place(g, j):
                need(dve, pos_full, g * TPB + (j + 1))
                nc.vector.tensor_tensor(chosen[:, 1 - j % 2, :], chosen[:, j % 2, :], mask[:, j, :], ALU.add)
                for k in range(TOP1):
                    last = nc.vector.tensor_tensor_reduce(out=junk[:, k, :], in0=onehot[:, j, k, :], in1=pL[:, 0:E1],
                                                          scale=1.0, scalar=0.0, op0=ALU.mult, op1=ALU.add,
                                                          accum_out=posf[:, k:k + 1])
                last.then_inc(pos_read, 1)
                dve.drain()
                nc.vector.tensor_scalar(drop[:], posf[:], float(CAP1), float(E1 * CAP1), ALU.is_ge, ALU.mult)
                nc.vector.tensor_scalar(row(kept1, g * TPB + j), posf[:], float(CAP1), None, ALU.is_lt)
                nc.vector.scalar_tensor_tensor(slotf[:], idxf[:, j, :], float(CAP1), posf[:], ALU.mult, ALU.add)
                dve.drain()
                nc.vector.tensor_tensor(drop[:], slotf[:], drop[:], ALU.add)
                nc.vector.tensor_scalar(posf[:], posf[:], float(CAP1 - 1), None, ALU.min)
                dve.drain()
                nc.vector.scalar_tensor_tensor(row(take1, g * TPB + j), idxf[:, j, :], float(CAP1), posf[:],
                                               ALU.mult, ALU.add)
                nc.vector.tensor_copy(slot1[:, j, :], drop[:]).then_inc(slot_ready, 1)
                dve.drain()

            def scale_and_bias(ln, ready):
                nc.vector.tensor_copy(ln[:, :, 0], rstd[:])
                nc.vector.scalar_tensor_tensor(ln[:, :, 1], mv[:, :, 0], -1.0, rstd[:], ALU.mult,
                                               ALU.mult).then_inc(ready, TPB)

            def statistics():
                dve.drain()
                for j in range(TPB):
                    nc.vector.bn_aggr(mv[:, j, :], bn[:, j, :])
                dve.drain()
                rsqrt(nc, dve, rstd[:], mv[:, :, 1], half[:], (ve[:], nt[:]))

            def combine(g, j):
                t = (g + 1) * TPB + j
                need(dve, gathered[j], g * 32 + 32 * 2)
                for k in range(2):
                    last = nc.vector.scalar_tensor_tensor(row(x_sb, t), y0[:, j, k, :], row(wmix, t)[:, k:k + 1],
                                                          row(x_sb, t), ALU.mult, ALU.add)
                    dve.drain()
                last.then_inc(x2_ready, 1)

            def spread(g, j):
                nc.vector.bn_stats(bn[:, j, :], row(x_sb, (g + 1) * TPB + j))

            def attend(g):
                dve.drain()
                nc.vector.tensor_scalar(rstd[:], rstd[:], gates[:, 1:2], None, ALU.mult)
                for j in range(TPB):
                    nc.vector.scalar_tensor_tensor(z[:, j, :], z[:, j, :], mv[:, j, 0:1], gamma[:],
                                                   ALU.subtract, ALU.mult)

            def attended(g):
                dve.drain()
                for j in range(TPB):
                    t = (g + 1) * TPB + j
                    need(dve, xb_ready, t + 1)
                    nc.vector.scalar_tensor_tensor(row(x_sb, t), z[:, j, :], rstd[:, j:j + 1], row(x_sb, t),
                                                   ALU.mult, ALU.add).then_inc(x3_ready, 1)

            def step(g):
                for n in range(SharedExperts.CHUNKS):
                    if with_shared(g):
                        shared.product(dve, g, n, pU)
                    if routed(g) and n in PLACED:
                        place(g, PLACED[n])
                    if prepared(g):
                        if n == 0:
                            combine(g, 0)
                            combine(g, 1)
                        if n == 1:
                            combine(g, 2)
                            spread(g, 0)
                            spread(g, 1)
                            combine(g, 3)
                        if n == 2:
                            spread(g, 2)
                            spread(g, 3)
                            statistics()
                            need(dve, z_ready, g * TPB + TPB)
                            scale_and_bias(lnz, lnz_ready)
                            if isinstance(g, int):
                                dve.wait_ge(small_loaded, 64)
                                nc.vector.tensor_scalar(beta[:], beta[:], gates[:, 1:2], None,
                                                        ALU.mult).then_inc(beta_ready, 1)
                                split(1)
                        if n == 5:
                            for j in range(TPB):
                                need(dve, y_ready, g * TPB + (TPB + j + 1))
                                nc.vector.bn_stats(bn[:, j, :], z[:, j, :])
                            statistics()
                        if n == 6:
                            attend(g)
                        if n == 7:
                            attended(g)
                            dve.drain()
                            for j in range(TPB):
                                spread(g, j)
                            statistics()
                            need(dve, flat_ready, g * TPB + TPB)
                            need(dve, scattered, (g + 1) * (TPB * TOP1 * 16))
                            scale_and_bias(lnf, lnf_ready)
                if isinstance(g, int) and g == -1:
                    for j in range(TPB):
                        dve.wait_ge(fT_ready, j + 1)
                        cols = slice(j * P, j * P + P)
                        nc.vector.tensor_tensor(flat_lo[:, :, cols], flatTt[:, j],
                                                flat_hi[:, :, cols], ALU.subtract).then_inc(fT_kept, 1)
                for j in range(TPB):
                    if with_shared(g):
                        shared.add(dve, g, j, g * TPB + j, pY)
                    if prepared(g) and j >= 2:
                        choose(g + 1, 2 * (j - 2))
                        choose(g + 1, 2 * (j - 2) + 1)

            groups(dve, step)


def expert_slot(T, n):
    if n in (5, 6):
        return T["w1"][:, n - 5]
    t, at = {0: ("y0", 0), 1: ("y0", 3), 2: ("stage_up", 0), 3: ("stage_gate", 0), 4: ("stage_gate", 3),
             7: ("stage_up", DB)}[n]
    t = T[t][:]
    t = t.rearrange("p j k d -> p (j k) d") if len(t.shape) == 4 else t.rearrange("p s (b h) -> p (s b) h", h=D)
    return t[:, at:at + 3, :]


def load_expert(sp, A, T, n, e):
    slot = expert_slot(T, n)
    for k, name in enumerate(("L1_ffn_Wg", "L1_ffn_Wu", "L1_ffn_Wd")):
        if isinstance(e, int):
            w = A[name][e].rearrange("(p b) h -> p (b h)", p=P)
        else:
            w = A[name][bass.ds(e, 1)].rearrange("o (p b) h -> p (o b h)", p=P)
        sp.dma_start(slot[:, k, :], w).then_inc(T["s_w1"][n], 16)


def experts(nc, A, T):
    c = ExitStack()
    with c:
        def sb(name, shape, dt=F32):
            return c.enter_context(nc.sbuf_tensor(name, shape, dt))

        def sem(name):
            return c.enter_context(nc.semaphore(name))

        bank, ident, top1, kept1, wt1 = T["bank"], T["ident"], T["top1"], T["kept1"], T["wt1"]
        RING = 4
        AHEAD = RING - 1
        T["w1"] = sb("m1_w", [P, 2, 3, D])
        loaded = T["s_w1"]
        slots = [expert_slot(T, n) for n in range(W_RING)]
        up_w = [[t[:, k, :].rearrange("p (b h) -> p b h", b=DB) for k in range(2)] for t in slots]
        xb = sb("m1_x", [P, RING, D])
        xT = T["y0"][:, TPB - 1].rearrange("p k (b t) -> p k b t", b=DB)
        spare = T["stage_gate"][:, 1, (DB - 1) * HSH:].rearrange("p (n t) -> p n t", t=CAP1)
        g, h = spare[:, 0:2], spare[:, 2:4]
        y = T["summary"]
        wsum = sb("wsum", [P, TILES])
        stored = [sem(f"m1_stored_{n}") for n in range(RING)]
        xT_full, xT_ready, h_full, g_ready, h_ready = (sem(n) for n in (
            "m1_xT_full", "m1_xT_ready", "m1_h_full", "m1_g_ready", "m1_h_ready"))
        y_full, y_ready = sem("m1_y_full"), sem("m1_y_ready")
        less_max, exp_ready = sem("m1_less_max"), sem("m1_exp_ready")
        pX, pH, pY = bank[0:2], bank[2:4], bank[4:6]
        block = c.enter_context(nc.Block())

        @block.sync
        def _(sp):
            def step(i, u, q):
                e = i + AHEAD
                if valid(e, n=E1):
                    need(sp, y_full, i)
                    sp.dma_start(xb[:, (q + AHEAD) % RING, :],
                                 T["tab1"][bass.ds(e * CAP1, CAP1), :]).then_inc(loaded[(q + AHEAD) % W_RING], 16)
                e = i + W_RING - 1
                if valid(e, n=E1) and (not isinstance(e, int) or e >= W_EARLY):
                    need(sp, y_full, i)
                    load_expert(sp, A, T, (q - 1) % W_RING, e)
                if valid(i - 1, n=E1):
                    n = (q - 1) % RING
                    need(sp, y_ready, i)
                    sp.dma_start(T["ytab1"][bass.ds((i - 1) * CAP1, CAP1), :], y[:, n, :]).then_inc(stored[n], 16)

            steps(sp, step, E1, W_RING, W_RING - 1, 1)
            for s in range(RING):
                sp.wait_ge(stored[s], 16 * E1 // RING)

        @block.tensor
        def _(pe):
            def step(i, u, q):
                s, o = q % 2, 1 - q % 2
                if valid(i + 1, n=E1):
                    n = (q + 1) % RING
                    need(pe, loaded[(q + 1) % W_RING], (u + (q + 1) // W_RING) * 64 + 64)
                    need(pe, xT_ready, i)
                    for b in range(DB):
                        last = nc.tensor.transpose(pX[o][:, b * P:b * P + P],
                                                   xb[:, n, :].rearrange("t (p b) -> t b p", b=DB)[:, b, :], ident[:])
                    last.then_inc(xT_full, 1)
                if valid(i, n=E1):
                    need(pe, xT_ready, i + 1)
                    need(pe, h_ready, i - 1)
                    for k, w in enumerate(up_w[q]):
                        for b in range(DB):
                            last = nc.tensor.matmul(pH[s][:, k * CAP1:(k + 1) * CAP1], w[:, b, :], xT[:, s, b, :],
                                                    start=(b == 0), stop=(b == DB - 1))
                    last.then_inc(h_full, 1)
                if valid(i - 1, n=E1):
                    need(pe, h_ready, i)
                    need(pe, y_ready, i - 2)
                    nc.tensor.matmul(pY[o][:], h[:, o, :], slots[(q - 1) % W_RING][:, 2, :],
                                     start=True, stop=True).then_inc(y_full, 1)

            steps(pe, step, E1, W_RING, 1, 1)

        @block.scalar
        def _(act):
            act.wait_ge(less_max, 1)
            nc.scalar.activation(wt1[:], wt1[:], ACT.Exp).then_inc(exp_ready, 1)

            def step(i, u, q):
                s, o = q % 2, 1 - q % 2
                if valid(i + 1, n=E1):
                    need(act, xT_full, i + 2)
                    need(act, h_full, i)
                    nc.scalar.copy(xT[:, o].rearrange("p d t -> p (d t)"), pX[o][:]).then_inc(xT_ready, 1)
                if valid(i, n=E1):
                    need(act, h_full, i + 1)
                    need(act, h_ready, i - 1)
                    nc.scalar.activation(g[:, s, :], pH[s][:, 0:CAP1], ACT.Silu).then_inc(g_ready, 1)

            steps(act, step, E1, RING, 1, 1)

        @block.vector
        def _(dve):
            shape = [P, TILES, TOP1]
            nc.vector.tensor_tensor(wt1[:], top1[:], top1[:, :, 0:1].broadcast_to(shape), ALU.subtract).then_inc(less_max, 1)
            dve.wait_ge(exp_ready, 1)
            nc.vector.tensor_reduce(wsum[:], wt1[:], AX.X, ALU.add)
            dve.drain()
            nc.vector.reciprocal(wsum[:], wsum[:])
            dve.drain()
            nc.vector.tensor_tensor(wt1[:], wt1[:], wsum[:].unsqueeze(2).broadcast_to(shape), ALU.mult)
            dve.drain()
            nc.vector.scalar_tensor_tensor(wt1[:], kept1[:], T["gates"][:, 3:4], wt1[:], ALU.mult, ALU.mult)
            dve.drain()

            def step(i, u, q):
                s, o = q % 2, 1 - q % 2
                if valid(i, n=E1):
                    need(dve, g_ready, i + 1)
                    need(dve, y_full, i - 1)
                    nc.vector.tensor_tensor(h[:, s, :], g[:, s, :], pH[s][:, CAP1:2 * CAP1], ALU.mult).then_inc(h_ready, 1)
                if valid(i - 1, n=E1):
                    need(dve, y_full, i)
                    need(dve, stored[(q - 1) % RING], (u + (q - 1) // RING) * 16)
                    nc.vector.tensor_copy(y[:, (q - 1) % RING, :], pY[o][:]).then_inc(y_ready, 1)

            steps(dve, step, E1, RING, 1, 1)


def finish(nc, A, T, out):
    c = ExitStack()
    with c:
        def sb(name, shape, dt=F32):
            return c.enter_context(nc.sbuf_tensor(name, shape, dt))

        def sem(name):
            return c.enter_context(nc.semaphore(name))

        x_sb, bank, take1, wt1 = T["x_sb"], T["bank"], T["take1"], T["wt1"]
        pY, pG, pU = bank[0:4], bank[4:6], bank[6:8]
        RING = 4
        G = B - 1
        y1 = sb("y1", [P, RING, TOP1, D])
        shared = SharedExperts(nc, T, c, "b")
        gathered = [sem(f"y1_gathered_{n}") for n in range(RING)]
        combined, stored = sem("combined"), sem("out_stored")
        out_v = out.rearrange("b (t p) d -> p (b t) d", p=P)
        block = c.enter_context(nc.Block())

        @block.sync
        def _(sp):
            for t in range(TILES):
                sp.wait_ge(combined, t + 1)
                if t >= G * TPB:
                    sp.wait_ge(shared.y_read, t - G * TPB + 1)
                sp.dma_start(out_v[:, t, :], x_sb[:, t, :]).then_inc(stored, 16)
            sp.wait_ge(stored, 16 * TILES)

        @block.gpsimd
        def _(pool):
            for t in range(TILES):
                need(pool, combined, t - RING + 1)
                for k in range(TOP1):
                    nc.gpsimd.indirect_dma_start(
                        y1[:, t % RING, k, :], None, T["ytab1"],
                        bass.IndirectOffsetOnAxis(take1[:, t, k:k + 1], 0)).then_inc(gathered[t % RING], 16)

        @block.tensor
        def _(pe):
            for n in range(SharedExperts.CHUNKS):
                shared.up(pe, 0, n, pG, pU)
            for j in range(TPB):
                shared.down(pe, 0, j, pY)

        @block.scalar
        def _(act):
            for n in range(SharedExperts.CHUNKS):
                shared.gate(act, 0, n, pG)

        @block.vector
        def _(dve):
            products = dict(zip((0, 1, 2, 3, 4, 6, 7, 8), range(SharedExperts.CHUNKS)))
            results = {G * TPB - 1 + j: j for j in range(TPB)}
            for t in range(TILES):
                q = t % RING
                dve.wait_ge(gathered[q], (t // RING + 1) * 16 * TOP1)
                for k in range(TOP1):
                    last = nc.vector.scalar_tensor_tensor(x_sb[:, t, :], y1[:, q, k, :], wt1[:, t, k:k + 1],
                                                          x_sb[:, t, :], ALU.mult, ALU.add)
                    if k < TOP1 - 1:
                        dve.drain()
                last.then_inc(combined, 1)
                if t in products:
                    shared.product(dve, 0, products[t], pU)
                if t in results:
                    shared.add(dve, 0, results[t], t + 1, pY)
                    dve.drain()


class SharedExperts:

    CHUNKS = NSH * HSH // P

    def __init__(self, nc, T, c, tag, hidden=None):
        self.nc, self.T = nc, T
        n = self.CHUNKS
        self.g = c.enter_context(nc.sbuf_tensor(f"sh_gate_{tag}", [P, 2, SEQ], F32))
        self.h = c.enter_context(nc.sbuf_tensor(f"sh_h_{tag}", [P, n, SEQ], F32)) if hidden is None else hidden
        self.up_full, self.g_ready, self.h_ready, self.y_full, self.y_read = (
            c.enter_context(nc.semaphore(f"sh_{s}_{tag}")) for s in ("up_full", "g_ready", "h_ready", "y_full", "y_read"))

    def up(self, pe, r, n, pG, pU):
        nc, T = self.nc, self.T
        s, at = n // (HSH // P), (n % (HSH // P)) * P
        if n >= 2:
            need(pe, self.h_ready, r * self.CHUNKS + (n - 1))
        for k, bank in ((0, pG[n % 2]), (1, pU[n % 2])):
            for d in range(DB):
                cols = slice(d * HSH + at, d * HSH + at + P)
                for part, (w, x) in enumerate(((T["w_hi"], T["flat_hi"]), (T["w_hi"], T["flat_lo"]), (T["w_lo"], T["flat_hi"]))):
                    last = nc.tensor.matmul(bank[:], w[:, k, s, cols], x[:, d, :], start=(d == 0 and part == 0),
                                            stop=(d == DB - 1 and part == 2))
        last.then_inc(self.up_full, 1)

    def gate(self, act, r, n, pG):
        need(act, self.up_full, r * self.CHUNKS + (n + 1))
        if n >= 2:
            need(act, self.h_ready, r * self.CHUNKS + (n - 1))
        self.nc.scalar.activation(self.g[:, n % 2, :], pG[n % 2][:], ACT.Silu).then_inc(self.g_ready, 1)

    def product(self, dve, r, n, pU, odd=None):
        odd = n % 2 if odd is None else odd
        need(dve, self.g_ready, r * self.CHUNKS + (n + 1))
        self.nc.vector.tensor_tensor(row(self.h, n), self.g[:, odd, :], pU[odd][:], ALU.mult).then_inc(self.h_ready, 1)

    def down(self, pe, r, j, pY):
        nc, sd = self.nc, self.T["w_sd"]
        need(pe, self.h_ready, r * self.CHUNKS + (self.CHUNKS - 1))
        for n in range(self.CHUNKS):
            if j == 0 and n == self.CHUNKS - 1:
                need(pe, self.h_ready, r * self.CHUNKS + self.CHUNKS)
            s, b = n // (HSH // P), n % (HSH // P)
            last = nc.tensor.matmul(pY[j][:], self.h[:, n, j * P:j * P + P], sd[:, s, b, :],
                                    start=(n == 0), stop=(n == self.CHUNKS - 1))
        last.then_inc(self.y_full, 1)

    def add(self, dve, r, j, t, pY):
        x = row(self.T["x_sb"], t)
        need(dve, self.y_full, r * TPB + (j + 1))
        self.nc.vector.scalar_tensor_tensor(x, pY[j][:], self.T["gates"][:, 3:4], x, ALU.mult,
                                            ALU.add).then_inc(self.y_read, 1)


INPUTS = (
    "x", "ctx_2048", "g_xattn", "g_ffn", "L0_ffn_w_gate", "L0_ffn_wi_0", "L0_ffn_wi_1", "L0_ffn_wo",
    "L1_xattn_decay", "L1_xattn_W_in", "L1_xattn_b_in", "L1_xattn_W_out", "L1_xattn_b_out",
    "L1_xattn_gamma", "L1_xattn_beta", "L1_ffn_Wr", "L1_ffn_router_bias", "L1_ffn_Wg", "L1_ffn_Wu",
    "L1_ffn_Wd", "L1_ffn_Sg", "L1_ffn_Su", "L1_ffn_Sd")


def kernel(**inputs):
    import numpy as np
    import concourse.bacc as bacc
    from concourse import mybir
    from concourse.bass_utils import run_bass_kernel_spmd

    nc = bacc.Bacc("TRN2", target_bir_lowering=False, num_devices=1)
    arrays, A = {}, {}
    for name in INPUTS:
        a = np.ascontiguousarray(inputs[name])
        if inputs[name].ndim == 0:
            a = a.reshape(1, 1)
        arrays[f"in_{name}"] = a
        A[name] = nc.dram_tensor(f"in_{name}", a.shape, mybir.dt.from_np(a.dtype), kind="ExternalInput").ap()
    out = nc.dram_tensor("out", inputs["x"].shape, mybir.dt.float32, kind="ExternalOutput").ap()
    build(nc, A, out)
    r = run_bass_kernel_spmd(nc, [arrays], core_ids=[0])
    return r.results[0]["out"]
```
